# Optimizing a Trainium2 kernel written in Bass

```python
import numpy as np
import jax
import jax.numpy as jnp

def _softmax(x, axis=-1):
    return jax.nn.softmax(x, axis=axis)

def _gelu(x):
    return jax.nn.gelu(x, approximate=True)

def _silu(x):
    return jax.nn.silu(x)

def _sigmoid(x):
    return jax.nn.sigmoid(x)

def _layernorm(x, axis=-1, eps=1e-05):
    m = jnp.mean(x, axis=axis, keepdims=True)
    v = jnp.var(x, axis=axis, keepdims=True)
    return (x - m) / jnp.sqrt(v + eps)

def _scatter_add(tgt, idx, src, axis=0):
    return tgt.at[idx].add(src)

def _segment_sum(src, seg, n):
    return jax.ops.segment_sum(src, seg, n)
kernel_name = 'mk_flamingo_gated_d2_seqx_r4_6f9f0f'

def setup_inputs(seed: int=0):
    np.random.seed(seed)
    _w = jnp.asarray

    def _rec_inputs():
        import jax
        import jax.numpy as jnp
        _rk = jax.random.key(seed)
        x = 7.22e-05 + 1 * jax.random.normal(jax.random.fold_in(_rk, 1), (32, 256, 256), jnp.float32)
        _lenS = 256 - jax.random.randint(jax.random.fold_in(_rk, 7), (32,), 0, max(1, 256 // 4) + 1, jnp.int32)
        _lenS2 = 256 - jax.random.randint(jax.random.fold_in(_rk, 8), (32,), 0, max(1, 256 // 4) + 1, jnp.int32)
        _ctx_1024P = jax.random.normal(jax.random.fold_in(_rk, 11), (32, 16, 256), jnp.float32)
        _ctx_1024c = jax.random.dirichlet(jax.random.fold_in(_rk, 511), 0.3 * jnp.ones((16,), jnp.float32), (32, 256))
        _ctx_1024t = jnp.einsum('bsk,bkd->bsd', _ctx_1024c, _ctx_1024P)
        _ctx_1024t = _ctx_1024t * jax.lax.rsqrt(jnp.mean(jnp.square(_ctx_1024t)) + 1e-12) * 0.953939
        ctx_1024 = 4.13588e-05 + 0.999923 * (_ctx_1024t + 0.3 * jax.random.normal(jax.random.fold_in(_rk, 611), (32, 256, 256), jnp.float32))
        _validS = jnp.arange(256)[None, :] < _lenS[:, None]
        _validS2 = jnp.arange(256)[None, :] < _lenS2[:, None]
        _causal = jnp.tril(jnp.ones((256, 256), dtype=bool))
        mask_1x1xSxS2_fk1 = jnp.where(jnp.broadcast_to(_validS2[0:1, None, None, :], (1, 1, 256, 256)), 1.0, 0.0).astype(jnp.float32)
        _g = jax.random.normal(jax.random.fold_in(_rk, 9001), (2, 2), jnp.float32)
        _g = jnp.sign(_g) * jnp.maximum(jnp.abs(_g), 1.0) + (_g == 0) * 1.0
        g_xattn = _g[0]
        g_ffn = _g[1]
        return (x, ctx_1024, mask_1x1xSxS2_fk1, g_xattn, g_ffn)
    x, ctx_1024, mask_1x1xSxS2_fk1, g_xattn, g_ffn = _rec_inputs()

    def _L0_xattn_setup():
        import jax, jax.numpy as jnp
        import numpy as np
        D_MODEL = 256
        NUM_HEADS = 16
        DEPTH = D_MODEL // NUM_HEADS
        B, S = (4, 512)
        NEG = -1000000000.0

        def _split_heads(x):
            b, s, _ = x.shape
            return x.reshape(b, s, NUM_HEADS, DEPTH).transpose(0, 2, 1, 3)
        key = jax.random.key(seed)
        ks = jax.random.split(key, 12)
        q = jax.random.normal(ks[0], (B, S, D_MODEL), dtype=jnp.float32)
        k = jax.random.normal(ks[1], (B, S, D_MODEL), dtype=jnp.float32)
        v = jax.random.normal(ks[2], (B, S, D_MODEL), dtype=jnp.float32)
        mask = (1.0 - jnp.tril(jnp.ones((S, S), dtype=jnp.float32)))[None, None]
        scale = 1.0 / np.sqrt(D_MODEL)
        Wq = jax.random.normal(ks[3], (D_MODEL, D_MODEL), dtype=jnp.float32) * scale
        Wk = jax.random.normal(ks[4], (D_MODEL, D_MODEL), dtype=jnp.float32) * scale
        Wv = jax.random.normal(ks[5], (D_MODEL, D_MODEL), dtype=jnp.float32) * scale
        Wo = jax.random.normal(ks[6], (D_MODEL, D_MODEL), dtype=jnp.float32) * scale
        bq = jnp.zeros((D_MODEL,), jnp.float32)
        bk = jnp.zeros((D_MODEL,), jnp.float32)
        bv = jnp.zeros((D_MODEL,), jnp.float32)
        bo = jnp.zeros((D_MODEL,), jnp.float32)
        return {'query': q, 'key': k, 'value': v, 'mask': mask, 'Wq': Wq, 'bq': bq, 'Wk': Wk, 'bk': bk, 'Wv': Wv, 'bv': bv, 'Wo': Wo, 'bo': bo}
    _L0_xattn_all = _L0_xattn_setup()
    _L0_xattn_in = {k: v for k, v in _L0_xattn_all.items() if k in ('Wq', 'bq', 'Wk', 'bk', 'Wv', 'bv', 'Wo', 'bo')}
    del _L0_xattn_all

    def _L0_ffn_setup():
        import jax, jax.numpy as jnp
        import numpy as np
        E = 64
        K = 6
        CAP = 128
        ROUTE_SCALE = 1.0
        key = jax.random.key(seed)
        ks = jax.random.split(key, 9)
        B, S, D, I = (2, 256, 256, 176)
        SI = 2 * I
        s = 0.02
        return {'x': jax.random.normal(ks[0], (B, S, D), jnp.float32), 'gate_w': jax.random.normal(ks[1], (E, D), jnp.float32) * s, 'gate_b': jnp.zeros((E,), jnp.float32), 'w1': jax.random.normal(ks[2], (E, I, D), jnp.float32) * s, 'w2': jax.random.normal(ks[3], (E, D, I), jnp.float32) * s, 'w3': jax.random.normal(ks[4], (E, I, D), jnp.float32) * s, 'ws1': jax.random.normal(ks[5], (SI, D), jnp.float32) * s, 'ws2': jax.random.normal(ks[6], (D, SI), jnp.float32) * s, 'ws3': jax.random.normal(ks[7], (SI, D), jnp.float32) * s}
    _L0_ffn_all = _L0_ffn_setup()
    _L0_ffn_in = {k: v for k, v in _L0_ffn_all.items() if k in ('gate_w', 'gate_b', 'w1', 'w2', 'w3', 'ws1', 'ws2', 'ws3')}
    del _L0_ffn_all

    def _L1_xattn_setup():
        import jax, jax.numpy as jnp
        import numpy as np
        H = 16
        D_K = 64
        D_V = 64
        D_MODEL = 256
        B, N = (4, 512)
        key = jax.random.key(seed)
        ks = jax.random.split(key, 7)
        return {'Q': jax.random.normal(ks[0], (B, N, D_MODEL), dtype=jnp.float32), 'K': jax.random.normal(ks[1], (B, N, D_MODEL), dtype=jnp.float32), 'V': jax.random.normal(ks[2], (B, N, D_MODEL), dtype=jnp.float32), 'W_Q': jax.random.normal(ks[3], (D_MODEL, D_K * H), dtype=jnp.float32) * 0.02, 'W_K': jax.random.normal(ks[4], (D_MODEL, D_K * H), dtype=jnp.float32) * 0.02, 'W_V': jax.random.normal(ks[5], (D_MODEL, D_V * H), dtype=jnp.float32) * 0.02, 'W_O': jax.random.normal(ks[6], (D_V * H, D_MODEL), dtype=jnp.float32) * 0.02}
    _L1_xattn_all = _L1_xattn_setup()
    _L1_xattn_in = {k: v for k, v in _L1_xattn_all.items() if k in ('W_Q', 'W_K', 'W_V', 'W_O')}
    del _L1_xattn_all

    def _L1_ffn_setup():
        import jax, jax.numpy as jnp
        import numpy as np
        DIM = 256
        NUM_EXPERTS = 8
        HIDDEN = 1024
        CAP_FACTOR = 2.0
        B, S = (4, 512)
        key = jax.random.key(seed)
        ks = jax.random.split(key, 6)
        scale_r = 1.0 / np.sqrt(DIM)
        scale_1 = 1.0 / np.sqrt(DIM)
        scale_2 = 1.0 / np.sqrt(HIDDEN)
        return {'x': jax.random.normal(ks[0], (B, S, DIM), dtype=jnp.float32), 'router_w': jax.random.uniform(ks[1], (NUM_EXPERTS, DIM), jnp.float32, -scale_r, scale_r), 'w1': jax.random.uniform(ks[2], (NUM_EXPERTS, DIM, HIDDEN), jnp.float32, -scale_1, scale_1), 'b1': jax.random.uniform(ks[3], (NUM_EXPERTS, HIDDEN), jnp.float32, -scale_1, scale_1), 'w2': jax.random.uniform(ks[4], (NUM_EXPERTS, HIDDEN, DIM), jnp.float32, -scale_2, scale_2), 'b2': jax.random.uniform(ks[5], (NUM_EXPERTS, DIM), jnp.float32, -scale_2, scale_2)}
    _L1_ffn_all = _L1_ffn_setup()
    _L1_ffn_in = {k: v for k, v in _L1_ffn_all.items() if k in ('router_w', 'w1', 'b1', 'w2', 'b2')}
    del _L1_ffn_all
    return {'x': x, 'ctx_1024': ctx_1024, 'mask_1x1xSxS2_fk1': mask_1x1xSxS2_fk1, 'g_xattn': g_xattn, 'g_ffn': g_ffn, 'L0_xattn_Wq': _L0_xattn_in['Wq'], 'L0_xattn_bq': _L0_xattn_in['bq'], 'L0_xattn_Wk': _L0_xattn_in['Wk'], 'L0_xattn_bk': _L0_xattn_in['bk'], 'L0_xattn_Wv': _L0_xattn_in['Wv'], 'L0_xattn_bv': _L0_xattn_in['bv'], 'L0_xattn_Wo': _L0_xattn_in['Wo'], 'L0_xattn_bo': _L0_xattn_in['bo'], 'L0_ffn_gate_w': _L0_ffn_in['gate_w'], 'L0_ffn_gate_b': _L0_ffn_in['gate_b'], 'L0_ffn_w1': _L0_ffn_in['w1'], 'L0_ffn_w2': _L0_ffn_in['w2'], 'L0_ffn_w3': _L0_ffn_in['w3'], 'L0_ffn_ws1': _L0_ffn_in['ws1'], 'L0_ffn_ws2': _L0_ffn_in['ws2'], 'L0_ffn_ws3': _L0_ffn_in['ws3'], 'L1_xattn_W_Q': _L1_xattn_in['W_Q'], 'L1_xattn_W_K': _L1_xattn_in['W_K'], 'L1_xattn_W_V': _L1_xattn_in['W_V'], 'L1_xattn_W_O': _L1_xattn_in['W_O'], 'L1_ffn_router_w': _L1_ffn_in['router_w'], 'L1_ffn_w1': _L1_ffn_in['w1'], 'L1_ffn_b1': _L1_ffn_in['b1'], 'L1_ffn_w2': _L1_ffn_in['w2'], 'L1_ffn_b2': _L1_ffn_in['b2']}

def reference(x, ctx_1024, mask_1x1xSxS2_fk1, g_xattn, g_ffn, L0_xattn_Wq, L0_xattn_bq, L0_xattn_Wk, L0_xattn_bk, L0_xattn_Wv, L0_xattn_bv, L0_xattn_Wo, L0_xattn_bo, L0_ffn_gate_w, L0_ffn_gate_b, L0_ffn_w1, L0_ffn_w2, L0_ffn_w3, L0_ffn_ws1, L0_ffn_ws2, L0_ffn_ws3, L1_xattn_W_Q, L1_xattn_W_K, L1_xattn_W_V, L1_xattn_W_O, L1_ffn_router_w, L1_ffn_w1, L1_ffn_b1, L1_ffn_w2, L1_ffn_b2):
    import jax
    import jax.numpy as jnp

    def _L0_xattn_ref(query, key, value, mask, Wq, bq, Wk, bk, Wv, bv, Wo, bo):
        import jax, jax.numpy as jnp
        import numpy as np
        D_MODEL = 256
        NUM_HEADS = 16
        DEPTH = D_MODEL // NUM_HEADS
        B, S = (4, 512)
        NEG = -1000000000.0

        def _split_heads(x):
            b, s, _ = x.shape
            return x.reshape(b, s, NUM_HEADS, DEPTH).transpose(0, 2, 1, 3)
        q = _split_heads(query @ Wq + bq)
        k = _split_heads(key @ Wk + bk)
        v = _split_heads(value @ Wv + bv)
        scores = jnp.einsum('bhqd,bhkd->bhqk', q, k) / jnp.sqrt(jnp.asarray(DEPTH, q.dtype))
        scores = scores + mask * NEG
        weights = jax.nn.softmax(scores, axis=-1)
        out = jnp.einsum('bhqk,bhkd->bhqd', weights, v)
        out = out.transpose(0, 2, 1, 3).reshape(query.shape[0], -1, D_MODEL)
        return out @ Wo + bo

    def _L0_ffn_ref(x, gate_w, gate_b, w1, w2, w3, ws1, ws2, ws3):
        import jax, jax.numpy as jnp
        import numpy as np
        E = 64
        K = 6
        CAP = 128
        ROUTE_SCALE = 1.0
        shape = x.shape
        D = shape[-1]
        xf = x.reshape(-1, D)
        T = xf.shape[0]
        scores = jax.nn.softmax(xf @ gate_w.T, axis=-1)
        _, idx = jax.lax.top_k(scores + gate_b, K)
        weights = jnp.take_along_axis(scores, idx, axis=1) * ROUTE_SCALE
        flat_e = idx.reshape(-1)
        order = jnp.argsort(flat_e)
        se = flat_e[order]
        counts = jnp.bincount(flat_e, length=E)
        starts = jnp.cumsum(counts) - counts
        pos = jnp.arange(T * K) - starts[se]
        tok = order // K
        xb = jnp.zeros((E, CAP, D), xf.dtype).at[se, pos].set(xf[tok], mode='drop')
        h = jax.nn.silu(jnp.einsum('ecd,eid->eci', xb, w1)) * jnp.einsum('ecd,eid->eci', xb, w3)
        yb = jnp.einsum('eci,edi->ecd', h, w2)
        valid = (pos < CAP).astype(xf.dtype)
        contrib = yb[se, jnp.minimum(pos, CAP - 1)]
        wf = weights.reshape(-1)[order] * valid
        y = jnp.zeros_like(xf).at[tok].add(contrib * wf[:, None])
        z = jax.nn.silu(xf @ ws1.T) * (xf @ ws3.T) @ ws2.T
        return (y + z).reshape(shape)

    def _L1_xattn_ref(Q, K, V, W_Q, W_K, W_V, W_O):
        import jax, jax.numpy as jnp
        import numpy as np
        H = 16
        D_K = 64
        D_V = 64
        D_MODEL = 256
        B, N = (4, 512)
        b, n, _ = Q.shape
        q = (Q @ W_Q).reshape(b, n, H, D_K)
        k = (K @ W_K).reshape(b, n, H, D_K)
        v = (V @ W_V).reshape(b, n, H, D_V)
        scores = jnp.einsum('bqhd,bkhd->bhqk', q, k) / jnp.sqrt(jnp.asarray(D_K, q.dtype))
        attn = jax.nn.softmax(scores, axis=2)
        out = jnp.einsum('bhqk,bkhd->bqhd', attn, v).reshape(b, n, H * D_V)
        return out @ W_O

    def _L1_ffn_ref(x, router_w, w1, b1, w2, b2):
        import jax, jax.numpy as jnp
        import numpy as np
        DIM = 256
        NUM_EXPERTS = 8
        HIDDEN = 1024
        CAP_FACTOR = 2.0
        B, S = (4, 512)
        Bz, Sz, Dz = x.shape
        E = router_w.shape[0]
        capacity = max(1, int(Sz * CAP_FACTOR / E) + 1)
        scores = jax.nn.softmax(jnp.einsum('bsd,ed->bse', x, router_w), axis=-1)
        scores_t = jnp.swapaxes(scores, 1, 2)
        gate_vals, sel_idx = jax.lax.top_k(scores_t, capacity)
        b_idx = jnp.arange(Bz)[:, None, None]
        tokens = x[b_idx, sel_idx]
        h = jnp.einsum('becd,edh->bech', tokens, w1) + b1[None, :, None, :]
        h = jax.nn.gelu(h, approximate=False)
        y = jnp.einsum('bech,ehd->becd', h, w2) + b2[None, :, None, :]
        gated = y * gate_vals[..., None]
        out = jnp.zeros_like(x).at[b_idx, sel_idx].add(gated)
        return out
    x = x + jnp.tanh(g_xattn[0]) * _L0_xattn_ref(_layernorm(x, axis=-1), ctx_1024, ctx_1024, mask_1x1xSxS2_fk1, L0_xattn_Wq, L0_xattn_bq, L0_xattn_Wk, L0_xattn_bk, L0_xattn_Wv, L0_xattn_bv, L0_xattn_Wo, L0_xattn_bo)
    x = x + jnp.tanh(g_ffn[0]) * _L0_ffn_ref(_layernorm(x, axis=-1), L0_ffn_gate_w, L0_ffn_gate_b, L0_ffn_w1, L0_ffn_w2, L0_ffn_w3, L0_ffn_ws1, L0_ffn_ws2, L0_ffn_ws3)
    x = x + jnp.tanh(g_xattn[1]) * _L1_xattn_ref(_layernorm(x, axis=-1), ctx_1024, ctx_1024, L1_xattn_W_Q, L1_xattn_W_K, L1_xattn_W_V, L1_xattn_W_O)
    x = x + jnp.tanh(g_ffn[1]) * _L1_ffn_ref(_layernorm(x, axis=-1), L1_ffn_router_w, L1_ffn_w1, L1_ffn_b1, L1_ffn_w2, L1_ffn_b2)
    return x

_drawn_inputs = setup_inputs


def setup_inputs(seed=0):
    import zlib

    import numpy as np

    out = dict(_drawn_inputs(seed))
    spreads = {'g_ffn': (-1.0, 0.6),
     'L0_xattn_bq': (0.0, 0.385),
     'L0_xattn_bk': (0.0, 2.0),
     'L0_xattn_bv': (0.0, 0.1),
     'L0_xattn_bo': (0.0, 0.1),
     'L0_ffn_gate_b': (0.0, 0.8)}
    factors = {'L0_ffn_gate_w': 8.0,
     'L0_ffn_w1': 8.0,
     'L0_ffn_w2': 8.0,
     'L0_ffn_w3': 8.0,
     'L0_ffn_ws1': 4.068,
     'L0_ffn_ws2': 4.05,
     'L0_ffn_ws3': 4.066,
     'L1_xattn_W_Q': 8.0,
     'L1_xattn_W_K': 8.0,
     'L1_ffn_b1': 30.511,
     'L1_ffn_b2': 21.583}
    for name, (base, spread) in spreads.items():
        noise = np.random.default_rng([zlib.crc32(name.encode()), seed]).standard_normal(out[name].shape)
        drawn = base * np.exp(spread * noise) if base else spread * noise
        out[name] = jnp.asarray(drawn.astype(out[name].dtype))
    for name, factor in factors.items():
        out[name] = (out[name] * factor).astype(out[name].dtype)
    return out
```

```python
from contextlib import ExitStack

import concourse.bass as bass
from concourse import mybir

F32 = mybir.dt.float32
U32 = mybir.dt.uint32
I32 = mybir.dt.int32
ALU = mybir.AluOpType
ACT = mybir.ActivationFunctionType
AX = mybir.AxisListType.X

P = 128
BATCH, S, D = 32, 256, 256
ST = S // P
DC = D // P
HEADS = 16
DEPTH = D // HEADS
HPC = P // DEPTH
PACK = 4
PAD = P // PACK
NEG = -1.0e9
EPS = 1e-5
HUGE = 3.0e38
BIG_SLOT = 1.0e6

E0, TOPK, CAP0, I0 = 64, 6, 128, 176
SI = 2 * I0
SI_CHUNKS = [(0, 128), (128, 128), (256, SI - 256)]
I0_CHUNKS = [(0, 128), (128, I0 - 128)]

DK = 64
HD = HEADS * DK
E1, HID = 8, 1024
CAP1 = int(S * 2.0 / E1) + 1
SLOTS = E1 * CAP1
HC = HID // P
GC = 5
GS = SLOTS // GC


def after(eng, sem, value, alone=None):
    if isinstance(value, int) and value <= 0:
        return
    eng.wait_ge(sem, value)
    if alone is not None and not isinstance(value, int):
        eng.sem_inc(alone, 1)


class Chain:

    def __init__(self, eng, sem, size, step, alone=None):
        self.eng, self.sem, self.size, self.base, self.count = eng, sem, size, step * size, 0
        self.alone = alone

    def done(self, ins):
        self.count += 1
        ins.then_inc(self.sem, 1)

    def wait(self):
        after(self.eng, self.sem, self.base + self.count, self.alone)

    def end(self):
        assert self.count == self.size, (self.count, self.size)


def tiles(ap):
    return ap.rearrange("(t p) d -> p t d", p=P)


def attention_and_router(nc, sb, psum, sem, io, dram, keep, NB):
    wq, wk, wv, wo = (sb(n, [P, DC, D]) for n in ("wq", "wk", "wv", "wo"))
    gate_w = sb("gate_w", [P, DC, E0])
    ws1, ws3 = sb("ws1", [P, DC, SI]), sb("ws3", [P, DC, SI])
    ws2 = sb("ws2", [P, 3, D])
    bq, bk = sb("bq", [P, DC]), sb("bk", [P, DC])
    bv, bo = sb("bv", [P, D]), sb("bo", [P, D])
    gate_b = sb("gate_b", [P, E0])
    mask = sb("mask", [P, ST, S])
    row_id = sb("row_id", [P, 1], I32)
    head_row_i = sb("head_row_i", [P, 1], I32)
    head_row = sb("head_row", [P, 1])
    head_id = sb("head_id", [P, HPC])
    head_scale = sb("head_scale", [P, HPC])
    upper = sb("upper", [P, P])
    ones = sb("ones", [P, P])
    minus_half = sb("minus_half", [P, 2])
    expert_base = sb("expert_base", [P, E0])

    x_in = sb("x_in", [P, ST, D])
    stats = sb("stats", [P, ST, 6])
    mv = sb("mv", [P, ST, 2])
    var_eps = sb("var_eps", [P, ST])
    rstd = sb("rstd", [P, ST])
    xln = sb("xln", [P, ST, D])
    xlnT = sb("xlnT", [P, DC, S])
    ctxT = sb("ctxT", [P, DC, S])
    q = sb("q", [P, DC, S])
    qm = sb("qm", [P, 4, S])
    kT = sb("kT", [P, DC, S])
    vx = sb("vx", [P, ST, HEADS * PAD])
    neg_s = sb("neg_s", [P, 4, ST, S])
    neg_max = sb("neg_max", [P, 4, ST])
    probs = sb("probs", [P, 4, ST, S])
    probsT = sb("probsT", [P, 2 * PACK, ST, S])
    oT = sb("oT", [P, 2, S])
    inv_sum = sb("inv_sum", [P, 2, ST, PACK])
    attn = sb("attn", [P, ST, D])
    attnT = sb("attnT", [P, DC, S])
    xr = sb("xr", [P, ST, D])
    stats2 = sb("stats2", [P, ST, 6])
    mv2 = sb("mv2", [P, ST, 2])
    var_eps2 = sb("var_eps2", [P, ST])
    rstd2 = sb("rstd2", [P, ST])
    xf = sb("xf", [P, ST, D])
    xfT = sb("xfT", [P, DC, S])
    r_negmax = sb("r_negmax", [P, ST])
    r_exp = sb("r_exp", [P, ST, E0])
    r_sum = sb("r_sum", [P, ST])
    r_inv = sb("r_inv", [P, ST])
    scores = sb("scores", [P, ST, E0])
    biased = sb("biased", [P, ST, E0 + 2])
    top8 = sb("top8", [P, ST, 8])
    replaced = sb("replaced", [P, ST, E0 + 2])
    chosen = sb("chosen", [P, ST, E0])
    seen = sb("seen", [P, E0])
    fits = sb("fits", [P, ST, E0])
    numbered = sb("numbered", [P, ST, E0])
    slot_of = sb("slot_of", [P, ST, E0])
    weight_of = sb("weight_of", [P, ST, E0])
    slot8 = sb("slot8", [P, ST, 8])
    no_slot = sb("no_slot", [P, ST, 8])
    picked = sb("picked", [P, ST * TOPK, E0])
    slots = sb("slots", [P, ST, 8], U32)
    w8 = sb("w8", [P, ST, 8])
    th = sb("th", [P, 2, S])
    silu2 = sb("silu2", [P, 2, S])
    hidden = sb("hidden", [P, 3, S])
    zero_rows = sb("zero_rows", [P, 8, D])
    ident, tanh_g, slots_all, w_all = keep["ident"], keep["tanh_g"], keep["slots_all"], keep["w_all"]

    ps_s = [psum(f"ps_s{i}") for i in range(2)]
    ps_t = [psum(f"ps_t{i}") for i in range(2)]
    ps_o = [psum(f"ps_o{i}") for i in range(2)]
    ps_m = [psum(f"ps_m{i}") for i in range(2)]

    s_const = sem("a_const_loaded")
    s_zero = sem("a_zeros_stored")
    s_x = sem("a_x_loaded")
    s_ctx = sem("a_ctx_loaded")
    s_xr = sem("a_residual_loaded")
    s_store = sem("a_x1_stored")
    s_scat = sem("a_rows_scattered")
    s_pc = sem("a_pool_consts")
    s_setup = sem("a_vector_setup")
    s_tanh = sem("a_tanh_ready")
    s_zset = sem("a_zero_rows_ready")
    v_waits, p_waits = sem("a_vector_waits"), sem("a_pool_waits")
    v_ln = sem("a_ln1_chain")
    p_rs1 = sem("a_rstd1_ready")
    p_rs1c = sem("a_rstd1_chain")
    v_xln = sem("a_xln_ready")
    t_xln = sem("a_xlnT_in_psum")
    a_xln = sem("a_xlnT_ready")
    t_q = sem("a_q_in_psum")
    a_q, v_q = sem("a_q_ready"), sem("a_head_q_ready")
    t_k, a_k = sem("a_k_in_psum"), sem("a_k_ready")
    t_v, v_v = sem("a_v_in_psum"), sem("a_v_ready")
    t_s = sem("a_scores_in_psum")
    v_m = sem("a_scores_masked")
    a_e = sem("a_probs_ready")
    t_t = sem("a_probsT_in_psum")
    te = [sem("a_probsT_even_ready"), sem("a_probsT_odd_ready")]
    t_pv = sem("a_pv_done")
    a_o, t_o = sem("a_oT_ready"), sem("a_o_in_psum")
    v_inv = sem("a_inv_sum")
    v_on = sem("a_attn_ready")
    t_ot, a_ot = sem("a_attnT_in_psum"), sem("a_attnT_ready")
    t_wo = sem("a_wo_in_psum")
    p_xr = sem("a_residual_biased")
    v_x1 = sem("a_x1_ready")
    v_st = sem("a_ln2_chain")
    p_rs2 = sem("a_rstd2_ready")
    p_rs2c = sem("a_rstd2_chain")
    v_xf = sem("a_xf_ready")
    t_xf, a_xf = sem("a_xfT_in_psum"), sem("a_xfT_ready")
    t_r = sem("a_logits_in_psum")
    v_rm = sem("a_logits_max")
    a_r = sem("a_logits_exp")
    v_rc = sem("a_router_chain")
    v_ch = sem("a_chosen_ready")
    t_pos = sem("a_positions_in_psum")
    p_seen = sem("a_seen_updated")
    v_pos = sem("a_position_chain")
    v_slot = sem("a_slots_ready")
    t_h = sem("a_hidden_in_psum")
    a_th = sem("a_hidden_tanh")
    v_hc = sem("a_hidden_chain")
    v_h = sem("a_hidden_ready")
    t_z = sem("a_z_in_psum")
    v_z = sem("a_x1z_ready")

    RC, PC = 8, 8
    STEPS = HEADS + 4
    GROUPS = HEADS // PACK
    N_CONST = 16

    with nc.Block() as block:

        @block.sync
        def _(sp):
            for dst, src in ((wq, io["wq"]), (wk, io["wk"]), (wv, io["wv"]), (wo, io["wo"]),
                             (gate_w, io["gate_w"]), (ws1, io["ws1"]), (ws3, io["ws3"])):
                sp.dma_start(dst[:], src.rearrange("(c p) n -> p c n", p=P)).then_inc(s_const, 16)
            sp.dma_start(ws2[:, 0:2, :], io["ws2"][0:256].rearrange("(c p) n -> p c n", p=P)).then_inc(s_const, 16)
            sp.dma_start(ws2[0:SI - 256, 2, :], io["ws2"][256:SI]).then_inc(s_const, 16)
            sp.dma_start(bq[:], io["bq"].rearrange("(c p) -> p c", p=P), allow_slow_non_contiguous=True).then_inc(s_const, 16)
            sp.dma_start(bk[:], io["bk"].rearrange("(c p) -> p c", p=P), allow_slow_non_contiguous=True).then_inc(s_const, 16)
            sp.dma_start(bv[:], io["bv"].rearrange("(a n) -> a n", a=1).broadcast_to([P, D])).then_inc(s_const, 16)
            sp.dma_start(bo[:], io["bo"].rearrange("(a n) -> a n", a=1).broadcast_to([P, D])).then_inc(s_const, 16)
            sp.dma_start(gate_b[:], io["gate_b"].rearrange("(a n) -> a n", a=1).broadcast_to([P, E0])).then_inc(s_const, 16)
            sp.dma_start(mask[:], tiles(io["mask"])).then_inc(s_const, 16)
            sp.dma_start(keep["gates"][:], io["gates"].rearrange("(a n) -> a n", a=1).broadcast_to([P, 4])).then_inc(s_const, 16)
            sp.dma_start(x_in[:], tiles(io["x"][0])).then_inc(s_x, 16)
            sp.dma_start(ctxT[:], tiles(io["ctxT"][0])).then_inc(s_ctx, 16)
            sp.dma_start(xr[:], tiles(io["x"][0])).then_inc(s_xr, 16)
            sp.wait_ge(s_zset, 1)
            for i in range(8):
                sp.dma_start(dram["rows"][i * 1024:(i + 1) * 1024].rearrange("(p r) d -> p r d", p=P),
                             zero_rows[:]).then_inc(s_zero, 16)

            def loads(b):
                sp.wait_ge(v_xln, b + 1)
                sp.dma_start(x_in[:], tiles(io["x"][b + 1])).then_inc(s_x, 16)
                sp.wait_ge(t_v, b + 1)
                sp.dma_start(ctxT[:], tiles(io["ctxT"][b + 1])).then_inc(s_ctx, 16)

            def store(p):
                sp.wait_ge(v_z, p + 1)
                sp.dma_start(tiles(dram["x1"][p]), xr[:]).then_inc(s_store, 16)
                sp.wait_ge(s_store, (p + 1) * 16)

            def residual(b):
                sp.dma_start(xr[:], tiles(io["x"][b])).then_inc(s_xr, 16)

            loads(0)
            loads(1)
            store(0)
            residual(1)
            with sp.Fori(2, NB - 1) as b:
                loads(b)
                store(b - 1)
                residual(b)
            store(NB - 2)
            residual(NB - 1)
            store(NB - 1)
            sp.wait_ge(s_zero, 16 * 8)

        @block.gpsimd
        def _(pool):
            pool.memset(zero_rows[:], 0.0).then_inc(s_zset, 1)
            pool.memset(ident[:], 0.0).then_inc(s_pc, 1)
            pool.memset(upper[:], 1.0).then_inc(s_pc, 1)
            pool.memset(ones[:], 1.0).then_inc(s_pc, 1)
            pool.memset(seen[:], 0.0).then_inc(s_pc, 1)
            pool.memset(minus_half[:], -0.5).then_inc(s_pc, 1)
            pool.iota(row_id[:], [[0, 1]], base=0, channel_multiplier=1).then_inc(s_pc, 1)
            pool.iota(expert_base[:], [[CAP0, E0]], base=0, channel_multiplier=0,
                      allow_small_or_imprecise_dtypes=True).then_inc(s_pc, 1)
            pool.iota(head_id[:], [[1, HPC]], base=0, channel_multiplier=0,
                      allow_small_or_imprecise_dtypes=True).then_inc(s_pc, 1)
            pool.wait_ge(s_pc, 8)
            pool.affine_select(out=ident[:], in_=ident[:], compare_op=ALU.not_equal, fill=1.0, base=0,
                               pattern=[[-1, P]], channel_multiplier=1).then_inc(s_pc, 1)
            pool.affine_select(out=upper[:], in_=upper[:], compare_op=ALU.is_ge, fill=0.0, base=0,
                               pattern=[[1, P]], channel_multiplier=-1).then_inc(s_pc, 1)

            def rsqrt(b, mv_, var_eps_, rstd_, chain, stats_done, stats_size, ready):
                after(pool, stats_done, (b + 1) * stats_size, alone=p_waits)
                pool.tensor_scalar(var_eps_[:], mv_[:, :, 1], EPS, None, ALU.add).then_inc(chain, 1)
                pool.wait_ge(chain, b + 1)
                pool.tensor_tensor(rstd_[:], var_eps_[:], minus_half[:], ALU.pow).then_inc(ready, 1)

            def bias_residual(p):
                pool.wait_ge(s_xr, (p + 1) * 16)
                if isinstance(p, int) and p == 0:
                    pool.wait_ge(s_setup, 3)
                for t in range(ST):
                    ins = pool.tensor_tensor(xr[:, t, :], xr[:, t, :], bo[:], ALU.add)
                ins.then_inc(p_xr, 1)

            def scatter(p):
                for t in range(ST):
                    pool.wait_ge(t_pos, p + 1)
                    if t:
                        pool.wait_ge(p_seen, ST * p + t)
                    pool.tensor_tensor(seen[:], seen[:], chosen[:, t, :], ALU.add).then_inc(p_seen, 1)
                after(pool, v_slot, p + 1, alone=p_waits)
                if isinstance(p, int) and p == 0:
                    pool.wait_ge(s_zero, 16 * 8)
                for t in range(ST):
                    for k in range(TOPK):
                        pool.indirect_dma_start(
                            out=dram["rows"], out_offset=bass.IndirectOffsetOnAxis(ap=slots[:, t, k:k + 1], axis=0),
                            in_=xf[:, t, :], in_offset=None,
                            bounds_check=E0 * CAP0 - 1, oob_is_err=False).then_inc(s_scat, 16)

            def ffn(p):
                bias_residual(p)
                rsqrt(p, mv2, var_eps2, rstd2, p_rs2c, v_st, 4, p_rs2)
                scatter(p)

            rsqrt(0, mv, var_eps, rstd, p_rs1c, v_ln, 4, p_rs1)
            rsqrt(1, mv, var_eps, rstd, p_rs1c, v_ln, 4, p_rs1)
            ffn(0)
            rsqrt(2, mv, var_eps, rstd, p_rs1c, v_ln, 4, p_rs1)
            with pool.Fori(2, NB - 1) as b:
                ffn(b - 1)
                rsqrt(b + 1, mv, var_eps, rstd, p_rs1c, v_ln, 4, p_rs1)
            ffn(NB - 2)
            ffn(NB - 1)
            pool.wait_ge(s_scat, 16 * ST * TOPK * NB)

        @block.vector
        def _(dve):
            dve.wait_ge(s_const, 16 * N_CONST)
            dve.wait_ge(s_pc, 10)
            dve.memset(vx[:], 0.0).then_inc(s_setup, 1)
            dve.memset(biased[:], -HUGE).then_inc(s_setup, 1)
            dve.wait_ge(s_tanh, 1)
            dve.tensor_scalar(bo[:], bo[:], tanh_g[:, 0:1], None, ALU.mult).then_inc(s_setup, 1)
            dve.tensor_scalar(mask[:], mask[:], NEG, None, ALU.mult).then_inc(s_setup, 1)
            dve.tensor_scalar(head_row_i[:], row_id[:], DEPTH.bit_length() - 1, None, ALU.logical_shift_right).then_inc(s_setup, 1)
            dve.wait_ge(s_setup, 5)
            dve.memset(vx[:, :, :].rearrange("p t (h e) -> p (t h) e", e=PAD)[:, :, DEPTH], 1.0).then_inc(s_setup, 1)
            dve.tensor_copy(head_row[:], head_row_i[:]).then_inc(s_setup, 1)
            dve.wait_ge(s_setup, 7)
            dve.tensor_scalar(head_scale[:], head_id[:], head_row[:, 0:1], DEPTH ** -0.5, ALU.is_equal, ALU.mult).then_inc(s_setup, 1)
            dve.wait_ge(s_setup, 8)

            def layernorm1(b):
                c = Chain(dve, v_ln, 4, b, alone=v_waits)
                dve.wait_ge(s_x, (b + 1) * 16)
                for t in range(ST):
                    c.done(dve.bn_stats(stats[:, t, :], x_in[:, t, :]))
                c.wait()
                for t in range(ST):
                    c.done(dve.bn_aggr(mv[:, t, :], stats[:, t, :]))
                c.wait()
                c.end()

            def layernorm1_apply(b):
                dve.wait_ge(p_rs1, b + 1)
                after(dve, t_xln, b)
                for t in range(ST):
                    ins = dve.tensor_scalar(xln[:, t, :], x_in[:, t, :], mv[:, t, 0:1], rstd[:, t:t + 1],
                                            ALU.subtract, ALU.mult)
                ins.then_inc(v_xln, 1)

            def head_q(b, i):
                if i == 0:
                    dve.wait_ge(a_q, b + 1)
                after(dve, t_s, HEADS * b + i - 3)
                dve.tensor_scalar(qm[:, i % 4, :], q[:, i // HPC, :], head_scale[:, i % HPC:i % HPC + 1], None,
                                  ALU.mult).then_inc(v_q, 1)

            def v_evac(b):
                dve.wait_ge(t_v, b + 1)
                for t in range(ST):
                    ins = dve.tensor_tensor(
                        vx[:, t, :].rearrange("p (h e) -> p h e", e=PAD)[:, :, 0:DEPTH],
                        ps_m[1][:, t * D:(t + 1) * D].rearrange("p (h e) -> p h e", e=DEPTH),
                        bv[:].rearrange("p (h e) -> p h e", e=DEPTH), ALU.add)
                ins.then_inc(v_v, 1)

            def mask_and_max(b, i):
                after(dve, t_s, HEADS * b + i + 1, alone=v_waits)
                after(dve, a_e, HEADS * b + i - 3, alone=v_waits)
                for t in range(ST):
                    ins = dve.tensor_tensor_reduce(
                        out=neg_s[:, i % 4, t, :], in0=ps_s[i % 2][:, t * S:(t + 1) * S], in1=mask[:, t, :],
                        scale=-1.0, scalar=HUGE, op0=ALU.add, op1=ALU.min, accum_out=neg_max[:, i % 4, t:t + 1])
                ins.then_inc(v_m, 1)

            def probsT_evac(b, i):
                dve.wait_ge(t_t, HEADS * b + i + 1)
                after(dve, t_pv, GROUPS * b + i // PACK - 1)
                dve.tensor_copy(probsT[:, i % (2 * PACK), :, :], ps_t[1][:, :]).then_inc(te[1], 1)

            def normalise(b, g):
                dve.wait_ge(t_o, GROUPS * b + g + 1)
                if g == 0:
                    after(dve, t_ot, b)
                o = ps_o[g % 2][:, S:2 * S].rearrange("p (t h e) -> p t h e", t=ST, e=PAD)
                dve.reciprocal(inv_sum[:, g % 2, :, :], o[:, :, :, DEPTH]).then_inc(v_inv, 1)
                dve.wait_ge(v_inv, GROUPS * b + g + 1)
                dve.tensor_tensor(attn[:, :, g * PACK * DEPTH:(g + 1) * PACK * DEPTH].rearrange("p t (h e) -> p t h e", e=DEPTH),
                                  o[:, :, :, 0:DEPTH],
                                  inv_sum[:, g % 2, :, :].unsqueeze(3).broadcast_to([P, ST, PACK, DEPTH]),
                                  ALU.mult).then_inc(v_on, 1)

            def add_attention(p):
                dve.wait_ge(t_wo, p + 1)
                dve.wait_ge(p_xr, p + 1)
                dve.scalar_tensor_tensor(out=xr[:], in0=ps_m[1][:, :], scalar=tanh_g[:, 0:1], in1=xr[:],
                                         op0=ALU.mult, op1=ALU.add).then_inc(v_x1, 1)
                c = Chain(dve, v_st, 4, p, alone=v_waits)
                dve.wait_ge(v_x1, p + 1)
                for t in range(ST):
                    c.done(dve.bn_stats(stats2[:, t, :], xr[:, t, :]))
                c.wait()
                for t in range(ST):
                    c.done(dve.bn_aggr(mv2[:, t, :], stats2[:, t, :]))
                c.wait()
                c.end()

            def layernorm2(p):
                dve.wait_ge(p_rs2, p + 1)
                after(dve, s_scat, 16 * ST * TOPK * p)
                for t in range(ST):
                    ins = dve.tensor_scalar(xf[:, t, :], xr[:, t, :], mv2[:, t, 0:1], rstd2[:, t:t + 1],
                                            ALU.subtract, ALU.mult)
                ins.then_inc(v_xf, 1)

            def router_max(p):
                dve.wait_ge(t_r, p + 1)
                dve.tensor_reduce(r_negmax[:], ps_m[1][:, 0:ST * E0].rearrange("p (t e) -> p t e", e=E0),
                                  AX, ALU.max, negate=True).then_inc(v_rm, 1)

            def choose(p):
                c = Chain(dve, v_rc, RC, p, alone=v_waits)
                dve.wait_ge(a_r, p + 1)
                c.done(dve.reciprocal(r_inv[:], r_sum[:]))
                c.wait()
                c.done(dve.tensor_tensor(scores[:], r_exp[:], r_inv[:].unsqueeze(2).broadcast_to([P, ST, E0]), ALU.mult))
                c.wait()
                c.done(dve.tensor_tensor(biased[:, :, 0:E0], scores[:], gate_b[:].unsqueeze(1).broadcast_to([P, ST, E0]), ALU.add))
                c.wait()
                for t in range(ST):
                    c.done(dve.max(top8[:, t, :], biased[:, t, :]))
                c.wait()
                c.done(dve.memset(top8[:, :, TOPK:8], -HUGE))
                c.wait()
                for t in range(ST):
                    c.done(dve.match_replace(replaced[:, t, :], top8[:, t, :], biased[:, t, :], HUGE))
                c.wait()
                after(dve, p_seen, ST * p)
                dve.tensor_scalar(chosen[:], replaced[:, :, 0:E0], 0.9 * HUGE, None, ALU.is_ge).then_inc(v_ch, 1)
                c.end()

            def hidden_evac(p, ic):
                n = SI_CHUNKS[ic][1]
                ps = ps_m[ic % 2]
                c = Chain(dve, v_hc, 1, 3 * p + ic)
                dve.wait_ge(a_th, 3 * p + ic + 1)
                c.done(dve.scalar_tensor_tensor(out=silu2[0:n, ic % 2, :], in0=th[0:n, ic % 2, :], scalar=1.0,
                                                in1=ps[0:n, 0:S], op0=ALU.add, op1=ALU.mult))
                c.wait()
                dve.scalar_tensor_tensor(out=hidden[0:n, ic, :], in0=silu2[0:n, ic % 2, :], scalar=0.5,
                                         in1=ps[0:n, S:2 * S], op0=ALU.mult, op1=ALU.mult).then_inc(v_h, 1)

            def add_shared(p):
                dve.wait_ge(t_z, p + 1)
                dve.scalar_tensor_tensor(out=xr[:], in0=ps_m[1][:, :], scalar=tanh_g[:, 2:3], in1=xr[:],
                                         op0=ALU.mult, op1=ALU.add).then_inc(v_z, 1)

            def make_slots(p):
                dve.wait_ge(t_pos, p + 1)
                dve.wait_ge(v_ch, p + 1)
                pos = ps_m[0][:, 0:ST * E0].rearrange("p (t e) -> p t e", e=E0)
                c = Chain(dve, v_pos, PC + ST * TOPK, p, alone=v_waits)
                c.done(dve.scalar_tensor_tensor(out=fits[:], in0=pos, scalar=float(CAP0), in1=chosen[:],
                                                op0=ALU.is_le, op1=ALU.mult))
                c.done(dve.tensor_tensor(numbered[:], pos, expert_base[:].unsqueeze(1).broadcast_to([P, ST, E0]), ALU.add))
                c.wait()
                c.done(dve.tensor_tensor(slot_of[:], fits[:], numbered[:], ALU.mult))
                c.wait()
                c.done(dve.scalar_tensor_tensor(out=weight_of[:], in0=slot_of[:], scalar=0.5, in1=scores[:],
                                                op0=ALU.is_ge, op1=ALU.mult))
                for t in range(ST):
                    c.done(dve.max(slot8[:, t, :], slot_of[:, t, :]))
                c.wait()
                for t in range(ST):
                    for k in range(TOPK):
                        c.done(dve.scalar_tensor_tensor(out=picked[:, t * TOPK + k, :], in0=slot_of[:, t, :], scalar=slot8[:, t, k:k + 1],
                                                        in1=weight_of[:, t, :], op0=ALU.is_equal, op1=ALU.mult,
                                                        accum_out=w8[:, t, k:k + 1]))
                c.done(dve.tensor_scalar(no_slot[:], slot8[:], 0.5, BIG_SLOT, ALU.is_lt, ALU.mult))
                c.wait()
                after(dve, s_scat, 16 * ST * TOPK * p)
                c.done(dve.scalar_tensor_tensor(out=slots[:], in0=slot8[:], scalar=-1.0, in1=no_slot[:],
                                                op0=ALU.add, op1=ALU.add))
                c.wait()
                c.end()
                dve.tensor_copy(slots_all[:, bass.ds(p * ST, ST), :], slots[:])
                dve.tensor_copy(w_all[:, bass.ds(p * ST, ST), 0:TOPK], w8[:, :, 0:TOPK]).then_inc(v_slot, 1)

            def ffn_at(p, i):
                if p is None:
                    return
                if i == 2:
                    add_attention(p)
                if i == 3:
                    layernorm2(p)
                if i == 6:
                    router_max(p)
                if i == 7:
                    hidden_evac(p, 0)
                if i == 8:
                    choose(p)
                    hidden_evac(p, 1)
                if i == 9:
                    hidden_evac(p, 2)
                if i == 11:
                    add_shared(p)
                if i == 12:
                    make_slots(p)

            def batch(b, p, last):
                head_q(b, 0)
                head_q(b, 1)
                for i in range(STEPS):
                    if i + 2 < HEADS:
                        head_q(b, i + 2)
                    if i < HEADS:
                        mask_and_max(b, i)
                    if 2 <= i < HEADS + 2 and i % 2 == 1:
                        probsT_evac(b, i - 2)
                    if i >= 7 and i % PACK == 3:
                        normalise(b, (i - 7) // PACK)
                    ffn_at(p, i)
                    if not last:
                        if i == 9:
                            layernorm1(b + 1)
                        if i == 13:
                            layernorm1_apply(b + 1)
                        if i == STEPS - 1:
                            v_evac(b + 1)

            layernorm1(0)
            layernorm1_apply(0)
            v_evac(0)
            batch(0, None, False)
            batch(1, 0, False)
            with dve.Fori(2, NB - 1) as b:
                batch(b, b - 1, False)
            batch(NB - 1, NB - 2, True)
            for i in range(HEADS):
                ffn_at(NB - 1, i)

        @block.scalar
        def _(act):
            act.wait_ge(s_const, 16 * N_CONST)
            act.activation(tanh_g[:], keep["gates"][:], ACT.Tanh).then_inc(s_tanh, 1)
            act.wait_ge(s_setup, 8)

            def project_evac(b, part):
                if part == 0:
                    act.wait_ge(t_xln, b + 1)
                    act.activation(xlnT[:], ps_m[0][:, :], ACT.Copy).then_inc(a_xln, 1)
                    return
                if part == 1:
                    act.wait_ge(t_q, b + 1)
                    after(act, v_q, HEADS * b)
                dst, bank, bias, ready = (q, ps_m[1], bq, a_q) if part == 1 else (kT, ps_m[0], bk, a_k)
                if part == 2:
                    act.wait_ge(t_k, b + 1)
                for c in range(DC):
                    ins = act.activation(dst[:, c, :], bank[:, c * S:(c + 1) * S], ACT.Identity,
                                         bias=bias[:, c:c + 1], scale=1.0)
                ins.then_inc(ready, 1)

            def exponentials(b, i):
                act.wait_ge(v_m, HEADS * b + i + 1)
                after(act, t_t, HEADS * b + i - 3)
                for t in range(ST):
                    ins = act.activation(probs[:, i % 4, t, :], neg_s[:, i % 4, t, :], ACT.Exp,
                                         bias=neg_max[:, i % 4, t:t + 1], scale=-1.0)
                ins.then_inc(a_e, 1)

            def probsT_evac(b, i):
                act.wait_ge(t_t, HEADS * b + i + 1)
                after(act, t_pv, GROUPS * b + i // PACK - 1)
                act.activation(probsT[:, i % (2 * PACK), :, :], ps_t[0][:, :], ACT.Copy).then_inc(te[0], 1)

            def oT_evac(b, g):
                act.wait_ge(t_pv, GROUPS * b + g + 1)
                after(act, t_o, GROUPS * b + g - 1)
                act.activation(oT[:, g % 2, :], ps_o[g % 2][:, 0:S], ACT.Copy).then_inc(a_o, 1)

            def ffn_at(p, i):
                if p is None:
                    return
                if i == 0:
                    act.wait_ge(t_ot, p + 1)
                    act.activation(attnT[:], ps_m[0][:, :], ACT.Copy).then_inc(a_ot, 1)
                if i == 5:
                    act.wait_ge(t_xf, p + 1)
                    act.activation(xfT[:], ps_m[0][:, :], ACT.Copy).then_inc(a_xf, 1)
                if i == 6:
                    act.wait_ge(v_rm, p + 1)
                    for t in range(ST):
                        ins = act.activation(r_exp[:, t, :], ps_m[1][:, t * E0:(t + 1) * E0], ACT.Exp,
                                             bias=r_negmax[:, t:t + 1], accum_out=r_sum[:, t:t + 1])
                    ins.then_inc(a_r, 1)
                if i in (7, 8, 9):
                    ic = i - 7
                    n = SI_CHUNKS[ic][1]
                    act.wait_ge(t_h, 3 * p + ic + 1)
                    act.activation(th[0:n, ic % 2, :], ps_m[ic % 2][0:n, 0:S], ACT.Tanh, scale=0.5).then_inc(a_th, 1)

            def batch(b, p, last):
                for i in range(STEPS):
                    if 1 <= i < HEADS + 1:
                        exponentials(b, i - 1)
                    if 2 <= i < HEADS + 2 and i % 2 == 0:
                        probsT_evac(b, i - 2)
                    if i >= 6 and i % PACK == 2:
                        oT_evac(b, (i - 6) // PACK)
                    ffn_at(p, i)
                    if not last and 0 <= i - HEADS < 3:
                        project_evac(b + 1, i - HEADS)

            for part in range(3):
                project_evac(0, part)
            batch(0, None, False)
            batch(1, 0, False)
            with act.Fori(2, NB - 1) as b:
                batch(b, b - 1, False)
            batch(NB - 1, NB - 2, True)
            for i in range(HEADS):
                ffn_at(NB - 1, i)

        @block.tensor
        def _(pe):
            pe.wait_ge(s_const, 16 * N_CONST)
            pe.wait_ge(s_pc, 10)

            def transposed(dst, src):
                for c in range(DC):
                    for t in range(ST):
                        ins = pe.transpose(dst[:, c * S + t * P:c * S + (t + 1) * P], src[:, t, c * P:(c + 1) * P], ident[:])
                return ins

            def project(b, part):
                if part == 0:
                    pe.wait_ge(v_xln, b + 1)
                    transposed(ps_m[0], xln).then_inc(t_xln, 1)
                if part == 1:
                    pe.wait_ge(a_xln, b + 1)
                    for c in range(DC):
                        for k in range(DC):
                            ins = pe.matmul(ps_m[1][:, c * S:(c + 1) * S], wq[:, k, c * P:(c + 1) * P], xlnT[:, k, :],
                                            start=(k == 0), stop=(k == DC - 1))
                    ins.then_inc(t_q, 1)
                if part == 2:
                    pe.wait_ge(s_ctx, (b + 1) * 16)
                    for c in range(DC):
                        for k in range(DC):
                            ins = pe.matmul(ps_m[0][:, c * S:(c + 1) * S], wk[:, k, c * P:(c + 1) * P], ctxT[:, k, :],
                                            start=(k == 0), stop=(k == DC - 1))
                    ins.then_inc(t_k, 1)
                if part == 3:
                    pe.wait_ge(a_q, b + 1)
                    for t in range(ST):
                        for k in range(DC):
                            ins = pe.matmul(ps_m[1][:, t * D:(t + 1) * D], ctxT[:, k, t * P:(t + 1) * P], wv[:, k, :],
                                            start=(k == 0), stop=(k == DC - 1))
                    ins.then_inc(t_v, 1)

            def head_scores(b, i):
                pe.wait_ge(v_q, HEADS * b + i + 1)
                after(pe, v_m, HEADS * b + i - 1)
                for t in range(ST):
                    ins = pe.matmul(ps_s[i % 2][:, t * S:(t + 1) * S], qm[:, i % 4, t * P:(t + 1) * P],
                                    kT[:, i // HPC, :], start=True, stop=True)
                ins.then_inc(t_s, 1)

            def head_transpose(b, i):
                pe.wait_ge(a_e, HEADS * b + i + 1)
                after(pe, te[i % 2], HEADS // 2 * b + i // 2)
                for k in range(ST):
                    for t in range(ST):
                        ins = pe.transpose(ps_t[i % 2][:, k * S + t * P:k * S + (t + 1) * P],
                                           probs[:, i % 4, t, k * P:(k + 1) * P], ident[:])
                ins.then_inc(t_t, 1)

            def group_values(b, g):
                for parity in range(2):
                    pe.wait_ge(te[parity], HEADS // 2 * b + PACK // 2 * (g + 1))
                if g == 0:
                    pe.wait_ge(v_v, b + 1)
                after(pe, v_on, GROUPS * b + g - 1)
                for k in range(ST):
                    for j in range(PACK):
                        h = g * PACK + j
                        ins = pe.matmul(ps_o[g % 2][j * PAD:(j + 1) * PAD, 0:S], vx[:, k, h * PAD:(h + 1) * PAD],
                                        probsT[:, h % (2 * PACK), k, :], start=(k == 0), stop=(k == ST - 1))
                ins.then_inc(t_pv, 1)

            def group_turn(b, g):
                pe.wait_ge(a_o, GROUPS * b + g + 1)
                for t in range(ST):
                    ins = pe.transpose(ps_o[g % 2][:, S + t * P:S + (t + 1) * P], oT[:, g % 2, t * P:(t + 1) * P], ident[:])
                ins.then_inc(t_o, 1)

            def ffn_at(p, i):
                if p is None:
                    return
                if i == 0:
                    pe.wait_ge(v_on, GROUPS * (p + 1))
                    transposed(ps_m[0], attn).then_inc(t_ot, 1)
                if i == 1:
                    pe.wait_ge(a_ot, p + 1)
                    for t in range(ST):
                        for k in range(DC):
                            ins = pe.matmul(ps_m[1][:, t * D:(t + 1) * D], attnT[:, k, t * P:(t + 1) * P], wo[:, k, :],
                                            start=(k == 0), stop=(k == DC - 1))
                    ins.then_inc(t_wo, 1)
                if i == 5:
                    pe.wait_ge(v_xf, p + 1)
                    transposed(ps_m[0], xf).then_inc(t_xf, 1)
                if i == 6:
                    pe.wait_ge(a_xf, p + 1)
                    for t in range(ST):
                        for k in range(DC):
                            ins = pe.matmul(ps_m[1][:, t * E0:(t + 1) * E0], xfT[:, k, t * P:(t + 1) * P], gate_w[:, k, :],
                                            start=(k == 0), stop=(k == DC - 1))
                    ins.then_inc(t_r, 1)
                if i in (7, 8, 9):
                    ic = i - 7
                    o, n = SI_CHUNKS[ic]
                    if ic == 1:
                        pe.wait_ge(a_r, p + 1)
                    if ic == 2:
                        pe.wait_ge(v_h, 3 * p + 1)
                    for j, w in enumerate((ws1, ws3)):
                        for k in range(DC):
                            ins = pe.matmul(ps_m[ic % 2][0:n, j * S:(j + 1) * S], w[:, k, o:o + n], xfT[:, k, :],
                                            start=(k == 0), stop=(k == DC - 1))
                    ins.then_inc(t_h, 1)
                if i == 11:
                    pe.wait_ge(v_h, 3 * p + 3)
                    for t in range(ST):
                        for ic, (o, n) in enumerate(SI_CHUNKS):
                            ins = pe.matmul(ps_m[1][:, t * D:(t + 1) * D], hidden[0:n, ic, t * P:(t + 1) * P],
                                            ws2[0:n, ic, :], start=(ic == 0), stop=(ic == 2))
                    ins.then_inc(t_z, 1)
                if i == 12:
                    pe.wait_ge(v_ch, p + 1)
                    after(pe, p_seen, ST * p)
                    for t in range(ST):
                        o = ps_m[0][:, t * E0:(t + 1) * E0]
                        pe.matmul(o, ones[:], seen[:], start=True, stop=False)
                        if t:
                            pe.matmul(o, ones[:], chosen[:, 0, :], start=False, stop=False)
                        ins = pe.matmul(o, upper[:], chosen[:, t, :], start=False, stop=True)
                    ins.then_inc(t_pos, 1)

            def batch(b, p, last):
                pe.wait_ge(a_k, b + 1)
                pe.wait_ge(v_v, b + 1)
                for i in range(STEPS):
                    if i < HEADS:
                        head_scores(b, i)
                    if 2 <= i < HEADS + 2:
                        head_transpose(b, i - 2)
                    if i >= 6 and i % PACK == 2:
                        group_values(b, (i - 6) // PACK)
                    if i >= 7 and i % PACK == 3:
                        group_turn(b, (i - 7) // PACK)
                    ffn_at(p, i)
                    if not last and i >= HEADS:
                        if i == HEADS and p is not None:
                            pe.wait_ge(v_slot, p + 1)
                        project(b + 1, i - HEADS)

            for part in range(4):
                project(0, part)
            batch(0, None, False)
            batch(1, 0, False)
            with pe.Fori(2, NB - 1) as b:
                batch(b, b - 1, False)
            batch(NB - 1, NB - 2, True)
            for i in range(HEADS):
                ffn_at(NB - 1, i)


def experts(nc, sb, psum, sem, io, dram, keep, NE):
    RING = 4
    w1, w3 = sb("w1", [P, RING, DC, I0]), sb("w3", [P, RING, DC, I0])
    w2 = sb("w2", [P, RING, 2, D])
    rows = sb("rows", [P, RING, D])
    rowsT = sb("rowsT", [P, 2, DC, P])
    th = sb("th", [P, 2, 2, P])
    silu2 = sb("silu2", [P, 2, 2, P])
    hidden = sb("hidden", [P, 2, 2, P])
    y = sb("y", [P, 2, D])
    ident = keep["ident"]
    ps_t = [psum(f"ps_rows{i}") for i in range(2)]
    ps_h = [psum(f"ps_hid{i}") for i in range(2)]
    ps_y = [psum(f"ps_y{i}") for i in range(2)]

    s_w = [sem(f"b_expert{r}_loaded") for r in range(RING)]
    s_y = [sem(f"b_y{r}_stored") for r in range(2)]
    t_rows, a_rows = sem("b_rowsT_in_psum"), sem("b_rowsT_ready")
    t_h, a_th = sem("b_hidden_in_psum"), sem("b_hidden_tanh")
    v_s, v_h = sem("b_silu_ready"), sem("b_hidden_ready")
    t_y, a_y = sem("b_y_in_psum"), sem("b_y_ready")
    QUADS = (NE - RING) // RING

    def walk(eng, step):
        for e in range(RING + 1):
            step(e, e % RING, e // RING + 1)
        with eng.Fori(1, QUADS) as quad:
            for u in range(RING):
                step(quad * RING + (1 + u), (1 + u) % RING, quad + (2 if u == RING - 1 else 1))
        for e in range(QUADS * RING + 1, NE):
            step(e, e % RING, e // RING + 1)

    with nc.Block() as block:

        @block.sync
        def _(sp):
            def load(e, r):
                if not (isinstance(e, int) and e < RING):
                    sp.wait_ge(t_y, e - (RING - 1))
                for dst, src in ((w1[:, r], io["w1"][e]), (w3[:, r], io["w3"][e])):
                    sp.dma_start(dst, src.rearrange("(c p) n -> p c n", p=P)).then_inc(s_w[r], 16)
                sp.dma_start(w2[:, r, 0, :], io["w2"][e, 0:P]).then_inc(s_w[r], 16)
                sp.dma_start(w2[0:I0 - P, r, 1, :], io["w2"][e, P:I0]).then_inc(s_w[r], 16)
                sp.dma_start(rows[:, r, :], dram["rows"][bass.ds(e * CAP0, CAP0), :] if not isinstance(e, int)
                             else dram["rows"][e * CAP0:(e + 1) * CAP0, :]).then_inc(s_w[r], 16)

            for e in range(RING):
                load(e, e)
            with sp.Fori(1, NE // RING) as turn:
                for r in range(RING):
                    load(turn * RING + r, r)

        @block.tensor
        def _(pe):
            def turn_rows(e, r, n):
                pe.wait_ge(s_w[r], n * 16 * 5)
                after(pe, a_rows, e - 1)
                for c in range(DC):
                    ins = pe.transpose(ps_t[r % 2][:, c * P:(c + 1) * P], rows[:, r, c * P:(c + 1) * P], ident[:])
                ins.then_inc(t_rows, 1)

            def up(e, r):
                pe.wait_ge(a_rows, e + 1)
                after(pe, v_h, e - 1)
                for j, w in enumerate((w1, w3)):
                    for ic, (o, m) in enumerate(I0_CHUNKS):
                        for k in range(DC):
                            col = (2 * j + ic) * P
                            ins = pe.matmul(ps_h[r % 2][0:m, col:col + P], w[:, r, k, o:o + m], rowsT[:, r % 2, k, :],
                                            start=(k == 0), stop=(k == DC - 1))
                ins.then_inc(t_h, 1)

            def down(e, r):
                pe.wait_ge(v_h, e + 1)
                after(pe, a_y, e - 1)
                for ic, (o, m) in enumerate(I0_CHUNKS):
                    ins = pe.matmul(ps_y[r % 2][:, 0:D], hidden[0:m, r % 2, ic, :], w2[0:m, r, ic, :],
                                    start=(ic == 0), stop=(ic == 1))
                ins.then_inc(t_y, 1)

            turn_rows(0, 0, 1)
            up(0, 0)

            def step(e, r, n):
                if isinstance(e, int) and e == 0:
                    return
                turn_rows(e, r, n)
                down(e - 1, (r - 1) % RING)
                up(e, r)
            walk(pe, step)
            down(NE - 1, (NE - 1) % RING)

        @block.scalar
        def _(act):
            def step(e, r, n):
                act.wait_ge(t_rows, e + 1)
                after(act, t_h, e - 1)
                act.activation(rowsT[:, r % 2, :, :], ps_t[r % 2][:, 0:DC * P], ACT.Copy).then_inc(a_rows, 1)
                act.wait_ge(t_h, e + 1)
                after(act, v_h, e - 1)
                act.activation(th[:, r % 2, 0, :], ps_h[r % 2][:, 0:P], ACT.Tanh, scale=0.5)
                m = I0 - P
                act.activation(th[0:m, r % 2, 1, :], ps_h[r % 2][0:m, P:2 * P], ACT.Tanh, scale=0.5).then_inc(a_th, 1)
            walk(act, step)

        @block.vector
        def _(dve):
            def store_y(e, r, n2):
                dve.wait_ge(t_y, e + 1)
                after(dve, s_y[r % 2], n2 * 16)
                dve.tensor_copy(y[:, r % 2, :], ps_y[r % 2][:, 0:D]).then_inc(a_y, 1)

            def step(e, r, n):
                dve.wait_ge(a_th, e + 1)
                after(dve, t_y, e - 1)
                for ic, (o, m) in enumerate(I0_CHUNKS):
                    ins = dve.scalar_tensor_tensor(out=silu2[0:m, r % 2, ic, :], in0=th[0:m, r % 2, ic, :], scalar=1.0,
                                                   in1=ps_h[r % 2][0:m, ic * P:(ic + 1) * P], op0=ALU.add, op1=ALU.mult)
                ins.then_inc(v_s, 1)
                dve.wait_ge(v_s, e + 1)
                for ic, (o, m) in enumerate(I0_CHUNKS):
                    ins = dve.scalar_tensor_tensor(out=hidden[0:m, r % 2, ic, :], in0=silu2[0:m, r % 2, ic, :], scalar=0.5,
                                                   in1=ps_h[r % 2][0:m, (2 + ic) * P:(3 + ic) * P], op0=ALU.mult, op1=ALU.mult)
                ins.then_inc(v_h, 1)

            def step_and_store(e, r, n):
                step(e, r, n)
                if isinstance(e, int):
                    if e > 0:
                        store_y(e - 1, (e - 1) % RING, (e - 1) // 2)
                else:
                    quad = n - (2 if r == 0 else 1)
                    store_y(e - 1, (r - 1) % RING, quad * 2 + ((r - 1) % RING) // 2)
            walk(dve, step_and_store)
            store_y(NE - 1, (NE - 1) % RING, (NE - 1) // 2)

        @block.gpsimd
        def _(pool):
            def store(e, r):
                pool.wait_ge(a_y, e + 1)
                dst = dram["y"][e * CAP0:(e + 1) * CAP0, :] if isinstance(e, int) else dram["y"][bass.ds(e * CAP0, CAP0), :]
                pool.dma_start(dst, y[:, r % 2, :]).then_inc(s_y[r % 2], 16)
            with pool.Fori(0, NE // RING) as quad:
                for r in range(RING):
                    store(quad * RING + r, r)
            for r in range(2):
                pool.wait_ge(s_y[r], 16 * NE // 2)


def attention_and_top(nc, sb, psum, sem, io, dram, keep, NB):
    wq, wk, wv = (sb(n, [P, DC, HD]) for n in ("wq", "wk", "wv"))
    wo = sb("wo", [P, HD // P, D])
    router_w = sb("router_w", [P, DC, E1])
    minus_half = sb("minus_half", [P, 2])
    x1 = sb("x1", [P, ST, D])
    gathered = sb("gathered", [P, ST * TOPK, D])
    slots = sb("slots", [P, ST, 8], U32)
    w8 = sb("w8", [P, ST, 8])
    x2 = sb("x2", [P, ST, D])
    x2_kept = sb("x2_kept", [P, ST, D])
    stats, mv = sb("stats", [P, ST, 6]), sb("mv", [P, ST, 2])
    var_eps, rstd = sb("var_eps", [P, ST]), sb("rstd", [P, ST])
    xln, xlnT = sb("xln", [P, ST, D]), sb("xlnT", [P, DC, S])
    ctxT = sb("ctxT", [P, DC, S])
    qT, kT = sb("qT", [P, HD // P, S]), sb("kT", [P, HD // P, S])
    v = sb("v", [P, ST, HD])
    neg_max = sb("neg_max", [P, 4, ST])
    sums, inv = sb("sums", [P, 4, ST]), sb("inv", [P, 4, ST])
    probs = sb("probs", [P, 4, ST, S])
    vs = sb("vs", [P, 4, ST, DK])
    attnT = sb("attnT", [P, HD // P, S])
    x3 = sb("x3", [P, ST, D])
    stats2, mv2 = sb("stats2", [P, ST, 6]), sb("mv2", [P, ST, 2])
    var_eps2, rstd2 = sb("var_eps2", [P, ST]), sb("rstd2", [P, ST])
    xn, xnT = sb("xn", [P, ST, D]), sb("xnT", [P, DC, S])
    r_negmax, r_exp = sb("r_negmax", [P, ST]), sb("r_exp", [P, ST, E1])
    r_sum, r_inv = sb("r_sum", [P, ST]), sb("r_inv", [P, ST])
    ident, tanh_g, slots_all, w_all = keep["ident"], keep["tanh_g"], keep["slots_all"], keep["w_all"]
    gate_all = keep["gate_all"]

    ps_s = [psum(f"ps_c_s{i}") for i in range(4)]
    ps_o = [psum(f"ps_c_o{i}") for i in range(2)]
    ps_m = [psum(f"ps_c_m{i}") for i in range(2)]

    s_const, s_x, s_ctx = sem("c_const_loaded"), sem("c_x1_loaded"), sem("c_ctx_loaded")
    s_x3, s_xn = sem("c_x3_stored"), sem("c_x3n_stored")
    s_gat = sem("c_rows_gathered")
    p_const, v_const = sem("c_pool_consts"), sem("c_vector_consts")
    v_waits, p_waits = sem("c_vector_waits"), sem("c_pool_waits")
    v_sl, v_add, v_comb = sem("c_slots_copied"), sem("c_rows_chain"), sem("c_x2_ready")
    v_ln, p_rs, p_rsc, v_xln = sem("c_ln_chain"), sem("c_rstd"), sem("c_rstd_chain"), sem("c_xln_ready")
    t_x, a_x = sem("c_xlnT_in_psum"), sem("c_xlnT_ready")
    t_fill = sem("c_projection_in_psum")
    ev = [sem("c_projection_even_bank_ready"), sem("c_projection_odd_bank_ready")]
    t_s, v_m, a_e = sem("c_scores_in_psum"), sem("c_max_ready"), sem("c_probs_ready")
    v_inv, v_vs = sem("c_inv_sums"), sem("c_v_scaled")
    t_pv = sem("c_pv_done")
    ot = [sem("c_attnT_even_ready"), sem("c_attnT_odd_ready")]
    t_wo, v_x3, p_x2 = sem("c_wo_in_psum"), sem("c_x3_ready"), sem("c_x2_kept")
    v_st, p_rs2, p_rs2c, v_xn = sem("c_ln2_chain"), sem("c_rstd2"), sem("c_rstd2_chain"), sem("c_xn_ready")
    t_xn, a_xn = sem("c_xnT_in_psum"), sem("c_xnT_ready")
    t_r, v_rm, a_r, v_ri, v_gate = (sem(f"c_router_{n}") for n in ("in_psum", "max", "exp", "inv", "scores"))

    FILLS = 12
    PAIRS = HEADS // 2
    LAG = 3

    with nc.Block() as block:

        @block.sync
        def _(sp):
            sp.dma_start(x1[:], tiles(dram["x1"][0])).then_inc(s_x, 16)
            sp.dma_start(ctxT[:], tiles(io["ctxT"][0])).then_inc(s_ctx, 16)
            for dst, src in ((wq, io["w_q"]), (wk, io["w_k"]), (wv, io["w_v"]), (wo, io["w_o"]), (router_w, io["router_w"])):
                sp.dma_start(dst[:], src.rearrange("(c p) n -> p c n", p=P)).then_inc(s_const, 16)
            for e in range(E1):
                sp.dma_start(keep["f1"][:, e], io["f1"][e].rearrange("(c p) n -> p c n", p=P)).then_inc(keep["s_f1"], 16)

            def loads(b):
                sp.wait_ge(v_comb, b + 1)
                sp.dma_start(x1[:], tiles(dram["x1"][b + 1])).then_inc(s_x, 16)
                sp.wait_ge(t_fill, FILLS * (b + 1))
                sp.dma_start(ctxT[:], tiles(io["ctxT"][b + 1])).then_inc(s_ctx, 16)

            def stores(p):
                sp.wait_ge(v_x3, p + 1)
                sp.dma_start(tiles(dram["x3"][p]), x3[:]).then_inc(s_x3, 16)
                sp.wait_ge(v_xn, p + 1)
                sp.dma_start(tiles(dram["x3n"][p]), xn[:]).then_inc(s_xn, 16)

            loads(0)
            with sp.Fori(1, NB - 1) as b:
                loads(b)
                stores(b - 1)
            stores(NB - 2)
            stores(NB - 1)
            sp.wait_ge(s_x3, 16 * NB)
            sp.wait_ge(s_xn, 16 * NB)
            sp.wait_ge(keep["s_f1"], 16 * E1)

        @block.gpsimd
        def _(pool):
            pool.memset(minus_half[:], -0.5).then_inc(p_const, 1)
            pool.memset(gathered[:], 0.0).then_inc(p_const, 1)
            pool.wait_ge(p_const, 2)

            def rsqrt(b, mv_, var_eps_, rstd_, chain, stats_done, ready):
                after(pool, stats_done, (b + 1) * 4, alone=p_waits)
                pool.tensor_scalar(var_eps_[:], mv_[:, :, 1], EPS, None, ALU.add).then_inc(chain, 1)
                pool.wait_ge(chain, b + 1)
                pool.tensor_tensor(rstd_[:], var_eps_[:], minus_half[:], ALU.pow).then_inc(ready, 1)

            def gather(b):
                after(pool, v_comb, b, alone=p_waits)
                after(pool, v_sl, b + 1, alone=p_waits)
                for t in range(ST):
                    for k in range(TOPK):
                        pool.indirect_dma_start(
                            out=gathered[:, t * TOPK + k, :], out_offset=None, in_=dram["y"],
                            in_offset=bass.IndirectOffsetOnAxis(ap=slots[:, t, k:k + 1], axis=0),
                            bounds_check=E0 * CAP0 - 1, oob_is_err=False).then_inc(s_gat, 16)

            def keep_x2(b):
                after(pool, v_comb, b + 1, alone=p_waits)
                after(pool, v_x3, b, alone=p_waits)
                pool.tensor_copy(x2_kept[:], x2[:]).then_inc(p_x2, 1)

            def batch(b, p, last):
                keep_x2(b)
                if p is not None:
                    rsqrt(p, mv2, var_eps2, rstd2, p_rs2c, v_st, p_rs2)
                if not last:
                    gather(b + 1)
                    rsqrt(b + 1, mv, var_eps, rstd, p_rsc, v_ln, p_rs)

            gather(0)
            rsqrt(0, mv, var_eps, rstd, p_rsc, v_ln, p_rs)
            batch(0, None, False)
            with pool.Fori(1, NB - 1) as b:
                batch(b, b - 1, False)
            batch(NB - 1, NB - 2, True)
            rsqrt(NB - 1, mv2, var_eps2, rstd2, p_rs2c, v_st, p_rs2)

        @block.vector
        def _(dve):
            def take_slots(b):
                after(dve, s_gat, 16 * ST * TOPK * b)
                dve.tensor_copy(slots[:], slots_all[:, bass.ds(b * ST, ST), :] if not isinstance(b, int)
                                else slots_all[:, b * ST:(b + 1) * ST, :])
                dve.tensor_scalar(w8[:, :, 0:TOPK], w_all[:, bass.ds(b * ST, ST), 0:TOPK] if not isinstance(b, int)
                                  else w_all[:, b * ST:(b + 1) * ST, 0:TOPK], tanh_g[:, 2:3], None, ALU.mult).then_inc(v_sl, 1)

            def combine(b):
                dve.wait_ge(s_x, 16 * (b + 1))
                dve.wait_ge(s_gat, 16 * ST * TOPK * (b + 1))
                dve.wait_ge(v_sl, b + 1)
                after(dve, p_x2, b)
                c = Chain(dve, v_add, ST * (TOPK - 1), b)
                for k in range(TOPK):
                    if k:
                        c.wait()
                    for t in range(ST):
                        ins = dve.scalar_tensor_tensor(out=x2[:, t, :], in0=gathered[:, t * TOPK + k, :],
                                                       scalar=w8[:, t, k:k + 1], in1=(x2 if k else x1)[:, t, :],
                                                       op0=ALU.mult, op1=ALU.add)
                        if k < TOPK - 1:
                            c.done(ins)
                c.end()
                ins.then_inc(v_comb, 1)

            def statistics(b, src, stats_, mv_, chain_sem, ready, value):
                c = Chain(dve, chain_sem, 4, b, alone=v_waits)
                dve.wait_ge(ready, value)
                for t in range(ST):
                    c.done(dve.bn_stats(stats_[:, t, :], src[:, t, :]))
                c.wait()
                for t in range(ST):
                    c.done(dve.bn_aggr(mv_[:, t, :], stats_[:, t, :]))
                c.wait()
                c.end()

            def layernorm1(b):
                dve.wait_ge(p_rs, b + 1)
                after(dve, t_x, b)
                for t in range(ST):
                    ins = dve.tensor_scalar(xln[:, t, :], x2[:, t, :], mv[:, t, 0:1], rstd[:, t:t + 1],
                                            ALU.subtract, ALU.mult)
                ins.then_inc(v_xln, 1)

            def layernorm2(p):
                dve.wait_ge(p_rs2, p + 1)
                after(dve, s_xn, 16 * p)
                for t in range(ST):
                    ins = dve.tensor_scalar(xn[:, t, :], x3[:, t, :], mv2[:, t, 0:1], rstd2[:, t:t + 1],
                                            ALU.subtract, ALU.mult)
                ins.then_inc(v_xn, 1)

            def fill_evac(b, n):
                dve.wait_ge(t_fill, FILLS * b + n + 1)
                evacuate(lambda dst, src, scale: dve.tensor_scalar(dst, src, scale, None, ALU.mult) if scale != 1.0
                         else dve.tensor_copy(dst, src), n, ps_m[1]).then_inc(ev[1], 1)

            def evacuate(copy, n, bank):
                src = bank[:, :].rearrange("p (c s) -> p c s", c=2)
                if n < 4:
                    return copy(qT[:, 2 * n:2 * n + 2, :], src, DK ** -0.5)
                if n < 8:
                    return copy(kT[:, 2 * (n - 4):2 * (n - 4) + 2, :], src, 1.0)
                return copy(v[:, (n - 8) // 2, (n % 2) * 512:(n % 2 + 1) * 512], bank[:, :], 1.0)

            keep["evacuate"] = evacuate

            def head_max(b, i):
                dve.wait_ge(t_s, HEADS * b + i + 1)
                dve.tensor_reduce(neg_max[:, i % 4, :], ps_s[i % 4][:, :].rearrange("p (k s) -> p k s", k=ST),
                                  AX, ALU.max, negate=True).then_inc(v_m, 1)

            def scale_v(b, i):
                dve.wait_ge(a_e, HEADS * b + i + 1)
                dve.reciprocal(inv[:, i % 4, :], sums[:, i % 4, :]).then_inc(v_inv, 1)
                dve.wait_ge(v_inv, HEADS * b + i + 1)
                after(dve, t_pv, HEADS * b + i - 3)
                dve.tensor_tensor(vs[:, i % 4, :, :], v[:, :, i * DK:(i + 1) * DK],
                                  inv[:, i % 4, :].unsqueeze(2).broadcast_to([P, ST, DK]), ALU.mult).then_inc(v_vs, 1)

            def attnT_evac(b, c):
                dve.wait_ge(t_pv, HEADS * b + 2 * c + 2)
                dve.tensor_copy(attnT[:, c, :], ps_o[1][:, 0:S]).then_inc(ot[1], 1)

            def add_attention(p):
                dve.wait_ge(t_wo, p + 1)
                dve.wait_ge(p_x2, p + 1)
                after(dve, s_x3, 16 * p)
                dve.scalar_tensor_tensor(out=x3[:], in0=ps_m[1][:, :], scalar=tanh_g[:, 1:2], in1=x2_kept[:],
                                         op0=ALU.mult, op1=ALU.add).then_inc(v_x3, 1)
                statistics(p, x3, stats2, mv2, v_st, v_x3, p + 1)

            def tail_at(p, i):
                if p is None:
                    return
                if i == 0:
                    add_attention(p)
                if i == 1:
                    layernorm2(p)
                if i == 6:
                    dve.wait_ge(t_r, p + 1)
                    dve.tensor_reduce(r_negmax[:], ps_m[1][:, 0:ST * E1].rearrange("p (t e) -> p t e", e=E1),
                                      AX, ALU.max, negate=True).then_inc(v_rm, 1)
                if i == 7:
                    dve.wait_ge(a_r, p + 1)
                    dve.reciprocal(r_inv[:], r_sum[:]).then_inc(v_ri, 1)
                    dve.wait_ge(v_ri, p + 1)
                    for t in range(ST):
                        dst = gate_all[:, t, p * E1:(p + 1) * E1] if isinstance(p, int) else gate_all[:, t, bass.ds(p * E1, E1)]
                        ins = dve.tensor_scalar(dst, r_exp[:, t, :], r_inv[:, t:t + 1], None, ALU.mult)
                    ins.then_inc(v_gate, 1)

            def batch(b, p, last):
                for n in range(0, FILLS, 2):
                    fill_evac(b, n)
                for i in range(HEADS + LAG):
                    if i < HEADS:
                        head_max(b, i)
                    if 1 <= i < HEADS + 1:
                        scale_v(b, i - 1)
                    if i >= LAG and (i - LAG) % 4 == 3:
                        attnT_evac(b, (i - LAG) // 2)
                    tail_at(p, i)
                    if not last:
                        if i == 8:
                            take_slots(b + 1)
                        if i == 12:
                            combine(b + 1)
                            statistics(b + 1, x2, stats, mv, v_ln, v_comb, b + 2)
                        if i == 14:
                            layernorm1(b + 1)

            dve.wait_ge(p_const, 2)
            take_slots(0)
            combine(0)
            statistics(0, x2, stats, mv, v_ln, v_comb, 1)
            layernorm1(0)
            batch(0, None, False)
            with dve.Fori(1, NB - 1) as b:
                batch(b, b - 1, False)
            batch(NB - 1, NB - 2, True)
            for i in range(HEADS):
                tail_at(NB - 1, i)

        @block.scalar
        def _(act):
            def fill_evac(b, n):
                act.wait_ge(t_fill, FILLS * b + n + 1)
                keep["evacuate"](lambda dst, src, scale: act.activation(dst, src, ACT.Copy, scale=scale),
                                 n, ps_m[0]).then_inc(ev[0], 1)

            def exponentials(b, i):
                act.wait_ge(v_m, HEADS * b + i + 1)
                after(act, t_pv, HEADS * b + i - 3)
                after(act, v_inv, HEADS * b + i - 3)
                for k in range(ST):
                    ins = act.activation(probs[:, i % 4, k, :], ps_s[i % 4][:, k * S:(k + 1) * S], ACT.Exp,
                                         bias=neg_max[:, i % 4, k:k + 1], accum_out=sums[:, i % 4, k:k + 1])
                ins.then_inc(a_e, 1)

            def tail_at(p, i):
                if p is None:
                    return
                if i == 4:
                    act.wait_ge(t_xn, p + 1)
                    act.activation(xnT[:], ps_m[0][:, :], ACT.Copy).then_inc(a_xn, 1)
                if i == 6:
                    act.wait_ge(v_rm, p + 1)
                    after(act, v_gate, p)
                    for t in range(ST):
                        ins = act.activation(r_exp[:, t, :], ps_m[1][:, t * E1:(t + 1) * E1], ACT.Exp,
                                             bias=r_negmax[:, t:t + 1], accum_out=r_sum[:, t:t + 1])
                    ins.then_inc(a_r, 1)

            def batch(b, p):
                act.wait_ge(t_x, b + 1)
                act.activation(xlnT[:], ps_m[0][:, :], ACT.Copy).then_inc(a_x, 1)
                for n in range(1, FILLS, 2):
                    fill_evac(b, n)
                for i in range(HEADS + LAG):
                    if i < HEADS:
                        exponentials(b, i)
                    if i >= LAG and (i - LAG) % 4 == 1:
                        c = (i - LAG) // 2
                        act.wait_ge(t_pv, HEADS * b + 2 * c + 2)
                        act.activation(attnT[:, c, :], ps_o[0][:, 0:S], ACT.Copy).then_inc(ot[0], 1)
                    tail_at(p, i)

            batch(0, None)
            with act.Fori(1, NB) as b:
                batch(b, b - 1)
            for i in range(HEADS):
                tail_at(NB - 1, i)

        @block.tensor
        def _(pe):
            pe.wait_ge(s_const, 16 * 5)

            def transposed(dst, src):
                for c in range(DC):
                    for t in range(ST):
                        ins = pe.transpose(dst[:, c * S + t * P:c * S + (t + 1) * P], src[:, t, c * P:(c + 1) * P], ident[:])
                return ins

            def project(b, p):
                pe.wait_ge(v_xln, b + 1)
                transposed(ps_m[0], xln).then_inc(t_x, 1)
                pe.wait_ge(s_ctx, 16 * (b + 1))
                if p is not None:
                    after(pe, a_r, p)
                for n in range(FILLS):
                    if n == 0:
                        pe.wait_ge(a_x, b + 1)
                    elif n >= 2:
                        pe.wait_ge(ev[(n + 1) % 2], FILLS // 2 * b + n // 2)
                    bank = ps_m[(n + 1) % 2]
                    if n < 8:
                        w, x = (wq, xlnT) if n < 4 else (wk, ctxT)
                        for j in range(2):
                            c = 2 * (n % 4) + j
                            for k in range(DC):
                                ins = pe.matmul(bank[:, j * S:(j + 1) * S], w[:, k, c * P:(c + 1) * P], x[:, k, :],
                                                start=(k == 0), stop=(k == DC - 1))
                    else:
                        t, half = (n - 8) // 2, n % 2
                        for k in range(DC):
                            ins = pe.matmul(bank[:, :], ctxT[:, k, t * P:(t + 1) * P], wv[:, k, half * 512:(half + 1) * 512],
                                            start=(k == 0), stop=(k == DC - 1))
                    ins.then_inc(t_fill, 1)

            def head_scores(b, i):
                c, r = i // 2, DK * (i % 2)
                after(pe, a_e, HEADS * b + i - 3)
                for k in range(ST):
                    ins = pe.matmul(ps_s[i % 4][:, k * S:(k + 1) * S], kT[r:r + DK, c, k * P:(k + 1) * P],
                                    qT[r:r + DK, c, :], start=True, stop=True)
                ins.then_inc(t_s, 1)

            def head_values(b, i):
                c, r = i // 2, DK * (i % 2)
                pe.wait_ge(v_vs, HEADS * b + i + 1)
                if i % 2 == 0:
                    after(pe, ot[c % 2], PAIRS // 2 * b + c // 2)
                for k in range(ST):
                    ins = pe.matmul(ps_o[c % 2][r:r + DK, 0:S], vs[:, i % 4, k, :], probs[:, i % 4, k, :],
                                    start=(k == 0), stop=(k == ST - 1))
                ins.then_inc(t_pv, 1)

            def tail_at(p, i):
                if p is None:
                    return
                if i == 0:
                    for j in range(2):
                        pe.wait_ge(ot[j], PAIRS // 2 * (p + 1))
                    for t in range(ST):
                        for c in range(HD // P):
                            ins = pe.matmul(ps_m[1][:, t * D:(t + 1) * D], attnT[:, c, t * P:(t + 1) * P], wo[:, c, :],
                                            start=(c == 0), stop=(c == HD // P - 1))
                    ins.then_inc(t_wo, 1)
                if i == 4:
                    pe.wait_ge(v_xn, p + 1)
                    transposed(ps_m[0], xn).then_inc(t_xn, 1)
                if i == 6:
                    pe.wait_ge(a_xn, p + 1)
                    for t in range(ST):
                        for k in range(DC):
                            ins = pe.matmul(ps_m[1][:, t * E1:(t + 1) * E1], xnT[:, k, t * P:(t + 1) * P], router_w[:, k, :],
                                            start=(k == 0), stop=(k == DC - 1))
                    ins.then_inc(t_r, 1)

            def batch(b, p):
                project(b, p)
                for j in range(2):
                    pe.wait_ge(ev[j], FILLS // 2 * (b + 1))
                for i in range(HEADS + LAG):
                    if i < HEADS:
                        head_scores(b, i)
                    tail_at(p, i)
                    if i >= LAG:
                        head_values(b, i - LAG)

            batch(0, None)
            with pe.Fori(1, NB) as b:
                batch(b, b - 1)
            for i in range(HEADS):
                tail_at(NB - 1, i)


def choose_tokens(nc, sb, psum, sem, io, dram, keep, NB):
    rows_of = [(o, min(P, NB * E1 - o)) for o in range(0, NB * E1, P)]
    NT = len(rows_of)
    WIDE = S + 8
    work = sb("work", [P, NT, WIDE])
    top8 = sb("top8", [P, NT, 8])
    ones = sb("ones", [P, S])
    chosen, counted, place = (sb(n, [P, NT, S]) for n in ("chosen", "counted", "place"))
    gate_all, pos_all, ident = keep["gate_all"], keep["pos_all"], keep["ident"]
    ps = [psum(f"ps_e{i}") for i in range(2)]
    t_sc, v_ch, t_pos, v_pos = sem("e_scores_in_psum"), sem("e_chain"), sem("e_places_in_psum"), sem("e_places_ready")
    v_done = sem("e_places_turned")

    with nc.Block() as block:

        @block.tensor
        def _(pe):
            for i, (o, n) in enumerate(rows_of):
                for t in range(ST):
                    ins = pe.transpose(ps[0][0:n, i * S + t * P:i * S + (t + 1) * P], gate_all[:, t, o:o + n], ident[:])
            ins.then_inc(t_sc, 1)
            pe.wait_ge(v_pos, 1)
            for i, (o, n) in enumerate(rows_of):
                for t in range(ST):
                    ins = pe.transpose(ps[1][:, t * NB * E1 + o:t * NB * E1 + o + n], place[0:n, i, t * P:(t + 1) * P],
                                       ident[0:n, 0:n])
            ins.then_inc(t_pos, 1)

        @block.vector
        def _(dve):
            c = Chain(dve, v_ch, 0, 0)
            c.done(dve.memset(ones[:], 1.0))
            c.done(dve.memset(work[:, :, S:WIDE], -1.0))
            dve.wait_ge(t_sc, 1)
            for i, (o, n) in enumerate(rows_of):
                c.done(dve.tensor_copy(work[0:n, i, 0:S], ps[0][0:n, i * S:(i + 1) * S]))
            c.wait()
            for turn in range((CAP1 + 7) // 8):
                take = min(8, CAP1 - 8 * turn)
                for i, (o, n) in enumerate(rows_of):
                    c.done(dve.max(top8[0:n, i, :], work[0:n, i, :]))
                c.wait()
                if take < 8:
                    c.done(dve.memset(top8[:, :, take:8], -1.0))
                    c.wait()
                for i, (o, n) in enumerate(rows_of):
                    c.done(dve.match_replace(work[0:n, i, :], top8[0:n, i, :], work[0:n, i, :], -2.0))
                c.wait()
            for i, (o, n) in enumerate(rows_of):
                c.done(dve.tensor_scalar(chosen[0:n, i, :], work[0:n, i, 0:S], -1.5, None, ALU.is_lt))
            c.wait()
            for i, (o, n) in enumerate(rows_of):
                c.done(dve.tensor_tensor_scan(counted[0:n, i, :], ones[0:n, :], chosen[0:n, i, :], 0.0, ALU.mult, ALU.add))
            c.wait()
            for i, (o, n) in enumerate(rows_of):
                c.done(dve.tensor_tensor(place[0:n, i, :], counted[0:n, i, :], chosen[0:n, i, :], ALU.mult))
            c.wait()
            dve.tensor_copy(ones[:, 0:1], ones[:, 1:2]).then_inc(v_pos, 1)
            dve.wait_ge(t_pos, 1)
            dve.tensor_copy(pos_all[:, :, 0:NB * E1],
                            ps[1][:, 0:ST * NB * E1].rearrange("p (t e) -> p t e", t=ST)).then_inc(v_done, 1)


def expert_choice(nc, sb, psum, sem, io, out, dram, keep, NB):
    f1 = keep["f1"]
    f2 = sb("f2", [P, E1, HC, D])
    b1, b2 = sb("b1", [P, E1, HC]), sb("b2", [P, E1, DC])
    slot_id = sb("slot_id", [P, CAP1])
    xn, x3 = sb("xn", [P, ST, D]), sb("x3", [P, ST, D])
    sel, gated = sb("sel", [P, ST, SLOTS]), sb("gated", [P, ST, SLOTS])
    tokT = sb("tokT", [P, DC, SLOTS])
    gatedT = sb("gatedT", [GS, GC, S])
    hid = sb("hid", [P, 2, HC, CAP1])
    yT = sb("yT", [P, DC, SLOTS])
    y = sb("y", [GS, GC, D])
    ident, tanh_g, gate_all, pos_all = keep["ident"], keep["tanh_g"], keep["gate_all"], keep["pos_all"]

    ps_h = [[psum(f"ps_d_h{i}{j}") for j in range(2)] for i in range(2)]
    ps_y = [psum(f"ps_d_y{i}") for i in range(2)]
    ps_m = [psum(f"ps_d_m{i}") for i in range(2)]

    s_f2 = [sem(f"d_f2_{e % 2}_loaded") for e in range(2)]
    s_const, s_xn, s_x3, s_out = sem("d_const_loaded"), sem("d_xn_loaded"), sem("d_x3_loaded"), sem("d_out_stored")
    p_const = sem("d_pool_const")
    p_waits = sem("d_pool_waits")
    v_sel, p_gated = sem("d_sel_ready"), sem("d_gated_ready")
    t_tok = sem("d_tokens_in_psum")
    tok_ev = [sem("d_tokens_even_ready"), sem("d_tokens_odd_ready")]
    t_gt = sem("d_gatedT_in_psum")
    gt_ev = [sem("d_gatedT_even_ready"), sem("d_gatedT_odd_ready")]
    t_h, a_h = sem("d_hidden_in_psum"), sem("d_hidden_ready")
    t_y, v_y = sem("d_yT_in_psum"), sem("d_yT_ready")
    t_yt = sem("d_y_in_psum")
    yt_ev = [sem("d_y_even_ready"), sem("d_y_odd_ready")]
    t_out, v_out = sem("d_sum_in_psum"), sem("d_out_ready")

    HALF = SLOTS // 2
    GROUPS = [(0, 2), (2, 2), (4, 1)]

    def dyn(ap, t, b):
        return ap[:, t, b * E1:(b + 1) * E1] if isinstance(b, int) else ap[:, t, bass.ds(b * E1, E1)]

    with nc.Block() as block:

        @block.sync
        def _(sp):
            sp.dma_start(xn[:], tiles(dram["x3n"][0])).then_inc(s_xn, 16)
            sp.dma_start(x3[:], tiles(dram["x3"][0])).then_inc(s_x3, 16)
            sp.dma_start(b1[:], io["fb1"].rearrange("e (c p) -> p e c", p=P), allow_slow_non_contiguous=True).then_inc(s_const, 16)
            sp.dma_start(b2[:], io["fb2"].rearrange("e (c p) -> p e c", p=P), allow_slow_non_contiguous=True).then_inc(s_const, 16)
            for e in range(E1):
                if e >= 2:
                    sp.wait_ge(s_f2[e % 2], 16 * (e // 2))
                sp.dma_start(f2[:, e], io["f2"][e].rearrange("(c p) n -> p c n", p=P)).then_inc(s_f2[e % 2], 16)

            def load_xn(b):
                sp.wait_ge(t_tok, 4 * b)
                sp.dma_start(xn[:], tiles(dram["x3n"][b])).then_inc(s_xn, 16)

            def store(p):
                sp.wait_ge(v_out, p + 1)
                sp.dma_start(tiles(out[p]), x3[:]).then_inc(s_out, 16)
                sp.wait_ge(s_out, 16 * (p + 1))

            def load_x3(b):
                sp.dma_start(x3[:], tiles(dram["x3"][b])).then_inc(s_x3, 16)

            load_xn(1)
            with sp.Fori(1, NB - 1) as b:
                load_xn(b + 1)
                store(b - 1)
                load_x3(b)
            store(NB - 2)
            load_x3(NB - 1)
            store(NB - 1)

        @block.gpsimd
        def _(pool):
            pool.iota(slot_id[:], [[1, CAP1]], base=1, channel_multiplier=0,
                      allow_small_or_imprecise_dtypes=True).then_inc(p_const, 1)

            def gate(b):
                after(pool, v_sel, b + 1, alone=p_waits)
                after(pool, t_gt, len(GROUPS) * b, alone=p_waits)
                for t in range(ST):
                    ins = pool.tensor_tensor(gated[:, t, :].rearrange("p (e c) -> p e c", c=CAP1),
                                             sel[:, t, :].rearrange("p (e c) -> p e c", c=CAP1),
                                             dyn(gate_all, t, b).unsqueeze(2).broadcast_to([P, E1, CAP1]), ALU.mult)
                ins.then_inc(p_gated, 1)

            gate(0)
            gate(1)
            with pool.Fori(2, NB) as b:
                gate(b)

        @block.vector
        def _(dve):
            dve.wait_ge(p_const, 1)
            dve.wait_ge(s_const, 32)

            def select(b):
                after(dve, t_tok, 4 * b)
                after(dve, p_gated, b)
                for t in range(ST):
                    ins = dve.tensor_tensor(sel[:, t, :].rearrange("p (e c) -> p e c", c=CAP1),
                                            slot_id[:].unsqueeze(1).broadcast_to([P, E1, CAP1]),
                                            dyn(pos_all, t, b).unsqueeze(2).broadcast_to([P, E1, CAP1]), ALU.is_equal)
                ins.then_inc(v_sel, 1)

            def tail(p):
                dve.wait_ge(t_yt, 3 * p + 2)
                dve.tensor_copy(y[:, 2:4, :], ps_m[1][0:GS, :].rearrange("p (c d) -> p c d", c=2)).then_inc(yt_ev[1], 1)

            def add_out(p):
                dve.wait_ge(t_out, p + 1)
                dve.wait_ge(s_x3, 16 * (p + 1))
                dve.scalar_tensor_tensor(out=x3[:], in0=ps_m[1][:, :], scalar=tanh_g[:, 3:4], in1=x3[:],
                                         op0=ALU.mult, op1=ALU.add).then_inc(v_out, 1)

            def tokens_evac(b, j):
                dve.wait_ge(t_tok, 4 * b + j + 1)
                dve.tensor_copy(tokT[:, j // 2, (j % 2) * HALF:(j % 2 + 1) * HALF], ps_m[1][:, 0:HALF]).then_inc(tok_ev[1], 1)

            def yT_evac(b, e):
                dve.wait_ge(t_y, E1 * b + e + 1)
                for c in range(DC):
                    ins = dve.tensor_scalar(yT[:, c, e * CAP1:(e + 1) * CAP1], ps_y[e % 2][:, c * CAP1:(c + 1) * CAP1],
                                            b2[:, e, c:c + 1], None, ALU.add)
                ins.then_inc(v_y, 1)

            def batch(b, p, last):
                if p is not None:
                    tail(p)
                tokens_evac(b, 0)
                if p is not None:
                    add_out(p)
                tokens_evac(b, 3)
                dve.wait_ge(t_gt, 3 * b + 2)
                dve.tensor_copy(gatedT[:, 2:4, :], ps_m[1][0:GS, :].rearrange("p (c s) -> p c s", c=2)).then_inc(gt_ev[1], 1)
                for e in range(E1):
                    if e == 2 and not last:
                        select(b + 1)
                    yT_evac(b, e)

            select(0)
            batch(0, None, False)
            with dve.Fori(1, NB - 1) as b:
                batch(b, b - 1, False)
            batch(NB - 1, NB - 2, True)
            tail(NB - 1)
            add_out(NB - 1)

        @block.scalar
        def _(act):
            act.wait_ge(s_const, 32)

            def tail(p, g):
                o, n = GROUPS[g]
                act.wait_ge(t_yt, 3 * p + g + 1)
                act.activation(y[:, o:o + n, :], ps_m[0][0:GS, 0:n * D].rearrange("p (c d) -> p c d", c=n),
                               ACT.Copy).then_inc(yt_ev[0], 1)

            def tokens_evac(b, j):
                act.wait_ge(t_tok, 4 * b + j + 1)
                act.activation(tokT[:, j // 2, (j % 2) * HALF:(j % 2 + 1) * HALF], ps_m[0][:, 0:HALF], ACT.Copy).then_inc(tok_ev[0], 1)

            def gatedT_evac(b, g):
                o, n = GROUPS[g]
                act.wait_ge(t_gt, 3 * b + g + 1)
                act.activation(gatedT[:, o:o + n, :], ps_m[0][0:GS, 0:n * S].rearrange("p (c d) -> p c d", c=n),
                               ACT.Copy).then_inc(gt_ev[0], 1)

            def batch(b, p):
                if p is not None:
                    tail(p, 0)
                    tail(p, 2)
                tokens_evac(b, 1)
                tokens_evac(b, 2)
                gatedT_evac(b, 0)
                gatedT_evac(b, 2)
                for e in range(E1):
                    act.wait_ge(t_h, E1 * b + e + 1)
                    after(act, t_y, E1 * b + e - 1)
                    for c in range(HC):
                        ins = act.activation(hid[:, e % 2, c, :], ps_h[e % 2][c // 4][:, (c % 4) * CAP1:(c % 4 + 1) * CAP1],
                                             ACT.Gelu, bias=b1[:, e, c:c + 1])
                    ins.then_inc(a_h, 1)

            batch(0, None)
            with act.Fori(1, NB) as b:
                batch(b, b - 1)
            tail(NB - 1, 0)
            tail(NB - 1, 2)

        @block.tensor
        def _(pe):
            def turn_y(p, g):
                o, n = GROUPS[g]
                for c in range(n):
                    for d in range(DC):
                        ins = pe.transpose(ps_m[g % 2][0:GS, c * D + d * P:c * D + (d + 1) * P],
                                           yT[:, d, (o + c) * GS:(o + c + 1) * GS], ident[:])
                ins.then_inc(t_yt, 1)

            def tokens(b, j):
                bank = ps_m[1 if j in (0, 3) else 0]
                c, half = j // 2, j % 2
                for t in range(ST):
                    ins = pe.matmul(bank[:, 0:HALF], xn[:, t, c * P:(c + 1) * P], sel[:, t, half * HALF:(half + 1) * HALF],
                                    start=(t == 0), stop=(t == ST - 1))
                ins.then_inc(t_tok, 1)

            def turn_gates(b, g):
                o, n = GROUPS[g]
                for c in range(n):
                    for t in range(ST):
                        ins = pe.transpose(ps_m[g % 2][0:GS, c * S + t * P:c * S + (t + 1) * P],
                                           gated[:, t, (o + c) * GS:(o + c + 1) * GS], ident[:])
                ins.then_inc(t_gt, 1)

            def sum_back(p):
                for t in range(ST):
                    for c in range(GC):
                        ins = pe.matmul(ps_m[1][:, t * D:(t + 1) * D], gatedT[:, c, t * P:(t + 1) * P], y[:, c, :],
                                        start=(c == 0), stop=(c == GC - 1))
                ins.then_inc(t_out, 1)

            def turn_all_y(p):
                pe.wait_ge(v_y, E1 * (p + 1))
                turn_y(p, 0)
                turn_y(p, 1)
                pe.wait_ge(yt_ev[0], 2 * p + 1)
                turn_y(p, 2)

            def up(b, e):
                if b is not None:
                    after(pe, a_h, E1 * b + e - 1)
                for c in range(HC):
                    for k in range(DC):
                        ins = pe.matmul(ps_h[e % 2][c // 4][:, (c % 4) * CAP1:(c % 4 + 1) * CAP1],
                                        f1[:, e, k, c * P:(c + 1) * P], tokT[:, k, e * CAP1:(e + 1) * CAP1],
                                        start=(k == 0), stop=(k == DC - 1))
                ins.then_inc(t_h, 1)

            def down(b, e):
                pe.wait_ge(a_h, E1 * b + e + 1)
                after(pe, v_y, E1 * b + e - 1)
                if isinstance(b, int) and b == 0:
                    pe.wait_ge(s_f2[e % 2], 16 * (e // 2 + 1))
                for d in range(DC):
                    for c in range(HC):
                        ins = pe.matmul(ps_y[e % 2][:, d * CAP1:(d + 1) * CAP1], f2[:, e, c, d * P:(d + 1) * P],
                                        hid[:, e % 2, c, :], start=(c == 0), stop=(c == HC - 1))
                ins.then_inc(t_y, 1)

            def batch(b, p):
                if p is not None:
                    turn_all_y(p)
                    pe.wait_ge(yt_ev[1], p + 1)
                pe.wait_ge(s_xn, 16 * (b + 1))
                pe.wait_ge(v_sel, b + 1)
                tokens(b, 0)
                if p is not None:
                    pe.wait_ge(yt_ev[0], 2 * (p + 1))
                tokens(b, 1)
                pe.wait_ge(tok_ev[1], 2 * b + 1)
                if p is not None:
                    sum_back(p)
                pe.wait_ge(tok_ev[0], 2 * b + 1)
                tokens(b, 2)
                if p is not None:
                    pe.wait_ge(v_out, p + 1)
                tokens(b, 3)
                pe.wait_ge(p_gated, b + 1)
                pe.wait_ge(tok_ev[0], 2 * (b + 1))
                turn_gates(b, 0)
                pe.wait_ge(tok_ev[1], 2 * (b + 1))
                turn_gates(b, 1)
                pe.wait_ge(gt_ev[0], 2 * b + 1)
                turn_gates(b, 2)
                up(b, 0)
                for e in range(1, E1):
                    up(b, e)
                    down(b, e - 1)
                down(b, E1 - 1)
                pe.wait_ge(gt_ev[0], 2 * (b + 1))
                pe.wait_ge(gt_ev[1], b + 1)

            batch(0, None)
            with pe.Fori(1, NB) as b:
                batch(b, b - 1)
            turn_all_y(NB - 1)
            pe.wait_ge(yt_ev[1], NB)
            pe.wait_ge(yt_ev[0], 2 * NB)
            sum_back(NB - 1)


def build(nc, io, out, NB=BATCH, NE=E0, debug=None):
    with ExitStack() as whole:
        stage_name = ["all"]

        def tensor(stack):
            return lambda name, shape, dt=F32: stack.enter_context(nc.sbuf_tensor(f"{stage_name[0]}_{name}", shape, dt))

        def bank(stack):
            return lambda name: stack.enter_context(nc.psum_tensor(name, [P, 512], F32))

        def sem(name):
            return whole.enter_context(nc.semaphore(name))

        dram = debug or {}
        for name, shape in (("x1", (BATCH, S, D)), ("rows", (E0 * CAP0, D)), ("y", (E0 * CAP0, D)),
                            ("x3", (BATCH, S, D)), ("x3n", (BATCH, S, D))):
            if name not in dram:
                dram[name] = nc.dram_tensor(f"{name}_scratch", shape, F32).ap()
        sb = tensor(whole)
        keep = {
            "ident": sb("ident", [P, P]), "gates": sb("gates", [P, 4]), "tanh_g": sb("tanh_g", [P, 4]),
            "slots_all": sb("slots_all", [P, BATCH * ST, 8], U32), "w_all": sb("w_all", [P, BATCH * ST, 8]),
        }
        with ExitStack() as stage:
            stage_name[0] = "a"
            attention_and_router(nc, tensor(stage), bank(stage), sem, io, dram, keep, NB)
        with ExitStack() as stage:
            stage_name[0] = "b"
            experts(nc, tensor(stage), bank(stage), sem, io, dram, keep, NE)
        keep["gate_all"] = sb("gate_all", [P, ST, BATCH * E1])
        keep["f1"] = sb("f1", [P, E1, DC, HID])
        keep["s_f1"] = sem("f1_loaded")
        with ExitStack() as stage:
            stage_name[0] = "c"
            attention_and_top(nc, tensor(stage), bank(stage), sem, io, dram, keep, NB)
        keep["pos_all"] = sb("pos_all", [P, ST, BATCH * E1])
        with ExitStack() as stage:
            stage_name[0] = "e"
            choose_tokens(nc, tensor(stage), bank(stage), sem, io, dram, keep, NB)
        with ExitStack() as stage:
            stage_name[0] = "d"
            expert_choice(nc, tensor(stage), bank(stage), sem, io, out, dram, keep, NB)


def lay_out(inputs, np):
    a = {k: np.asarray(v) for k, v in inputs.items()}
    t = lambda m: np.ascontiguousarray(np.swapaxes(m, -1, -2))
    return {
        "x": a["x"], "ctxT": t(a["ctx_1024"]), "mask": a["mask_1x1xSxS2_fk1"][0, 0],
        "gates": np.concatenate([a["g_xattn"], a["g_ffn"]]),
        "wq": a["L0_xattn_Wq"], "wk": a["L0_xattn_Wk"], "wv": a["L0_xattn_Wv"], "wo": a["L0_xattn_Wo"],
        "bq": a["L0_xattn_bq"], "bk": a["L0_xattn_bk"], "bv": a["L0_xattn_bv"], "bo": a["L0_xattn_bo"],
        "gate_w": t(a["L0_ffn_gate_w"]), "gate_b": a["L0_ffn_gate_b"],
        "w1": t(a["L0_ffn_w1"]), "w2": t(a["L0_ffn_w2"]), "w3": t(a["L0_ffn_w3"]),
        "ws1": t(a["L0_ffn_ws1"]), "ws2": t(a["L0_ffn_ws2"]), "ws3": t(a["L0_ffn_ws3"]),
        "w_q": a["L1_xattn_W_Q"], "w_k": a["L1_xattn_W_K"], "w_v": a["L1_xattn_W_V"], "w_o": a["L1_xattn_W_O"],
        "router_w": t(a["L1_ffn_router_w"]),
        "f1": a["L1_ffn_w1"], "fb1": a["L1_ffn_b1"], "f2": a["L1_ffn_w2"], "fb2": a["L1_ffn_b2"],
    }


def kernel(**inputs):
    import numpy as _np
    import concourse.bacc as _bacc
    from concourse import mybir as _mybir
    from concourse.bass_utils import run_bass_kernel_spmd as _run

    nc = _bacc.Bacc("TRN2", target_bir_lowering=False, num_devices=1)
    arrays, io = {}, {}
    for name, a in lay_out(inputs, _np).items():
        a = _np.ascontiguousarray(a)
        arrays[f"{name}_in"] = a
        io[name] = nc.dram_tensor(f"{name}_in", a.shape, _mybir.dt.from_np(a.dtype), kind="ExternalInput").ap()
    out = nc.dram_tensor("out", (BATCH, S, D), _mybir.dt.float32, kind="ExternalOutput").ap()
    build(nc, io, out)
    r = _run(nc, [arrays], core_ids=[0])
    return r.results[0]["out"]
```

```python
from contextlib import ExitStack

import concourse.bass as bass
from concourse import mybir

F32 = mybir.dt.float32
U32 = mybir.dt.uint32
I32 = mybir.dt.int32
ALU = mybir.AluOpType
ACT = mybir.ActivationFunctionType
AX = mybir.AxisListType.X

P = 128
BATCH, S, D = 32, 256, 256
ST = S // P
DC = D // P
HEADS = 16
DEPTH = D // HEADS
HPC = P // DEPTH
PACK = 4
PAD = P // PACK
NEG = -1.0e9
EPS = 1e-5
HUGE = 3.0e38
BIG_SLOT = 1.0e6

E0, TOPK, CAP0, I0 = 64, 6, 128, 176
SI = 2 * I0
SI_CHUNKS = [(0, 128), (128, 128), (256, SI - 256)]
I0_CHUNKS = [(0, 128), (128, I0 - 128)]

DK = 64
HD = HEADS * DK
E1, HID = 8, 1024
CAP1 = int(S * 2.0 / E1) + 1
SLOTS = E1 * CAP1
HC = HID // P
GC = 5
GS = SLOTS // GC


def after(eng, sem, value, alone=None):
    if isinstance(value, int) and value <= 0:
        return
    eng.wait_ge(sem, value)
    if alone is not None and not isinstance(value, int):
        eng.sem_inc(alone, 1)


class Chain:

    def __init__(self, eng, sem, size, step, alone=None):
        self.eng, self.sem, self.size, self.base, self.count = eng, sem, size, step * size, 0
        self.alone = alone

    def done(self, ins):
        self.count += 1
        ins.then_inc(self.sem, 1)

    def wait(self):
        after(self.eng, self.sem, self.base + self.count, self.alone)

    def end(self):
        assert self.count == self.size, (self.count, self.size)


class Fills:

    def __init__(self, per, present):
        self.per, self.present = per, present

    def upto(self, turn, n, bank=None):
        if not isinstance(turn, int):
            step = self.per if bank is None else self.per // 2
            return turn * step + (self.upto(1, n, bank) - step)
        return sum(self.present(r, m) and (r < turn or m <= n) and bank in (None, m % 2)
                   for r in range(-1, turn + 1) for m in range(self.per))


def tiles(ap):
    return ap.rearrange("(t p) d -> p t d", p=P)


def attention_and_router(nc, sb, psum, sem, io, dram, keep, NB):
    wq, wk, wv, wo = (sb(n, [P, DC, D]) for n in ("wq", "wk", "wv", "wo"))
    gate_w = sb("gate_w", [P, DC, E0])
    ws1, ws3 = sb("ws1", [P, DC, SI]), sb("ws3", [P, DC, SI])
    ws2 = sb("ws2", [P, 3, D])
    bq, bk = sb("bq", [P, DC]), sb("bk", [P, DC])
    bv, bo = sb("bv", [P, D]), sb("bo", [P, D])
    gate_b = sb("gate_b", [P, E0])
    mask = sb("mask", [P, ST, S])
    row_id = sb("row_id", [P, 1], I32)
    head_row_i = sb("head_row_i", [P, 1], I32)
    head_row = sb("head_row", [P, 1])
    head_id = sb("head_id", [P, HPC])
    head_scale = sb("head_scale", [P, HPC])
    upper = sb("upper", [P, P])
    ones = sb("ones", [P, P])
    minus_half = sb("minus_half", [P, 2])
    expert_base = sb("expert_base", [P, E0])

    x_in = sb("x_in", [P, ST, D])
    stats = sb("stats", [P, ST, 6])
    mv = sb("mv", [P, ST, 2])
    var_eps = sb("var_eps", [P, ST])
    rstd = sb("rstd", [P, ST])
    xln = sb("xln", [P, ST, D])
    xlnT = sb("xlnT", [P, DC, S])
    ctxT = sb("ctxT", [P, DC, S])
    q = sb("q", [P, DC, S])
    qm = sb("qm", [P, 4, S])
    kT = sb("kT", [P, DC, S])
    vx = sb("vx", [P, ST, HEADS * PAD])
    neg_s = sb("neg_s", [P, 4, ST, S])
    neg_max = sb("neg_max", [P, 4, ST])
    probs = sb("probs", [P, 4, ST, S])
    probsT = sb("probsT", [P, 2 * PACK, ST, S])
    oT = sb("oT", [P, 2, S])
    inv_sum = sb("inv_sum", [P, 2, ST, PACK])
    attn = sb("attn", [P, ST, D])
    attnT = sb("attnT", [P, DC, S])
    xr = sb("xr", [P, ST, D])
    stats2 = sb("stats2", [P, ST, 6])
    mv2 = sb("mv2", [P, ST, 2])
    var_eps2 = sb("var_eps2", [P, ST])
    rstd2 = sb("rstd2", [P, ST])
    xf = sb("xf", [P, ST, D])
    xfT = sb("xfT", [P, DC, S])
    r_negmax = sb("r_negmax", [P, ST])
    r_exp = sb("r_exp", [P, ST, E0])
    r_sum = sb("r_sum", [P, ST])
    r_inv = sb("r_inv", [P, ST])
    scores = sb("scores", [P, ST, E0])
    biased = sb("biased", [P, ST, E0 + 2])
    top8 = sb("top8", [P, ST, 8])
    replaced = sb("replaced", [P, ST, E0 + 2])
    chosen = sb("chosen", [P, ST, E0])
    seen = sb("seen", [P, E0])
    fits = sb("fits", [P, ST, E0])
    numbered = sb("numbered", [P, ST, E0])
    slot_of = sb("slot_of", [P, ST, E0])
    weight_of = sb("weight_of", [P, ST, E0])
    slot8 = sb("slot8", [P, ST, 8])
    no_slot = sb("no_slot", [P, ST, 8])
    picked = sb("picked", [P, ST * TOPK, E0])
    slots = sb("slots", [P, ST, 8], U32)
    w8 = sb("w8", [P, ST, 8])
    th = sb("th", [P, 2, S])
    silu2 = sb("silu2", [P, 2, S])
    hidden = sb("hidden", [P, 3, S])
    zero_rows = sb("zero_rows", [P, 8, D])
    ident, tanh_g, slots_all, w_all = keep["ident"], keep["tanh_g"], keep["slots_all"], keep["w_all"]

    ps_s = [psum(f"ps_s{i}") for i in range(2)]
    ps_t = [psum(f"ps_t{i}") for i in range(2)]
    ps_o = [psum(f"ps_o{i}") for i in range(2)]
    ps_m = [psum(f"ps_m{i}") for i in range(2)]

    s_const = sem("a_const_loaded")
    s_zero = sem("a_zeros_stored")
    s_x = sem("a_x_loaded")
    s_ctx = sem("a_ctx_loaded")
    s_xr = sem("a_residual_loaded")
    s_store = sem("a_x1_stored")
    s_scat = sem("a_rows_scattered")
    s_pc = sem("a_pool_consts")
    s_setup = sem("a_vector_setup")
    s_tanh = sem("a_tanh_ready")
    s_zset = sem("a_zero_rows_ready")
    v_waits, p_waits = sem("a_vector_waits"), sem("a_pool_waits")
    v_ln = sem("a_ln1_chain")
    p_rs1 = sem("a_rstd1_ready")
    p_rs1c = sem("a_rstd1_chain")
    v_xln = sem("a_xln_ready")
    t_xln = sem("a_xlnT_in_psum")
    a_xln = sem("a_xlnT_ready")
    t_q = sem("a_q_in_psum")
    a_q, v_q = sem("a_q_ready"), sem("a_head_q_ready")
    t_k, a_k = sem("a_k_in_psum"), sem("a_k_ready")
    t_v, v_v = sem("a_v_in_psum"), sem("a_v_ready")
    t_s = sem("a_scores_in_psum")
    v_m = sem("a_scores_masked")
    a_e = sem("a_probs_ready")
    t_t = sem("a_probsT_in_psum")
    te = [sem("a_probsT_even_ready"), sem("a_probsT_odd_ready")]
    t_pv = sem("a_pv_done")
    a_o, t_o = sem("a_oT_ready"), sem("a_o_in_psum")
    v_inv = sem("a_inv_sum")
    v_on = sem("a_attn_ready")
    t_ot, a_ot = sem("a_attnT_in_psum"), sem("a_attnT_ready")
    t_wo = sem("a_wo_in_psum")
    p_xr = sem("a_residual_biased")
    v_x1 = sem("a_x1_ready")
    v_st = sem("a_ln2_chain")
    p_rs2 = sem("a_rstd2_ready")
    p_rs2c = sem("a_rstd2_chain")
    v_xf = sem("a_xf_ready")
    t_xf, a_xf = sem("a_xfT_in_psum"), sem("a_xfT_ready")
    t_r = sem("a_logits_in_psum")
    v_rm = sem("a_logits_max")
    a_r = sem("a_logits_exp")
    v_rc = sem("a_router_chain")
    v_ch = sem("a_chosen_ready")
    t_pos = sem("a_positions_in_psum")
    p_seen = sem("a_seen_updated")
    v_pos = sem("a_position_chain")
    v_slot = sem("a_slots_ready")
    t_h = sem("a_hidden_in_psum")
    a_th = sem("a_hidden_tanh")
    v_hc = sem("a_hidden_chain")
    v_h = sem("a_hidden_ready")
    t_z = sem("a_z_in_psum")
    v_z = sem("a_x1z_ready")

    RC, PC = 8, 8
    STEPS = HEADS + 4
    GROUPS = HEADS // PACK
    N_CONST = 16

    with nc.Block() as block:

        @block.sync
        def _(sp):
            for dst, src in ((wq, io["wq"]), (wk, io["wk"]), (wv, io["wv"]), (wo, io["wo"]),
                             (gate_w, io["gate_w"]), (ws1, io["ws1"]), (ws3, io["ws3"])):
                sp.dma_start(dst[:], src.rearrange("(c p) n -> p c n", p=P)).then_inc(s_const, 16)
            sp.dma_start(ws2[:, 0:2, :], io["ws2"][0:256].rearrange("(c p) n -> p c n", p=P)).then_inc(s_const, 16)
            sp.dma_start(ws2[0:SI - 256, 2, :], io["ws2"][256:SI]).then_inc(s_const, 16)
            sp.dma_start(bq[:], io["bq"].rearrange("(c p) -> p c", p=P), allow_slow_non_contiguous=True).then_inc(s_const, 16)
            sp.dma_start(bk[:], io["bk"].rearrange("(c p) -> p c", p=P), allow_slow_non_contiguous=True).then_inc(s_const, 16)
            sp.dma_start(bv[:], io["bv"].rearrange("(a n) -> a n", a=1).broadcast_to([P, D])).then_inc(s_const, 16)
            sp.dma_start(bo[:], io["bo"].rearrange("(a n) -> a n", a=1).broadcast_to([P, D])).then_inc(s_const, 16)
            sp.dma_start(gate_b[:], io["gate_b"].rearrange("(a n) -> a n", a=1).broadcast_to([P, E0])).then_inc(s_const, 16)
            sp.dma_start(mask[:], tiles(io["mask"])).then_inc(s_const, 16)
            sp.dma_start(keep["gates"][:], io["gates"].rearrange("(a n) -> a n", a=1).broadcast_to([P, 4])).then_inc(s_const, 16)
            sp.dma_start(x_in[:], tiles(io["x"][0])).then_inc(s_x, 16)
            sp.dma_start(ctxT[:], tiles(io["ctxT"][0])).then_inc(s_ctx, 16)
            sp.dma_start(xr[:], tiles(io["x"][0])).then_inc(s_xr, 16)
            sp.wait_ge(s_zset, 1)
            for i in range(8):
                sp.dma_start(dram["rows"][i * 1024:(i + 1) * 1024].rearrange("(p r) d -> p r d", p=P),
                             zero_rows[:]).then_inc(s_zero, 16)

            def loads(b):
                sp.wait_ge(v_xln, b + 1)
                sp.dma_start(x_in[:], tiles(io["x"][b + 1])).then_inc(s_x, 16)
                sp.wait_ge(t_v, b + 1)
                sp.dma_start(ctxT[:], tiles(io["ctxT"][b + 1])).then_inc(s_ctx, 16)

            def store(p):
                sp.wait_ge(v_z, p + 1)
                sp.dma_start(tiles(dram["x1"][p]), xr[:]).then_inc(s_store, 16)
                sp.wait_ge(s_store, (p + 1) * 16)

            def residual(b):
                sp.dma_start(xr[:], tiles(io["x"][b])).then_inc(s_xr, 16)

            loads(0)
            loads(1)
            store(0)
            residual(1)
            with sp.Fori(2, NB - 1) as b:
                loads(b)
                store(b - 1)
                residual(b)
            store(NB - 2)
            residual(NB - 1)
            store(NB - 1)
            sp.wait_ge(s_zero, 16 * 8)

        @block.gpsimd
        def _(pool):
            pool.memset(zero_rows[:], 0.0).then_inc(s_zset, 1)
            pool.memset(ident[:], 0.0).then_inc(s_pc, 1)
            pool.memset(upper[:], 1.0).then_inc(s_pc, 1)
            pool.memset(ones[:], 1.0).then_inc(s_pc, 1)
            pool.memset(seen[:], 0.0).then_inc(s_pc, 1)
            pool.memset(minus_half[:], -0.5).then_inc(s_pc, 1)
            pool.iota(row_id[:], [[0, 1]], base=0, channel_multiplier=1).then_inc(s_pc, 1)
            pool.iota(expert_base[:], [[CAP0, E0]], base=0, channel_multiplier=0,
                      allow_small_or_imprecise_dtypes=True).then_inc(s_pc, 1)
            pool.iota(head_id[:], [[1, HPC]], base=0, channel_multiplier=0,
                      allow_small_or_imprecise_dtypes=True).then_inc(s_pc, 1)
            pool.wait_ge(s_pc, 8)
            pool.affine_select(out=ident[:], in_=ident[:], compare_op=ALU.not_equal, fill=1.0, base=0,
                               pattern=[[-1, P]], channel_multiplier=1).then_inc(s_pc, 1)
            pool.affine_select(out=upper[:], in_=upper[:], compare_op=ALU.is_ge, fill=0.0, base=0,
                               pattern=[[1, P]], channel_multiplier=-1).then_inc(s_pc, 1)

            def rsqrt(b, mv_, var_eps_, rstd_, chain, stats_done, stats_size, ready):
                after(pool, stats_done, (b + 1) * stats_size, alone=p_waits)
                pool.tensor_scalar(var_eps_[:], mv_[:, :, 1], EPS, None, ALU.add).then_inc(chain, 1)
                pool.wait_ge(chain, b + 1)
                pool.tensor_tensor(rstd_[:], var_eps_[:], minus_half[:], ALU.pow).then_inc(ready, 1)

            def bias_residual(p):
                pool.wait_ge(s_xr, (p + 1) * 16)
                if isinstance(p, int) and p == 0:
                    pool.wait_ge(s_setup, 3)
                for t in range(ST):
                    ins = pool.tensor_tensor(xr[:, t, :], xr[:, t, :], bo[:], ALU.add)
                ins.then_inc(p_xr, 1)

            def scatter(p):
                for t in range(ST):
                    pool.wait_ge(t_pos, p + 1)
                    if t:
                        pool.wait_ge(p_seen, ST * p + t)
                    pool.tensor_tensor(seen[:], seen[:], chosen[:, t, :], ALU.add).then_inc(p_seen, 1)
                after(pool, v_slot, p + 1, alone=p_waits)
                if isinstance(p, int) and p == 0:
                    pool.wait_ge(s_zero, 16 * 8)
                for t in range(ST):
                    for k in range(TOPK):
                        pool.indirect_dma_start(
                            out=dram["rows"], out_offset=bass.IndirectOffsetOnAxis(ap=slots[:, t, k:k + 1], axis=0),
                            in_=xf[:, t, :], in_offset=None,
                            bounds_check=E0 * CAP0 - 1, oob_is_err=False).then_inc(s_scat, 16)

            def ffn(p, last=False):
                bias_residual(p)
                rsqrt(p, mv2, var_eps2, rstd2, p_rs2c, v_st, 4, p_rs2)
                if not last:
                    rsqrt(p + 2, mv, var_eps, rstd, p_rs1c, v_ln, 4, p_rs1)
                scatter(p)

            rsqrt(0, mv, var_eps, rstd, p_rs1c, v_ln, 4, p_rs1)
            rsqrt(1, mv, var_eps, rstd, p_rs1c, v_ln, 4, p_rs1)
            ffn(0)
            with pool.Fori(2, NB - 1) as b:
                ffn(b - 1)
            ffn(NB - 2, last=True)
            ffn(NB - 1, last=True)
            pool.wait_ge(s_scat, 16 * ST * TOPK * NB)

        @block.vector
        def _(dve):
            dve.wait_ge(s_const, 16 * N_CONST)
            dve.wait_ge(s_pc, 10)
            dve.memset(vx[:], 0.0).then_inc(s_setup, 1)
            dve.memset(biased[:], -HUGE).then_inc(s_setup, 1)
            dve.wait_ge(s_tanh, 1)
            dve.tensor_scalar(bo[:], bo[:], tanh_g[:, 0:1], None, ALU.mult).then_inc(s_setup, 1)
            dve.tensor_scalar(mask[:], mask[:], NEG, None, ALU.mult).then_inc(s_setup, 1)
            dve.tensor_scalar(head_row_i[:], row_id[:], DEPTH.bit_length() - 1, None, ALU.logical_shift_right).then_inc(s_setup, 1)
            dve.wait_ge(s_setup, 5)
            dve.memset(vx[:, :, :].rearrange("p t (h e) -> p (t h) e", e=PAD)[:, :, DEPTH], 1.0).then_inc(s_setup, 1)
            dve.tensor_copy(head_row[:], head_row_i[:]).then_inc(s_setup, 1)
            dve.wait_ge(s_setup, 7)
            dve.tensor_scalar(head_scale[:], head_id[:], head_row[:, 0:1], DEPTH ** -0.5, ALU.is_equal, ALU.mult).then_inc(s_setup, 1)
            dve.wait_ge(s_setup, 8)

            def layernorm1(b):
                c = Chain(dve, v_ln, 4, b, alone=v_waits)
                dve.wait_ge(s_x, (b + 1) * 16)
                for t in range(ST):
                    c.done(dve.bn_stats(stats[:, t, :], x_in[:, t, :]))
                c.wait()
                for t in range(ST):
                    c.done(dve.bn_aggr(mv[:, t, :], stats[:, t, :]))
                c.wait()
                c.end()

            def layernorm1_apply(b):
                dve.wait_ge(p_rs1, b + 1)
                after(dve, t_xln, b)
                for t in range(ST):
                    ins = dve.tensor_scalar(xln[:, t, :], x_in[:, t, :], mv[:, t, 0:1], rstd[:, t:t + 1],
                                            ALU.subtract, ALU.mult)
                ins.then_inc(v_xln, 1)

            def head_q(b, i):
                if i == 0:
                    dve.wait_ge(a_q, b + 1)
                after(dve, t_s, HEADS * b + i - 3)
                dve.tensor_scalar(qm[:, i % 4, :], q[:, i // HPC, :], head_scale[:, i % HPC:i % HPC + 1], None,
                                  ALU.mult).then_inc(v_q, 1)

            def v_evac(b):
                dve.wait_ge(t_v, b + 1)
                for t in range(ST):
                    ins = dve.tensor_tensor(
                        vx[:, t, :].rearrange("p (h e) -> p h e", e=PAD)[:, :, 0:DEPTH],
                        ps_m[1][:, t * D:(t + 1) * D].rearrange("p (h e) -> p h e", e=DEPTH),
                        bv[:].rearrange("p (h e) -> p h e", e=DEPTH), ALU.add)
                ins.then_inc(v_v, 1)

            def mask_and_max(b, i):
                after(dve, t_s, HEADS * b + i + 1, alone=v_waits)
                after(dve, a_e, HEADS * b + i - 3, alone=v_waits)
                for t in range(ST):
                    ins = dve.tensor_tensor_reduce(
                        out=neg_s[:, i % 4, t, :], in0=ps_s[i % 2][:, t * S:(t + 1) * S], in1=mask[:, t, :],
                        scale=-1.0, scalar=HUGE, op0=ALU.add, op1=ALU.min, accum_out=neg_max[:, i % 4, t:t + 1])
                ins.then_inc(v_m, 1)

            def probsT_evac(b, i):
                dve.wait_ge(t_t, HEADS * b + i + 1)
                after(dve, t_pv, GROUPS * b + i // PACK - 1)
                dve.tensor_copy(probsT[:, i % (2 * PACK), :, :], ps_t[1][:, :]).then_inc(te[1], 1)

            def normalise(b, g):
                dve.wait_ge(t_o, GROUPS * b + g + 1)
                if g == 0:
                    after(dve, t_ot, b)
                o = ps_o[g % 2][:, S:2 * S].rearrange("p (t h e) -> p t h e", t=ST, e=PAD)
                dve.reciprocal(inv_sum[:, g % 2, :, :], o[:, :, :, DEPTH]).then_inc(v_inv, 1)
                dve.wait_ge(v_inv, GROUPS * b + g + 1)
                dve.tensor_tensor(attn[:, :, g * PACK * DEPTH:(g + 1) * PACK * DEPTH].rearrange("p t (h e) -> p t h e", e=DEPTH),
                                  o[:, :, :, 0:DEPTH],
                                  inv_sum[:, g % 2, :, :].unsqueeze(3).broadcast_to([P, ST, PACK, DEPTH]),
                                  ALU.mult).then_inc(v_on, 1)

            def add_attention(p):
                dve.wait_ge(t_wo, p + 1)
                dve.wait_ge(p_xr, p + 1)
                dve.scalar_tensor_tensor(out=xr[:], in0=ps_m[1][:, :], scalar=tanh_g[:, 0:1], in1=xr[:],
                                         op0=ALU.mult, op1=ALU.add).then_inc(v_x1, 1)
                c = Chain(dve, v_st, 4, p, alone=v_waits)
                dve.wait_ge(v_x1, p + 1)
                for t in range(ST):
                    c.done(dve.bn_stats(stats2[:, t, :], xr[:, t, :]))
                c.wait()
                for t in range(ST):
                    c.done(dve.bn_aggr(mv2[:, t, :], stats2[:, t, :]))
                c.wait()
                c.end()

            def layernorm2(p):
                dve.wait_ge(p_rs2, p + 1)
                after(dve, s_scat, 16 * ST * TOPK * p)
                for t in range(ST):
                    ins = dve.tensor_scalar(xf[:, t, :], xr[:, t, :], mv2[:, t, 0:1], rstd2[:, t:t + 1],
                                            ALU.subtract, ALU.mult)
                ins.then_inc(v_xf, 1)

            def router_max(p):
                dve.wait_ge(t_r, p + 1)
                dve.tensor_reduce(r_negmax[:], ps_m[1][:, 0:ST * E0].rearrange("p (t e) -> p t e", e=E0),
                                  AX, ALU.max, negate=True).then_inc(v_rm, 1)

            def choose(p):
                c = Chain(dve, v_rc, RC, p, alone=v_waits)
                dve.wait_ge(a_r, p + 1)
                c.done(dve.reciprocal(r_inv[:], r_sum[:]))
                c.wait()
                c.done(dve.tensor_tensor(scores[:], r_exp[:], r_inv[:].unsqueeze(2).broadcast_to([P, ST, E0]), ALU.mult))
                c.wait()
                c.done(dve.tensor_tensor(biased[:, :, 0:E0], scores[:], gate_b[:].unsqueeze(1).broadcast_to([P, ST, E0]), ALU.add))
                c.wait()
                for t in range(ST):
                    c.done(dve.max(top8[:, t, :], biased[:, t, :]))
                c.wait()
                c.done(dve.memset(top8[:, :, TOPK:8], -HUGE))
                c.wait()
                for t in range(ST):
                    c.done(dve.match_replace(replaced[:, t, :], top8[:, t, :], biased[:, t, :], HUGE))
                c.wait()
                after(dve, p_seen, ST * p)
                dve.tensor_scalar(chosen[:], replaced[:, :, 0:E0], 0.9 * HUGE, None, ALU.is_ge).then_inc(v_ch, 1)
                c.end()

            def hidden_evac(p, ic):
                n = SI_CHUNKS[ic][1]
                ps = ps_m[ic % 2]
                c = Chain(dve, v_hc, 1, 3 * p + ic)
                dve.wait_ge(a_th, 3 * p + ic + 1)
                c.done(dve.scalar_tensor_tensor(out=silu2[0:n, ic % 2, :], in0=th[0:n, ic % 2, :], scalar=1.0,
                                                in1=ps[0:n, 0:S], op0=ALU.add, op1=ALU.mult))
                c.wait()
                dve.scalar_tensor_tensor(out=hidden[0:n, ic, :], in0=silu2[0:n, ic % 2, :], scalar=0.5,
                                         in1=ps[0:n, S:2 * S], op0=ALU.mult, op1=ALU.mult).then_inc(v_h, 1)

            def add_shared(p):
                dve.wait_ge(t_z, p + 1)
                dve.scalar_tensor_tensor(out=xr[:], in0=ps_m[1][:, :], scalar=tanh_g[:, 2:3], in1=xr[:],
                                         op0=ALU.mult, op1=ALU.add).then_inc(v_z, 1)

            slot_chain = []

            def number_slots(p):
                dve.wait_ge(t_pos, p + 1)
                dve.wait_ge(v_ch, p + 1)
                pos = ps_m[0][:, 0:ST * E0].rearrange("p (t e) -> p t e", e=E0)
                c = Chain(dve, v_pos, PC + ST * TOPK, p, alone=v_waits)
                slot_chain[:] = [c]
                c.done(dve.scalar_tensor_tensor(out=fits[:], in0=pos, scalar=float(CAP0), in1=chosen[:],
                                                op0=ALU.is_le, op1=ALU.mult))
                c.done(dve.tensor_tensor(numbered[:], pos, expert_base[:].unsqueeze(1).broadcast_to([P, ST, E0]), ALU.add))
                c.wait()
                c.done(dve.tensor_tensor(slot_of[:], fits[:], numbered[:], ALU.mult))
                c.wait()
                c.done(dve.scalar_tensor_tensor(out=weight_of[:], in0=slot_of[:], scalar=0.5, in1=scores[:],
                                                op0=ALU.is_ge, op1=ALU.mult))
                for t in range(ST):
                    c.done(dve.max(slot8[:, t, :], slot_of[:, t, :]))
                c.wait()

            def pick_weights(t):
                for k in range(TOPK):
                    slot_chain[0].done(dve.scalar_tensor_tensor(
                        out=picked[:, t * TOPK + k, :], in0=slot_of[:, t, :], scalar=slot8[:, t, k:k + 1],
                        in1=weight_of[:, t, :], op0=ALU.is_equal, op1=ALU.mult, accum_out=w8[:, t, k:k + 1]))

            def finish_slots(p):
                c = slot_chain[0]
                c.done(dve.tensor_scalar(no_slot[:], slot8[:], 0.5, BIG_SLOT, ALU.is_lt, ALU.mult))
                c.wait()
                after(dve, s_scat, 16 * ST * TOPK * p)
                c.done(dve.scalar_tensor_tensor(out=slots[:], in0=slot8[:], scalar=-1.0, in1=no_slot[:],
                                                op0=ALU.add, op1=ALU.add))
                c.wait()
                c.end()
                dve.tensor_copy(slots_all[:, bass.ds(p * ST, ST), :], slots[:])
                dve.tensor_copy(w_all[:, bass.ds(p * ST, ST), 0:TOPK], w8[:, :, 0:TOPK]).then_inc(v_slot, 1)

            def ffn_at(p, i):
                if p is None:
                    return
                if i == 2:
                    add_attention(p)
                if i == 3:
                    layernorm2(p)
                if i == 6:
                    router_max(p)
                if i == 7:
                    hidden_evac(p, 0)
                if i == 8:
                    choose(p)
                    hidden_evac(p, 1)
                if i == 9:
                    hidden_evac(p, 2)
                if i == 11:
                    add_shared(p)
                if i == 12:
                    number_slots(p)
                    pick_weights(0)
                if i == 13:
                    pick_weights(1)
                    finish_slots(p)

            def batch(b, p, last):
                head_q(b, 0)
                head_q(b, 1)
                for i in range(STEPS):
                    if i + 2 < HEADS:
                        head_q(b, i + 2)
                    if i < HEADS:
                        mask_and_max(b, i)
                    if 2 <= i < HEADS + 2 and i % 2 == 1:
                        probsT_evac(b, i - 2)
                    if i >= 7 and i % PACK == 3:
                        normalise(b, (i - 7) // PACK)
                    ffn_at(p, i)
                    if not last:
                        if i == 9:
                            layernorm1(b + 1)
                        if i == 13:
                            layernorm1_apply(b + 1)
                        if i == STEPS - 1:
                            v_evac(b + 1)

            layernorm1(0)
            layernorm1_apply(0)
            v_evac(0)
            batch(0, None, False)
            batch(1, 0, False)
            with dve.Fori(2, NB - 1) as b:
                batch(b, b - 1, False)
            batch(NB - 1, NB - 2, True)
            for i in range(HEADS):
                ffn_at(NB - 1, i)

        @block.scalar
        def _(act):
            act.wait_ge(s_const, 16 * N_CONST)
            act.activation(tanh_g[:], keep["gates"][:], ACT.Tanh).then_inc(s_tanh, 1)
            act.wait_ge(s_setup, 8)

            def project_evac(b, part):
                if part == 0:
                    act.wait_ge(t_xln, b + 1)
                    act.activation(xlnT[:], ps_m[0][:, :], ACT.Copy).then_inc(a_xln, 1)
                    return
                if part == 1:
                    act.wait_ge(t_q, b + 1)
                    after(act, v_q, HEADS * b)
                dst, bank, bias, ready = (q, ps_m[1], bq, a_q) if part == 1 else (kT, ps_m[0], bk, a_k)
                if part == 2:
                    act.wait_ge(t_k, b + 1)
                for c in range(DC):
                    ins = act.activation(dst[:, c, :], bank[:, c * S:(c + 1) * S], ACT.Identity,
                                         bias=bias[:, c:c + 1], scale=1.0)
                ins.then_inc(ready, 1)

            def exponentials(b, i):
                act.wait_ge(v_m, HEADS * b + i + 1)
                after(act, t_t, HEADS * b + i - 3)
                for t in range(ST):
                    ins = act.activation(probs[:, i % 4, t, :], neg_s[:, i % 4, t, :], ACT.Exp,
                                         bias=neg_max[:, i % 4, t:t + 1], scale=-1.0)
                ins.then_inc(a_e, 1)

            def probsT_evac(b, i):
                act.wait_ge(t_t, HEADS * b + i + 1)
                after(act, t_pv, GROUPS * b + i // PACK - 1)
                act.activation(probsT[:, i % (2 * PACK), :, :], ps_t[0][:, :], ACT.Copy).then_inc(te[0], 1)

            def oT_evac(b, g):
                act.wait_ge(t_pv, GROUPS * b + g + 1)
                after(act, t_o, GROUPS * b + g - 1)
                act.activation(oT[:, g % 2, :], ps_o[g % 2][:, 0:S], ACT.Copy).then_inc(a_o, 1)

            def ffn_at(p, i):
                if p is None:
                    return
                if i == 0:
                    act.wait_ge(t_ot, p + 1)
                    act.activation(attnT[:], ps_m[0][:, :], ACT.Copy).then_inc(a_ot, 1)
                if i == 5:
                    act.wait_ge(t_xf, p + 1)
                    act.activation(xfT[:], ps_m[0][:, :], ACT.Copy).then_inc(a_xf, 1)
                if i == 6:
                    act.wait_ge(v_rm, p + 1)
                    for t in range(ST):
                        ins = act.activation(r_exp[:, t, :], ps_m[1][:, t * E0:(t + 1) * E0], ACT.Exp,
                                             bias=r_negmax[:, t:t + 1], accum_out=r_sum[:, t:t + 1])
                    ins.then_inc(a_r, 1)
                if i in (7, 8, 9):
                    ic = i - 7
                    n = SI_CHUNKS[ic][1]
                    act.wait_ge(t_h, 3 * p + ic + 1)
                    act.activation(th[0:n, ic % 2, :], ps_m[ic % 2][0:n, 0:S], ACT.Tanh, scale=0.5).then_inc(a_th, 1)

            def batch(b, p, last):
                for i in range(STEPS):
                    if 1 <= i < HEADS + 1:
                        exponentials(b, i - 1)
                    if 2 <= i < HEADS + 2 and i % 2 == 0:
                        probsT_evac(b, i - 2)
                    if i >= 6 and i % PACK == 2:
                        oT_evac(b, (i - 6) // PACK)
                    ffn_at(p, i)
                    if not last and 0 <= i - HEADS < 3:
                        project_evac(b + 1, i - HEADS)

            for part in range(3):
                project_evac(0, part)
            batch(0, None, False)
            batch(1, 0, False)
            with act.Fori(2, NB - 1) as b:
                batch(b, b - 1, False)
            batch(NB - 1, NB - 2, True)
            for i in range(HEADS):
                ffn_at(NB - 1, i)

        @block.tensor
        def _(pe):
            pe.wait_ge(s_const, 16 * N_CONST)
            pe.wait_ge(s_pc, 10)

            def transposed(dst, src):
                for c in range(DC):
                    for t in range(ST):
                        ins = pe.transpose(dst[:, c * S + t * P:c * S + (t + 1) * P], src[:, t, c * P:(c + 1) * P], ident[:])
                return ins

            def project(b, part):
                if part == 0:
                    pe.wait_ge(v_xln, b + 1)
                    transposed(ps_m[0], xln).then_inc(t_xln, 1)
                if part == 1:
                    pe.wait_ge(a_xln, b + 1)
                    for c in range(DC):
                        for k in range(DC):
                            ins = pe.matmul(ps_m[1][:, c * S:(c + 1) * S], wq[:, k, c * P:(c + 1) * P], xlnT[:, k, :],
                                            start=(k == 0), stop=(k == DC - 1))
                    ins.then_inc(t_q, 1)
                if part == 2:
                    pe.wait_ge(s_ctx, (b + 1) * 16)
                    for c in range(DC):
                        for k in range(DC):
                            ins = pe.matmul(ps_m[0][:, c * S:(c + 1) * S], wk[:, k, c * P:(c + 1) * P], ctxT[:, k, :],
                                            start=(k == 0), stop=(k == DC - 1))
                    ins.then_inc(t_k, 1)
                if part == 3:
                    pe.wait_ge(a_q, b + 1)
                    for t in range(ST):
                        for k in range(DC):
                            ins = pe.matmul(ps_m[1][:, t * D:(t + 1) * D], ctxT[:, k, t * P:(t + 1) * P], wv[:, k, :],
                                            start=(k == 0), stop=(k == DC - 1))
                    ins.then_inc(t_v, 1)

            def head_scores(b, i):
                pe.wait_ge(v_q, HEADS * b + i + 1)
                after(pe, v_m, HEADS * b + i - 1)
                for t in range(ST):
                    ins = pe.matmul(ps_s[i % 2][:, t * S:(t + 1) * S], qm[:, i % 4, t * P:(t + 1) * P],
                                    kT[:, i // HPC, :], start=True, stop=True)
                ins.then_inc(t_s, 1)

            def head_transpose(b, i):
                pe.wait_ge(a_e, HEADS * b + i + 1)
                after(pe, te[i % 2], HEADS // 2 * b + i // 2)
                for k in range(ST):
                    for t in range(ST):
                        ins = pe.transpose(ps_t[i % 2][:, k * S + t * P:k * S + (t + 1) * P],
                                           probs[:, i % 4, t, k * P:(k + 1) * P], ident[:])
                ins.then_inc(t_t, 1)

            def group_values(b, g):
                for parity in range(2):
                    pe.wait_ge(te[parity], HEADS // 2 * b + PACK // 2 * (g + 1))
                if g == 0:
                    pe.wait_ge(v_v, b + 1)
                after(pe, v_on, GROUPS * b + g - 1)
                for k in range(ST):
                    for j in range(PACK):
                        h = g * PACK + j
                        ins = pe.matmul(ps_o[g % 2][j * PAD:(j + 1) * PAD, 0:S], vx[:, k, h * PAD:(h + 1) * PAD],
                                        probsT[:, h % (2 * PACK), k, :], start=(k == 0), stop=(k == ST - 1))
                ins.then_inc(t_pv, 1)

            def group_turn(b, g):
                pe.wait_ge(a_o, GROUPS * b + g + 1)
                for t in range(ST):
                    ins = pe.transpose(ps_o[g % 2][:, S + t * P:S + (t + 1) * P], oT[:, g % 2, t * P:(t + 1) * P], ident[:])
                ins.then_inc(t_o, 1)

            def ffn_at(p, i):
                if p is None:
                    return
                if i == 0:
                    pe.wait_ge(v_on, GROUPS * (p + 1))
                    transposed(ps_m[0], attn).then_inc(t_ot, 1)
                if i == 1:
                    pe.wait_ge(a_ot, p + 1)
                    for t in range(ST):
                        for k in range(DC):
                            ins = pe.matmul(ps_m[1][:, t * D:(t + 1) * D], attnT[:, k, t * P:(t + 1) * P], wo[:, k, :],
                                            start=(k == 0), stop=(k == DC - 1))
                    ins.then_inc(t_wo, 1)
                if i == 5:
                    pe.wait_ge(v_xf, p + 1)
                    transposed(ps_m[0], xf).then_inc(t_xf, 1)
                if i == 6:
                    pe.wait_ge(a_xf, p + 1)
                    for t in range(ST):
                        for k in range(DC):
                            ins = pe.matmul(ps_m[1][:, t * E0:(t + 1) * E0], xfT[:, k, t * P:(t + 1) * P], gate_w[:, k, :],
                                            start=(k == 0), stop=(k == DC - 1))
                    ins.then_inc(t_r, 1)
                if i in (7, 8, 9):
                    ic = i - 7
                    o, n = SI_CHUNKS[ic]
                    if ic == 1:
                        pe.wait_ge(a_r, p + 1)
                    if ic == 2:
                        pe.wait_ge(v_h, 3 * p + 1)
                    for j, w in enumerate((ws1, ws3)):
                        for k in range(DC):
                            ins = pe.matmul(ps_m[ic % 2][0:n, j * S:(j + 1) * S], w[:, k, o:o + n], xfT[:, k, :],
                                            start=(k == 0), stop=(k == DC - 1))
                    ins.then_inc(t_h, 1)
                if i == 11:
                    pe.wait_ge(v_h, 3 * p + 3)
                    for t in range(ST):
                        for ic, (o, n) in enumerate(SI_CHUNKS):
                            ins = pe.matmul(ps_m[1][:, t * D:(t + 1) * D], hidden[0:n, ic, t * P:(t + 1) * P],
                                            ws2[0:n, ic, :], start=(ic == 0), stop=(ic == 2))
                    ins.then_inc(t_z, 1)
                if i == 12:
                    pe.wait_ge(v_ch, p + 1)
                    after(pe, p_seen, ST * p)
                    for t in range(ST):
                        o = ps_m[0][:, t * E0:(t + 1) * E0]
                        pe.matmul(o, ones[:], seen[:], start=True, stop=False)
                        if t:
                            pe.matmul(o, ones[:], chosen[:, 0, :], start=False, stop=False)
                        ins = pe.matmul(o, upper[:], chosen[:, t, :], start=False, stop=True)
                    ins.then_inc(t_pos, 1)

            def batch(b, p, last):
                pe.wait_ge(a_k, b + 1)
                pe.wait_ge(v_v, b + 1)
                for i in range(STEPS):
                    if i < HEADS:
                        head_scores(b, i)
                    if 2 <= i < HEADS + 2:
                        head_transpose(b, i - 2)
                    if i >= 6 and i % PACK == 2:
                        group_values(b, (i - 6) // PACK)
                    if i >= 7 and i % PACK == 3:
                        group_turn(b, (i - 7) // PACK)
                    ffn_at(p, i)
                    if not last and i >= HEADS:
                        if i == HEADS and p is not None:
                            pe.wait_ge(v_slot, p + 1)
                        project(b + 1, i - HEADS)

            for part in range(4):
                project(0, part)
            batch(0, None, False)
            batch(1, 0, False)
            with pe.Fori(2, NB - 1) as b:
                batch(b, b - 1, False)
            batch(NB - 1, NB - 2, True)
            for i in range(HEADS):
                ffn_at(NB - 1, i)


def experts(nc, sb, psum, sem, io, dram, keep, NE):
    RING = 4
    w1, w3 = sb("w1", [P, RING, DC, I0]), sb("w3", [P, RING, DC, I0])
    w2 = sb("w2", [P, RING, 2, D])
    rows = sb("rows", [P, RING, D])
    rowsT = sb("rowsT", [P, 2, DC, P])
    th = sb("th", [P, 2, 2, P])
    silu2 = sb("silu2", [P, 2, 2, P])
    hidden = sb("hidden", [P, 2, 2, P])
    y = sb("y", [P, 2, D])
    ident = keep["ident"]
    ps_t = [psum(f"ps_rows{i}") for i in range(2)]
    ps_h = [psum(f"ps_hid{i}") for i in range(2)]
    ps_y = [psum(f"ps_y{i}") for i in range(2)]

    s_w = [sem(f"b_expert{r}_loaded") for r in range(RING)]
    s_y = [sem(f"b_y{r}_stored") for r in range(2)]
    t_rows, a_rows = sem("b_rowsT_in_psum"), sem("b_rowsT_ready")
    t_h, a_th = sem("b_hidden_in_psum"), sem("b_hidden_tanh")
    v_s, v_h = sem("b_silu_ready"), sem("b_hidden_ready")
    t_y, a_y = sem("b_y_in_psum"), sem("b_y_ready")
    QUADS = (NE - RING) // RING

    def walk(eng, step):
        for e in range(RING + 1):
            step(e, e % RING, e // RING + 1)
        with eng.Fori(1, QUADS) as quad:
            for u in range(RING):
                step(quad * RING + (1 + u), (1 + u) % RING, quad + (2 if u == RING - 1 else 1))
        for e in range(QUADS * RING + 1, NE):
            step(e, e % RING, e // RING + 1)

    with nc.Block() as block:

        @block.sync
        def _(sp):
            def load(e, r):
                if not (isinstance(e, int) and e < RING):
                    sp.wait_ge(t_y, e - (RING - 1))
                for dst, src in ((w1[:, r], io["w1"][e]), (w3[:, r], io["w3"][e])):
                    sp.dma_start(dst, src.rearrange("(c p) n -> p c n", p=P)).then_inc(s_w[r], 16)
                sp.dma_start(w2[:, r, 0, :], io["w2"][e, 0:P]).then_inc(s_w[r], 16)
                sp.dma_start(w2[0:I0 - P, r, 1, :], io["w2"][e, P:I0]).then_inc(s_w[r], 16)
                sp.dma_start(rows[:, r, :], dram["rows"][bass.ds(e * CAP0, CAP0), :] if not isinstance(e, int)
                             else dram["rows"][e * CAP0:(e + 1) * CAP0, :]).then_inc(s_w[r], 16)

            for e in range(RING):
                load(e, e)
            for name, src in (("c_wk", "w_k"), ("c_wv", "w_v"), ("c_wq", "w_q"), ("c_wo", "w_o"), ("router_w", "router_w")):
                sp.dma_start(keep[name][:], io[src].rearrange("(c p) n -> p c n", p=P)).then_inc(keep["s_c_weights"], 16)
            with sp.Fori(1, NE // RING) as turn:
                for r in range(RING):
                    load(turn * RING + r, r)

        @block.tensor
        def _(pe):
            def turn_rows(e, r, n):
                pe.wait_ge(s_w[r], n * 16 * 5)
                after(pe, a_rows, e - 1)
                for c in range(DC):
                    ins = pe.transpose(ps_t[r % 2][:, c * P:(c + 1) * P], rows[:, r, c * P:(c + 1) * P], ident[:])
                ins.then_inc(t_rows, 1)

            def up(e, r):
                pe.wait_ge(a_rows, e + 1)
                after(pe, v_h, e - 1)
                for j, w in enumerate((w1, w3)):
                    for ic, (o, m) in enumerate(I0_CHUNKS):
                        for k in range(DC):
                            col = (2 * j + ic) * P
                            ins = pe.matmul(ps_h[r % 2][0:m, col:col + P], w[:, r, k, o:o + m], rowsT[:, r % 2, k, :],
                                            start=(k == 0), stop=(k == DC - 1))
                ins.then_inc(t_h, 1)

            def down(e, r):
                pe.wait_ge(v_h, e + 1)
                after(pe, a_y, e - 1)
                for ic, (o, m) in enumerate(I0_CHUNKS):
                    ins = pe.matmul(ps_y[r % 2][:, 0:D], hidden[0:m, r % 2, ic, :], w2[0:m, r, ic, :],
                                    start=(ic == 0), stop=(ic == 1))
                ins.then_inc(t_y, 1)

            turn_rows(0, 0, 1)
            up(0, 0)

            def step(e, r, n):
                if isinstance(e, int) and e == 0:
                    return
                turn_rows(e, r, n)
                down(e - 1, (r - 1) % RING)
                up(e, r)
            walk(pe, step)
            down(NE - 1, (NE - 1) % RING)

        @block.scalar
        def _(act):
            def step(e, r, n):
                act.wait_ge(t_rows, e + 1)
                after(act, t_h, e - 1)
                act.activation(rowsT[:, r % 2, :, :], ps_t[r % 2][:, 0:DC * P], ACT.Copy).then_inc(a_rows, 1)
                act.wait_ge(t_h, e + 1)
                after(act, v_h, e - 1)
                act.activation(th[:, r % 2, 0, :], ps_h[r % 2][:, 0:P], ACT.Tanh, scale=0.5)
                m = I0 - P
                act.activation(th[0:m, r % 2, 1, :], ps_h[r % 2][0:m, P:2 * P], ACT.Tanh, scale=0.5).then_inc(a_th, 1)
            walk(act, step)

        @block.vector
        def _(dve):
            def store_y(e, r, n2):
                dve.wait_ge(t_y, e + 1)
                after(dve, s_y[r % 2], n2 * 16)
                dve.tensor_copy(y[:, r % 2, :], ps_y[r % 2][:, 0:D]).then_inc(a_y, 1)

            def step(e, r, n):
                dve.wait_ge(a_th, e + 1)
                after(dve, t_y, e - 1)
                for ic, (o, m) in enumerate(I0_CHUNKS):
                    ins = dve.scalar_tensor_tensor(out=silu2[0:m, r % 2, ic, :], in0=th[0:m, r % 2, ic, :], scalar=1.0,
                                                   in1=ps_h[r % 2][0:m, ic * P:(ic + 1) * P], op0=ALU.add, op1=ALU.mult)
                ins.then_inc(v_s, 1)
                dve.wait_ge(v_s, e + 1)
                for ic, (o, m) in enumerate(I0_CHUNKS):
                    ins = dve.scalar_tensor_tensor(out=hidden[0:m, r % 2, ic, :], in0=silu2[0:m, r % 2, ic, :], scalar=0.5,
                                                   in1=ps_h[r % 2][0:m, (2 + ic) * P:(3 + ic) * P], op0=ALU.mult, op1=ALU.mult)
                ins.then_inc(v_h, 1)

            def step_and_store(e, r, n):
                step(e, r, n)
                if isinstance(e, int):
                    if e > 0:
                        store_y(e - 1, (e - 1) % RING, (e - 1) // 2)
                else:
                    quad = n - (2 if r == 0 else 1)
                    store_y(e - 1, (r - 1) % RING, quad * 2 + ((r - 1) % RING) // 2)
            walk(dve, step_and_store)
            store_y(NE - 1, (NE - 1) % RING, (NE - 1) // 2)

        @block.gpsimd
        def _(pool):
            def store(e, r):
                pool.wait_ge(a_y, e + 1)
                dst = dram["y"][e * CAP0:(e + 1) * CAP0, :] if isinstance(e, int) else dram["y"][bass.ds(e * CAP0, CAP0), :]
                pool.dma_start(dst, y[:, r % 2, :]).then_inc(s_y[r % 2], 16)
            with pool.Fori(0, NE // RING) as quad:
                for r in range(RING):
                    store(quad * RING + r, r)
            for r in range(2):
                pool.wait_ge(s_y[r], 16 * NE // 2)


def attention_and_top(nc, sb, psum, sem, io, dram, keep, NB):
    wq, wk, wv, wo, router_w = (keep[n] for n in ("c_wq", "c_wk", "c_wv", "c_wo", "router_w"))
    minus_half = sb("minus_half", [P, 2])
    x1 = sb("x1", [P, ST, D])
    gathered = sb("gathered", [P, ST * TOPK, D])
    slots = sb("slots", [P, ST, 8], U32)
    w8 = sb("w8", [P, ST, 8])
    x2 = sb("x2", [P, ST, D])
    x2_kept = sb("x2_kept", [P, ST, D])
    stats, mv = sb("stats", [P, ST, 6]), sb("mv", [P, ST, 2])
    var_eps, rstd = sb("var_eps", [P, ST]), sb("rstd", [P, ST])
    xln, xlnT = sb("xln", [P, ST, D]), sb("xlnT", [P, DC, S])
    ctxT = sb("ctxT", [P, DC, S])
    qT, kT = sb("qT", [P, HD // P, S]), sb("kT", [P, HD // P, S])
    v = sb("v", [P, ST, HD])
    RING = 8
    neg_max = sb("neg_max", [P, 4, ST])
    sums, inv = sb("sums", [P, RING, ST]), sb("inv", [P, RING, ST])
    probs = sb("probs", [P, RING, ST, S])
    vs = sb("vs", [P, RING, ST, DK])
    attnT = sb("attnT", [P, HD // P, S])
    x3 = sb("x3", [P, ST, D])
    stats2, mv2 = sb("stats2", [P, ST, 6]), sb("mv2", [P, ST, 2])
    var_eps2, rstd2 = sb("var_eps2", [P, ST]), sb("rstd2", [P, ST])
    xn, xnT = sb("xn", [P, ST, D]), sb("xnT", [P, DC, S])
    r_negmax, r_exp = sb("r_negmax", [P, ST]), sb("r_exp", [P, ST, E1])
    r_sum, r_inv = sb("r_sum", [P, ST]), sb("r_inv", [P, ST])
    ident, tanh_g, slots_all, w_all = keep["ident"], keep["tanh_g"], keep["slots_all"], keep["w_all"]
    gate_all = keep["gate_all"]

    ps_s = [psum(f"ps_c_s{i}") for i in range(4)]
    ps_o = [psum(f"ps_c_o{i}") for i in range(2)]
    ps_m = [psum(f"ps_c_m{i}") for i in range(2)]

    s_x, s_ctx = sem("c_x1_loaded"), sem("c_ctx_loaded")
    s_x3, s_xn = sem("c_x3_stored"), sem("c_x3n_stored")
    s_gat = sem("c_rows_gathered")
    p_const, v_const = sem("c_pool_consts"), sem("c_vector_consts")
    v_waits, p_waits = sem("c_vector_waits"), sem("c_pool_waits")
    v_sl, v_add, v_comb = sem("c_slots_copied"), sem("c_rows_chain"), sem("c_x2_ready")
    v_ln, p_rs, p_rsc, v_xln = sem("c_ln_chain"), sem("c_rstd"), sem("c_rstd_chain"), sem("c_xln_ready")
    t_fill = sem("c_fill_in_psum")
    ev = [sem("c_even_fill_ready"), sem("c_odd_fill_ready")]
    t_s, v_m, a_e = sem("c_scores_in_psum"), sem("c_max_ready"), sem("c_probs_ready")
    v_inv, v_vs = sem("c_inv_sums"), sem("c_v_scaled")
    t_pv = sem("c_pv_done")
    ot = [sem("c_attnT_even_ready"), sem("c_attnT_odd_ready")]
    p_x2 = sem("c_x2_kept")
    v_st, p_rs2, p_rs2c, v_xn = sem("c_ln2_chain"), sem("c_rstd2"), sem("c_rstd2_chain"), sem("c_xn_ready")
    v_rm, v_ri, v_gate = (sem(f"c_router_{n}") for n in ("max", "inv", "scores"))

    PAIRS = HEADS // 2
    STEPS = HEADS + 3
    FILLS = 16
    F_XNT, F_ROUTER = 0, 1
    F_K, F_V = 2, 6
    F_XLNT, F_WO, F_Q = 10, 11, 12

    def present(b, n):
        if n in (F_XNT, F_ROUTER):
            return b > 0
        return 0 <= b < NB if n == F_WO else b < NB - 1

    upto = Fills(FILLS, present).upto

    def empty(n, copy):
        bank = ps_m[n % 2]
        src = bank[:, :].rearrange("p (c s) -> p c s", c=2)
        if n < F_V:
            return copy(kT[:, 2 * (n - F_K):2 * (n - F_K) + 2, :], src, 1.0)
        if n < F_XLNT:
            return copy(v[:, (n - F_V) // 2, (n % 2) * 512:(n % 2 + 1) * 512], bank[:, :], 1.0)
        return copy(qT[:, 2 * (n - F_Q):2 * (n - F_Q) + 2, :], src, DK ** -0.5)

    with nc.Block() as block:

        @block.sync
        def _(sp):
            sp.dma_start(ctxT[:], tiles(io["ctxT"][0])).then_inc(s_ctx, 16)
            sp.dma_start(x1[:], tiles(dram["x1"][0])).then_inc(s_x, 16)
            for e in range(E1):
                sp.dma_start(keep["f1"][:, e], io["f1"][e].rearrange("(c p) n -> p c n", p=P)).then_inc(keep["s_f1"], 16)

            def loads(b):
                sp.wait_ge(v_comb, b + 1)
                sp.dma_start(x1[:], tiles(dram["x1"][b + 1])).then_inc(s_x, 16)
                sp.wait_ge(t_fill, upto(b - 1, F_V + 3))
                sp.dma_start(ctxT[:], tiles(io["ctxT"][b + 1])).then_inc(s_ctx, 16)

            def stores(p):
                sp.wait_ge(ev[1], upto(p, F_WO, 1))
                sp.dma_start(tiles(dram["x3"][p]), x3[:]).then_inc(s_x3, 16)
                sp.wait_ge(v_xn, p + 1)
                sp.dma_start(tiles(dram["x3n"][p]), xn[:]).then_inc(s_xn, 16)

            loads(0)
            loads(1)
            stores(0)
            with sp.Fori(2, NB - 1) as b:
                loads(b)
                stores(b - 1)
            stores(NB - 2)
            stores(NB - 1)
            sp.wait_ge(s_x3, 16 * NB)
            sp.wait_ge(s_xn, 16 * NB)
            sp.wait_ge(keep["s_f1"], 16 * E1)

        @block.gpsimd
        def _(pool):
            pool.memset(minus_half[:], -0.5).then_inc(p_const, 1)
            pool.memset(gathered[:], 0.0).then_inc(p_const, 1)
            pool.wait_ge(p_const, 2)

            def rsqrt(b, mv_, var_eps_, rstd_, chain, stats_done, ready):
                after(pool, stats_done, (b + 1) * 4, alone=p_waits)
                pool.tensor_scalar(var_eps_[:], mv_[:, :, 1], EPS, None, ALU.add).then_inc(chain, 1)
                pool.wait_ge(chain, b + 1)
                pool.tensor_tensor(rstd_[:], var_eps_[:], minus_half[:], ALU.pow).then_inc(ready, 1)

            def gather(b):
                after(pool, v_comb, b, alone=p_waits)
                after(pool, v_sl, b + 1, alone=p_waits)
                for t in range(ST):
                    for k in range(TOPK):
                        pool.indirect_dma_start(
                            out=gathered[:, t * TOPK + k, :], out_offset=None, in_=dram["y"],
                            in_offset=bass.IndirectOffsetOnAxis(ap=slots[:, t, k:k + 1], axis=0),
                            bounds_check=E0 * CAP0 - 1, oob_is_err=False).then_inc(s_gat, 16)

            def keep_x2(b):
                after(pool, v_comb, b + 1, alone=p_waits)
                if not (isinstance(b, int) and b == 0):
                    after(pool, ev[1], upto(b - 1, F_WO, 1), alone=p_waits)
                pool.tensor_copy(x2_kept[:], x2[:]).then_inc(p_x2, 1)

            def batch(b, p, last):
                keep_x2(b)
                if p is not None:
                    rsqrt(p, mv2, var_eps2, rstd2, p_rs2c, v_st, p_rs2)
                if not last:
                    gather(b + 1)
                    rsqrt(b + 1, mv, var_eps, rstd, p_rsc, v_ln, p_rs)

            gather(0)
            rsqrt(0, mv, var_eps, rstd, p_rsc, v_ln, p_rs)
            batch(0, None, False)
            batch(1, 0, False)
            with pool.Fori(2, NB - 1) as b:
                batch(b, b - 1, False)
            batch(NB - 1, NB - 2, True)
            rsqrt(NB - 1, mv2, var_eps2, rstd2, p_rs2c, v_st, p_rs2)

        @block.vector
        def _(dve):
            def take_slots(b):
                after(dve, s_gat, 16 * ST * TOPK * b)
                dve.tensor_copy(slots[:], slots_all[:, bass.ds(b * ST, ST), :] if not isinstance(b, int)
                                else slots_all[:, b * ST:(b + 1) * ST, :])
                dve.tensor_scalar(w8[:, :, 0:TOPK], w_all[:, bass.ds(b * ST, ST), 0:TOPK] if not isinstance(b, int)
                                  else w_all[:, b * ST:(b + 1) * ST, 0:TOPK], tanh_g[:, 2:3], None, ALU.mult).then_inc(v_sl, 1)

            def combine(b, k):
                if k == 0:
                    dve.wait_ge(s_x, 16 * (b + 1))
                    dve.wait_ge(s_gat, 16 * ST * TOPK * (b + 1))
                    dve.wait_ge(v_sl, b + 1)
                    after(dve, p_x2, b)
                else:
                    dve.wait_ge(v_add, ST * (TOPK - 1) * b + ST * k)
                for t in range(ST):
                    ins = dve.scalar_tensor_tensor(out=x2[:, t, :], in0=gathered[:, t * TOPK + k, :],
                                                   scalar=w8[:, t, k:k + 1], in1=(x2 if k else x1)[:, t, :],
                                                   op0=ALU.mult, op1=ALU.add)
                    if k < TOPK - 1:
                        ins.then_inc(v_add, 1)
                if k == TOPK - 1:
                    ins.then_inc(v_comb, 1)

            def statistics(b, src, stats_, mv_, chain_sem, ready, value):
                c = Chain(dve, chain_sem, 4, b, alone=v_waits)
                dve.wait_ge(ready, value)
                for t in range(ST):
                    c.done(dve.bn_stats(stats_[:, t, :], src[:, t, :]))
                c.wait()
                for t in range(ST):
                    c.done(dve.bn_aggr(mv_[:, t, :], stats_[:, t, :]))
                c.wait()
                c.end()

            def layernorm1(b):
                dve.wait_ge(p_rs, b + 1)
                after(dve, t_fill, upto(b - 2, F_XLNT) if not (isinstance(b, int) and b == 0) else 0)
                for t in range(ST):
                    ins = dve.tensor_scalar(xln[:, t, :], x2[:, t, :], mv[:, t, 0:1], rstd[:, t:t + 1],
                                            ALU.subtract, ALU.mult)
                ins.then_inc(v_xln, 1)

            def layernorm2(p):
                dve.wait_ge(p_rs2, p + 1)
                after(dve, s_xn, 16 * p)
                for t in range(ST):
                    ins = dve.tensor_scalar(xn[:, t, :], x3[:, t, :], mv2[:, t, 0:1], rstd2[:, t:t + 1],
                                            ALU.subtract, ALU.mult)
                ins.then_inc(v_xn, 1)

            def fill_evac(b, n):
                dve.wait_ge(t_fill, upto(b, n))
                empty(n, lambda dst, src, scale: dve.tensor_scalar(dst, src, scale, None, ALU.mult) if scale != 1.0
                      else dve.tensor_copy(dst, src)).then_inc(ev[1], 1)

            def head_max(b, i):
                dve.wait_ge(t_s, HEADS * b + i + 1)
                dve.tensor_reduce(neg_max[:, i % 4, :], ps_s[i % 4][:, :].rearrange("p (k s) -> p k s", k=ST),
                                  AX, ALU.max, negate=True).then_inc(v_m, 1)

            def scale_v(b, i):
                dve.wait_ge(a_e, HEADS * b + i + 1)
                dve.reciprocal(inv[:, i % RING, :], sums[:, i % RING, :]).then_inc(v_inv, 1)
                dve.wait_ge(v_inv, HEADS * b + i + 1)
                after(dve, t_pv, PAIRS * b + (i - RING) // 2 + 1)
                dve.tensor_tensor(vs[:, i % RING, :, :], v[:, :, i * DK:(i + 1) * DK],
                                  inv[:, i % RING, :].unsqueeze(2).broadcast_to([P, ST, DK]), ALU.mult).then_inc(v_vs, 1)

            def attnT_evac(b, c):
                dve.wait_ge(t_pv, PAIRS * b + c + 1)
                dve.tensor_copy(attnT[:, c, :], ps_o[1][:, 0:S]).then_inc(ot[1], 1)

            def add_attention(b):
                dve.wait_ge(t_fill, upto(b, F_WO))
                dve.wait_ge(p_x2, b + 1)
                after(dve, s_x3, 16 * b)
                dve.scalar_tensor_tensor(out=x3[:], in0=ps_m[1][:, :], scalar=tanh_g[:, 1:2], in1=x2_kept[:],
                                         op0=ALU.mult, op1=ALU.add).then_inc(ev[1], 1)
                statistics(b, x3, stats2, mv2, v_st, ev[1], upto(b, F_WO, 1))

            def tail_at(p, i):
                if p is None:
                    return
                if i == 1:
                    layernorm2(p)
                if i == 6:
                    dve.wait_ge(t_fill, upto(p + 1, F_ROUTER))
                    dve.tensor_reduce(r_negmax[:], ps_m[1][:, 0:ST * E1].rearrange("p (t e) -> p t e", e=E1),
                                      AX, ALU.max, negate=True).then_inc(v_rm, 1)
                if i == 8:
                    dve.wait_ge(ev[1], upto(p + 1, F_ROUTER, 1))
                    dve.reciprocal(r_inv[:], r_sum[:]).then_inc(v_ri, 1)
                    dve.wait_ge(v_ri, p + 1)
                    for t in range(ST):
                        dst = gate_all[:, t, p * E1:(p + 1) * E1] if isinstance(p, int) else gate_all[:, t, bass.ds(p * E1, E1)]
                        ins = dve.tensor_scalar(dst, r_exp[:, t, :], r_inv[:, t:t + 1], None, ALU.mult)
                    ins.then_inc(v_gate, 1)

            def batch(b, p, last):
                for i in range(STEPS):
                    if i < HEADS:
                        head_max(b, i)
                    if 1 <= i < HEADS + 1:
                        scale_v(b, i - 1)
                    if i >= 7 and i % 4 == 3:
                        attnT_evac(b, (i - 5) // 2)
                    tail_at(p, i)
                    if not last:
                        if i == 0:
                            take_slots(b + 1)
                        if i >= HEADS:
                            fill_evac(b, F_K + 1 + 2 * (i - HEADS))
                        if 12 <= i < 12 + TOPK:
                            combine(b + 1, i - 12)
                if not last:
                    statistics(b + 1, x2, stats, mv, v_ln, v_comb, b + 2)
                attnT_evac(b, PAIRS - 1)
                if not last:
                    layernorm1(b + 1)
                    fill_evac(b, F_V + 3)
                add_attention(b)
                if not last:
                    fill_evac(b, F_Q + 1)
                    fill_evac(b, F_Q + 3)

            dve.wait_ge(p_const, 2)
            take_slots(0)
            for n in range(F_K + 1, F_V + 4, 2):
                fill_evac(-1, n)
            for k in range(TOPK):
                combine(0, k)
            statistics(0, x2, stats, mv, v_ln, v_comb, 1)
            layernorm1(0)
            fill_evac(-1, F_Q + 1)
            fill_evac(-1, F_Q + 3)
            batch(0, None, False)
            batch(1, 0, False)
            with dve.Fori(2, NB - 1) as b:
                batch(b, b - 1, False)
            batch(NB - 1, NB - 2, True)
            for i in range(STEPS):
                tail_at(NB - 1, i)

        @block.scalar
        def _(act):
            def fill_evac(b, n):
                act.wait_ge(t_fill, upto(b, n))
                if n == F_XNT:
                    ins = act.activation(xnT[:], ps_m[0][:, :], ACT.Copy)
                elif n == F_XLNT:
                    ins = act.activation(xlnT[:], ps_m[0][:, :], ACT.Copy)
                else:
                    if n == F_V:
                        after(act, v_vs, HEADS * (b + 1))
                    ins = empty(n, lambda dst, src, scale: act.activation(dst, src, ACT.Copy, scale=scale))
                ins.then_inc(ev[0], 1)

            def exponentials(b, i):
                act.wait_ge(v_m, HEADS * b + i + 1)
                after(act, t_pv, PAIRS * b + (i - RING) // 2 + 1)
                for k in range(ST):
                    ins = act.activation(probs[:, i % RING, k, :], ps_s[i % 4][:, k * S:(k + 1) * S], ACT.Exp,
                                         bias=neg_max[:, i % 4, k:k + 1], accum_out=sums[:, i % RING, k:k + 1])
                ins.then_inc(a_e, 1)

            def tail_at(p, i):
                if p is None:
                    return
                if i == 4:
                    fill_evac(p + 1, F_XNT)
                if i == 6:
                    act.wait_ge(v_rm, p + 1)
                    after(act, v_gate, p)
                    for t in range(ST):
                        ins = act.activation(r_exp[:, t, :], ps_m[1][:, t * E1:(t + 1) * E1], ACT.Exp,
                                             bias=r_negmax[:, t:t + 1], accum_out=r_sum[:, t:t + 1])
                    ins.then_inc(ev[1], 1)

            def batch(b, p, last):
                for i in range(STEPS):
                    if i < HEADS:
                        exponentials(b, i)
                    if i >= 5 and i % 4 == 1:
                        c = (i - 5) // 2
                        act.wait_ge(t_pv, PAIRS * b + c + 1)
                        act.activation(attnT[:, c, :], ps_o[0][:, 0:S], ACT.Copy).then_inc(ot[0], 1)
                    tail_at(p, i)
                    if not last and i >= HEADS:
                        fill_evac(b, F_K + 2 * (i - HEADS))
                if not last:
                    for n in (F_V + 2, F_XLNT, F_Q, F_Q + 2):
                        fill_evac(b, n)

            for n in (*range(F_K, F_V + 4, 2), F_XLNT, F_Q, F_Q + 2):
                fill_evac(-1, n)
            batch(0, None, False)
            batch(1, 0, False)
            with act.Fori(2, NB - 1) as b:
                batch(b, b - 1, False)
            batch(NB - 1, NB - 2, True)
            for i in range(STEPS):
                tail_at(NB - 1, i)

        @block.tensor
        def _(pe):
            pe.wait_ge(keep["s_c_weights"], 16 * 5)

            def transposed(dst, src):
                for c in range(DC):
                    for t in range(ST):
                        ins = pe.transpose(dst[:, c * S + t * P:c * S + (t + 1) * P], src[:, t, c * P:(c + 1) * P], ident[:])
                return ins

            def fill(b, n):
                after(pe, ev[n % 2], upto(b, n, n % 2) - 1)
                bank = ps_m[n % 2]
                if n == F_XNT:
                    pe.wait_ge(v_xn, b)
                    ins = transposed(bank, xn)
                elif n == F_ROUTER:
                    pe.wait_ge(ev[0], upto(b, F_XNT, 0))
                    for t in range(ST):
                        for k in range(DC):
                            ins = pe.matmul(bank[:, t * E1:(t + 1) * E1], xnT[:, k, t * P:(t + 1) * P], router_w[:, k, :],
                                            start=(k == 0), stop=(k == DC - 1))
                elif n == F_XLNT:
                    pe.wait_ge(v_xln, b + 2)
                    ins = transposed(bank, xln)
                elif n == F_WO:
                    for j in range(2):
                        pe.wait_ge(ot[j], PAIRS // 2 * (b + 1))
                    for t in range(ST):
                        for c in range(HD // P):
                            ins = pe.matmul(bank[:, t * D:(t + 1) * D], attnT[:, c, t * P:(t + 1) * P], wo[:, c, :],
                                            start=(c == 0), stop=(c == HD // P - 1))
                elif F_V <= n < F_XLNT:
                    t, half = (n - F_V) // 2, n % 2
                    for k in range(DC):
                        ins = pe.matmul(bank[:, :], ctxT[:, k, t * P:(t + 1) * P], wv[:, k, half * 512:(half + 1) * 512],
                                        start=(k == 0), stop=(k == DC - 1))
                else:
                    w, x, first = (wq, xlnT, F_Q) if n >= F_Q else (wk, ctxT, F_K)
                    if n == F_Q:
                        pe.wait_ge(ev[0], upto(b, F_XLNT, 0))
                    if n == F_K:
                        pe.wait_ge(s_ctx, 16 * (b + 2))
                    for j in range(2):
                        c = 2 * (n - first) + j
                        for k in range(DC):
                            ins = pe.matmul(bank[:, j * S:(j + 1) * S], w[:, k, c * P:(c + 1) * P], x[:, k, :],
                                            start=(k == 0), stop=(k == DC - 1))
                ins.then_inc(t_fill, 1)

            def head_scores(b, i):
                c, r = i // 2, DK * (i % 2)
                if i % 4 == 0:
                    n = i // 4
                    for first in (F_K, F_Q):
                        pe.wait_ge(ev[n % 2], upto(b - 1, first + n, n % 2))
                after(pe, a_e, HEADS * b + i - 3)
                for k in range(ST):
                    ins = pe.matmul(ps_s[i % 4][:, k * S:(k + 1) * S], kT[r:r + DK, c, k * P:(k + 1) * P],
                                    qT[r:r + DK, c, :], start=True, stop=True)
                ins.then_inc(t_s, 1)

            def pair_values(b, c):
                pe.wait_ge(v_vs, HEADS * b + 2 * c + 2)
                after(pe, ot[c % 2], PAIRS // 2 * b + c // 2)
                for k in range(ST):
                    for j in range(2):
                        i = 2 * c + j
                        ins = pe.matmul(ps_o[c % 2][j * DK:(j + 1) * DK, 0:S], vs[:, i % RING, k, :], probs[:, i % RING, k, :],
                                        start=(k == 0), stop=(k == ST - 1))
                ins.then_inc(t_pv, 1)

            def batch(b, p, last):
                for i in range(STEPS):
                    if i < HEADS:
                        head_scores(b, i)
                    if p is not None and i == 4:
                        fill(b, F_XNT)
                    if p is not None and i == 6:
                        fill(b, F_ROUTER)
                    if not last and i >= HEADS:
                        fill(b, F_K + 2 * (i - HEADS))
                        fill(b, F_K + 2 * (i - HEADS) + 1)
                    if i >= 4 and i % 2 == 0:
                        pair_values(b, (i - 4) // 2)
                if not last:
                    for n in (F_V + 2, F_V + 3, F_XLNT):
                        fill(b, n)
                fill(b, F_WO)
                if not last:
                    for n in range(F_Q, F_Q + 4):
                        fill(b, n)

            for n in (*range(F_K, F_WO), *range(F_Q, F_Q + 4)):
                fill(-1, n)
            batch(0, None, False)
            batch(1, 0, False)
            with pe.Fori(2, NB - 1) as b:
                batch(b, b - 1, False)
            batch(NB - 1, NB - 2, True)
            fill(NB, F_XNT)
            fill(NB, F_ROUTER)


def choose_tokens(nc, sb, psum, sem, io, dram, keep, NB):
    rows_of = [(o, min(P, NB * E1 - o)) for o in range(0, NB * E1, P)]
    NT = len(rows_of)
    WIDE = S + 8
    work = sb("work", [P, NT, WIDE])
    top8 = sb("top8", [P, NT, 8])
    ones = sb("ones", [P, S])
    chosen, counted, place = (sb(n, [P, NT, S]) for n in ("chosen", "counted", "place"))
    gate_all, pos_all, ident = keep["gate_all"], keep["pos_all"], keep["ident"]
    ps = [psum(f"ps_e{i}") for i in range(2)]
    t_sc, v_ch, t_pos, v_pos = sem("e_scores_in_psum"), sem("e_chain"), sem("e_places_in_psum"), sem("e_places_ready")
    v_done = sem("e_places_turned")

    with nc.Block() as block:

        @block.tensor
        def _(pe):
            for i, (o, n) in enumerate(rows_of):
                for t in range(ST):
                    ins = pe.transpose(ps[0][0:n, i * S + t * P:i * S + (t + 1) * P], gate_all[:, t, o:o + n], ident[:])
            ins.then_inc(t_sc, 1)
            pe.wait_ge(v_pos, 1)
            for i, (o, n) in enumerate(rows_of):
                for t in range(ST):
                    ins = pe.transpose(ps[1][:, t * NB * E1 + o:t * NB * E1 + o + n], place[0:n, i, t * P:(t + 1) * P],
                                       ident[0:n, 0:n])
            ins.then_inc(t_pos, 1)

        @block.vector
        def _(dve):
            c = Chain(dve, v_ch, 0, 0)
            c.done(dve.memset(ones[:], 1.0))
            c.done(dve.memset(work[:, :, S:WIDE], -1.0))
            dve.wait_ge(t_sc, 1)
            for i, (o, n) in enumerate(rows_of):
                c.done(dve.tensor_copy(work[0:n, i, 0:S], ps[0][0:n, i * S:(i + 1) * S]))
            c.wait()
            for turn in range((CAP1 + 7) // 8):
                take = min(8, CAP1 - 8 * turn)
                for i, (o, n) in enumerate(rows_of):
                    c.done(dve.max(top8[0:n, i, :], work[0:n, i, :]))
                c.wait()
                if take < 8:
                    c.done(dve.memset(top8[:, :, take:8], -1.0))
                    c.wait()
                for i, (o, n) in enumerate(rows_of):
                    c.done(dve.match_replace(work[0:n, i, :], top8[0:n, i, :], work[0:n, i, :], -2.0))
                c.wait()
            for i, (o, n) in enumerate(rows_of):
                c.done(dve.tensor_scalar(chosen[0:n, i, :], work[0:n, i, 0:S], -1.5, None, ALU.is_lt))
            c.wait()
            for i, (o, n) in enumerate(rows_of):
                c.done(dve.tensor_tensor_scan(counted[0:n, i, :], ones[0:n, :], chosen[0:n, i, :], 0.0, ALU.mult, ALU.add))
            c.wait()
            for i, (o, n) in enumerate(rows_of):
                c.done(dve.tensor_tensor(place[0:n, i, :], counted[0:n, i, :], chosen[0:n, i, :], ALU.mult))
            c.wait()
            dve.tensor_copy(ones[:, 0:1], ones[:, 1:2]).then_inc(v_pos, 1)
            dve.wait_ge(t_pos, 1)
            dve.tensor_copy(pos_all[:, :, 0:NB * E1],
                            ps[1][:, 0:ST * NB * E1].rearrange("p (t e) -> p t e", t=ST)).then_inc(v_done, 1)


def expert_choice(nc, sb, psum, sem, io, out, dram, keep, NB):
    f1 = keep["f1"]
    NQ = NB // 2
    f2 = sb("f2", [P, E1, HC, D])
    b1, b2 = sb("b1", [P, E1, HC]), sb("b2", [P, E1, DC])
    slot_id = sb("slot_id", [P, CAP1])
    xn, x3 = sb("xn", [P, 2 * ST, D]), sb("x3", [P, 2 * ST, D])
    sel, gated = sb("sel", [P, 2 * ST, SLOTS]), sb("gated", [P, 2 * ST, SLOTS])
    tokT = sb("tokT", [P, DC, 2, SLOTS])
    gatedT = sb("gatedT", [GS, 2, GC, S])
    hid = sb("hid", [P, 2, HC, 2 * CAP1])
    yT = sb("yT", [P, DC, 2, SLOTS])
    y = sb("y", [GS, 2, GC, D])
    ident, tanh_g, gate_all, pos_all = keep["ident"], keep["tanh_g"], keep["gate_all"], keep["pos_all"]

    ps_h = [psum(f"ps_d_h{i}") for i in range(4)]
    ps_y = [psum(f"ps_d_y{i}") for i in range(2)]
    ps_m = [psum(f"ps_d_m{i}") for i in range(2)]

    s_f2 = [sem(f"d_f2_{e % 2}_loaded") for e in range(2)]
    s_const, s_xn, s_x3, s_out = sem("d_const_loaded"), sem("d_xn_loaded"), sem("d_x3_loaded"), sem("d_out_stored")
    p_const = sem("d_pool_const")
    p_waits = sem("d_pool_waits")
    v_sel, p_gated = sem("d_sel_ready"), sem("d_gated_ready")
    t_fill = sem("d_fill_in_psum")
    ev = [sem("d_even_fill_ready"), sem("d_odd_fill_ready")]
    t_h, a_h = sem("d_hidden_in_psum"), sem("d_hidden_ready")
    t_y, v_y = sem("d_yT_in_psum"), sem("d_yT_ready")

    HALF = SLOTS // 2
    N2 = 2 * CAP1
    UNITS = [(0, 3), (3, 3), (6, 2)]
    UPE = len(UNITS)

    FILLS = 20
    TOKENS = {1: (1, 0, 0), 2: (1, 0, 1), 4: (1, 1, 0), 6: (1, 1, 1),
              10: (0, 0, 0), 12: (0, 0, 1), 14: (0, 1, 0), 15: (0, 1, 1)}
    GATES = {7: (0, 0), 8: (0, 1), 9: (1, 0), 16: (1, 1), 17: (2, 0)}
    RESULTS = {11: (0, 0), 13: (0, 1), 18: (1, 0), 19: (1, 1), 0: (2, 0)}
    SUMS = {3: 0, 5: 1}
    OLD = (0, 3, 5)
    NEW = (10, 12, 14, 15)

    def present(q, n):
        if n in OLD:
            return q > 0
        return (q < NQ - 1) if n in NEW else (0 <= q < NQ)

    upto = Fills(FILLS, present).upto

    def chunks(g, u):
        return [(u, 2 * g), (u, 2 * g + 1)] if g < 2 else [(0, GC - 1), (1, GC - 1)]

    def part(buf, g, u):
        return buf[:, u, 2 * g:2 * g + 2, :] if g < 2 else buf[:, :, GC - 1, :]

    def dyn(ap, i, q):
        t, u = i % ST, i // ST
        return ap[:, t, bass.ds(q * (2 * E1) + u * E1, E1)] if not isinstance(q, int) \
            else ap[:, t, (2 * q + u) * E1:(2 * q + u + 1) * E1]

    def pair_of(ap, q):
        v_ = ap.rearrange("b (t p) d -> p (b t) d", p=P)
        return v_[:, q * 2 * ST:(q + 1) * 2 * ST, :] if isinstance(q, int) else v_[:, bass.ds(q * (2 * ST), 2 * ST), :]

    def empty(n, copy):
        bank = ps_m[n % 2]
        if n in TOKENS:
            half, u, c = TOKENS[n]
            return copy(tokT[:, c, u, half * HALF:(half + 1) * HALF], bank[:, 0:HALF])
        g, u = GATES[n] if n in GATES else RESULTS[n]
        return copy(part(gatedT if n in GATES else y, g, u), bank[0:GS, :].rearrange("p (c s) -> p c s", c=2))

    with nc.Block() as block:

        @block.sync
        def _(sp):
            sp.dma_start(xn[:], pair_of(dram["x3n"], 0)).then_inc(s_xn, 16)
            sp.dma_start(x3[:], pair_of(dram["x3"], 0)).then_inc(s_x3, 16)
            sp.dma_start(b1[:], io["fb1"].rearrange("e (c p) -> p e c", p=P), allow_slow_non_contiguous=True).then_inc(s_const, 16)
            sp.dma_start(b2[:], io["fb2"].rearrange("e (c p) -> p e c", p=P), allow_slow_non_contiguous=True).then_inc(s_const, 16)
            for e in range(E1):
                if e >= 2:
                    sp.wait_ge(s_f2[e % 2], 16 * (e // 2))
                sp.dma_start(f2[:, e], io["f2"][e].rearrange("(c p) n -> p c n", p=P)).then_inc(s_f2[e % 2], 16)

            def load_xn(q):
                sp.wait_ge(t_fill, upto(q - 1, 6))
                sp.dma_start(xn[:], pair_of(dram["x3n"], q)).then_inc(s_xn, 16)

            def store(p):
                sp.wait_ge(ev[1], upto(p + 1, 5, 1))
                sp.dma_start(pair_of(out, p), x3[:]).then_inc(s_out, 16)
                sp.wait_ge(s_out, 16 * (p + 1))

            def load_x3(q):
                sp.dma_start(x3[:], pair_of(dram["x3"], q)).then_inc(s_x3, 16)

            load_xn(1)
            with sp.Fori(1, NQ - 1) as q:
                store(q - 1)
                load_x3(q)
                load_xn(q + 1)
            store(NQ - 2)
            load_x3(NQ - 1)
            store(NQ - 1)

        @block.gpsimd
        def _(pool):
            pool.iota(slot_id[:], [[1, CAP1]], base=1, channel_multiplier=0,
                      allow_small_or_imprecise_dtypes=True).then_inc(p_const, 1)

            def gate(q):
                after(pool, v_sel, q + 1, alone=p_waits)
                after(pool, t_fill, upto(q - 1, 17), alone=p_waits)
                for i in range(2 * ST):
                    ins = pool.tensor_tensor(gated[:, i, :].rearrange("p (e c) -> p e c", c=CAP1),
                                             sel[:, i, :].rearrange("p (e c) -> p e c", c=CAP1),
                                             dyn(gate_all, i, q).unsqueeze(2).broadcast_to([P, E1, CAP1]), ALU.mult)
                ins.then_inc(p_gated, 1)

            pool.wait_ge(v_sel, 1)
            gate(0)
            gate(1)
            with pool.Fori(2, NQ) as q:
                gate(q)

        @block.vector
        def _(dve):
            dve.wait_ge(p_const, 1)
            dve.wait_ge(s_const, 32)

            def select(q):
                after(dve, t_fill, upto(q - 1, 6) if not (isinstance(q, int) and q == 0) else 0)
                after(dve, p_gated, q)
                for i in range(2 * ST):
                    ins = dve.tensor_tensor(sel[:, i, :].rearrange("p (e c) -> p e c", c=CAP1),
                                            slot_id[:].unsqueeze(1).broadcast_to([P, E1, CAP1]),
                                            dyn(pos_all, i, q).unsqueeze(2).broadcast_to([P, E1, CAP1]), ALU.is_equal)
                ins.then_inc(v_sel, 1)

            def fill_evac(q, n):
                dve.wait_ge(t_fill, upto(q, n))
                if n in SUMS:
                    u = SUMS[n]
                    if u == 0:
                        dve.wait_ge(s_x3, 16 * q)
                    ins = dve.scalar_tensor_tensor(out=x3[:, u * ST:(u + 1) * ST, :], in0=ps_m[1][:, :], scalar=tanh_g[:, 3:4],
                                                   in1=x3[:, u * ST:(u + 1) * ST, :], op0=ALU.mult, op1=ALU.add)
                else:
                    ins = empty(n, dve.tensor_copy)
                ins.then_inc(ev[1], 1)

            def yT_evac(q, e):
                dve.wait_ge(t_y, E1 * q + e + 1)
                for c in range(DC):
                    ins = dve.tensor_scalar(yT[:, c, :, e * CAP1:(e + 1) * CAP1],
                                            ps_y[e % 2][:, c * N2:(c + 1) * N2].rearrange("p (u s) -> p u s", u=2),
                                            b2[:, e, c:c + 1], None, ALU.add)
                ins.then_inc(v_y, 1)

            def pair(q, first, last):
                for s in range(E1 + 1):
                    n = 2 * s + 1
                    if not (first and n in OLD) and not (last and n in NEW):
                        fill_evac(q, n)
                    if s == 3 and not last:
                        select(q + 1)
                    if s > 0:
                        yT_evac(q, s - 1)
                fill_evac(q, FILLS - 1)

            select(0)
            fill_evac(-1, 15)
            pair(0, True, False)
            with dve.Fori(1, NQ - 1) as q:
                pair(q, False, False)
            pair(NQ - 1, False, True)
            fill_evac(NQ, 3)
            fill_evac(NQ, 5)

        @block.scalar
        def _(act):
            act.wait_ge(s_const, 32)

            def fill_evac(q, n):
                act.wait_ge(t_fill, upto(q, n))
                empty(n, lambda dst, src: act.activation(dst, src, ACT.Copy)).then_inc(ev[0], 1)

            def gelu(q, e):
                for i, (o, m) in enumerate(UNITS):
                    unit = UPE * e + i
                    act.wait_ge(t_h, q * (UPE * E1) + (unit + 1))
                    if i == 0:
                        after(act, t_y, E1 * q + e - 1)
                    for c in range(m):
                        ins = act.activation(hid[:, e % 2, o + c, :], ps_h[unit % 4][:, c * N2:(c + 1) * N2],
                                             ACT.Gelu, bias=b1[:, e, o + c:o + c + 1])
                    ins.then_inc(a_h, 1)

            def pair(q, first, last):
                for s in range(E1 + 1):
                    if s < E1:
                        gelu(q, s)
                    n = 2 * s
                    if not (first and n in OLD) and not (last and n in NEW):
                        fill_evac(q, n)
                fill_evac(q, FILLS - 2)

            for n in (10, 12, 14):
                fill_evac(-1, n)
            pair(0, True, False)
            with act.Fori(1, NQ - 1) as q:
                pair(q, False, False)
            pair(NQ - 1, False, True)
            fill_evac(NQ, 0)

        @block.tensor
        def _(pe):
            def fill(q, n):
                after(pe, ev[n % 2], upto(q, n, n % 2) - 1)
                bank = ps_m[n % 2]
                if n in TOKENS:
                    half, u, c = TOKENS[n]
                    if n == min(NEW):
                        pe.wait_ge(s_xn, 16 * (q + 2))
                        pe.wait_ge(v_sel, q + 2)
                    for t in range(ST):
                        i = u * ST + t
                        ins = pe.matmul(bank[:, 0:HALF], xn[:, i, c * P:(c + 1) * P], sel[:, i, half * HALF:(half + 1) * HALF],
                                        start=(t == 0), stop=(t == ST - 1))
                elif n in GATES:
                    if n == min(GATES):
                        pe.wait_ge(p_gated, q + 1)
                    for j, (u, c) in enumerate(chunks(*GATES[n])):
                        for t in range(ST):
                            ins = pe.transpose(bank[0:GS, j * S + t * P:j * S + (t + 1) * P],
                                               gated[:, u * ST + t, c * GS:(c + 1) * GS], ident[:])
                elif n in RESULTS:
                    pe.wait_ge(v_y, {0: E1 * q, 11: E1 * q + 4, 13: E1 * q + 4, 18: E1 * q + 7, 19: E1 * q + 7}[n])
                    for j, (u, c) in enumerate(chunks(*RESULTS[n])):
                        for d in range(DC):
                            ins = pe.transpose(bank[0:GS, j * D + d * P:j * D + (d + 1) * P],
                                               yT[:, d, u, c * GS:(c + 1) * GS], ident[:])
                else:
                    u = SUMS[n]
                    pe.wait_ge(ev[0], upto(q, 0, 0))
                    for t in range(ST):
                        for c in range(GC):
                            ins = pe.matmul(bank[:, t * D:(t + 1) * D], gatedT[:, u, c, t * P:(t + 1) * P], y[:, u, c, :],
                                            start=(c == 0), stop=(c == GC - 1))
                ins.then_inc(t_fill, 1)

            def up(q, e):
                if e % 4 == 0:
                    for bank, n in ((0, 14), (1, 15)) if e == 0 else ((0, 6), (1, 1)):
                        pe.wait_ge(ev[bank], upto(q - 1 if e == 0 else q, n, bank))
                for i, (o, m) in enumerate(UNITS):
                    unit = UPE * e + i
                    after(pe, a_h, q * (UPE * E1) + (unit - 3))
                    for c in range(m):
                        for k in range(DC):
                            ins = pe.matmul(ps_h[unit % 4][:, c * N2:(c + 1) * N2],
                                            f1[:, e, k, (o + c) * P:(o + c + 1) * P], tokT[:, k, :, e * CAP1:(e + 1) * CAP1],
                                            start=(k == 0), stop=(k == DC - 1))
                    ins.then_inc(t_h, 1)

            def down(q, e):
                pe.wait_ge(a_h, q * (UPE * E1) + UPE * (e + 1))
                after(pe, v_y, E1 * q + e - 1)
                if isinstance(q, int) and q == 0:
                    pe.wait_ge(s_f2[e % 2], 16 * (e // 2 + 1))
                for d in range(DC):
                    for c in range(HC):
                        ins = pe.matmul(ps_y[e % 2][:, d * N2:(d + 1) * N2], f2[:, e, c, d * P:(d + 1) * P],
                                        hid[:, e % 2, c, :], start=(c == 0), stop=(c == HC - 1))
                ins.then_inc(t_y, 1)

            def pair(q, first, last):
                for s in range(E1 + 1):
                    if s < E1:
                        up(q, s)
                    for n in (2 * s, 2 * s + 1):
                        if not (first and n in OLD) and not (last and n in NEW):
                            fill(q, n)
                    if s > 0:
                        down(q, s - 1)
                fill(q, FILLS - 2)
                fill(q, FILLS - 1)

            for n in NEW:
                fill(-1, n)
            pair(0, True, False)
            with pe.Fori(1, NQ - 1) as q:
                pair(q, False, False)
            pair(NQ - 1, False, True)
            for n in OLD:
                fill(NQ, n)


def build(nc, io, out, NB=BATCH, NE=E0, debug=None):
    with ExitStack() as whole:
        stage_name = ["all"]

        def tensor(stack):
            return lambda name, shape, dt=F32: stack.enter_context(nc.sbuf_tensor(f"{stage_name[0]}_{name}", shape, dt))

        def bank(stack):
            return lambda name: stack.enter_context(nc.psum_tensor(name, [P, 512], F32))

        def sem(name):
            return whole.enter_context(nc.semaphore(name))

        dram = debug or {}
        for name, shape in (("x1", (BATCH, S, D)), ("rows", (E0 * CAP0, D)), ("y", (E0 * CAP0, D)),
                            ("x3", (BATCH, S, D)), ("x3n", (BATCH, S, D))):
            if name not in dram:
                dram[name] = nc.dram_tensor(f"{name}_scratch", shape, F32).ap()
        sb = tensor(whole)
        keep = {
            "ident": sb("ident", [P, P]), "gates": sb("gates", [P, 4]), "tanh_g": sb("tanh_g", [P, 4]),
            "slots_all": sb("slots_all", [P, BATCH * ST, 8], U32), "w_all": sb("w_all", [P, BATCH * ST, 8]),
        }
        with ExitStack() as stage:
            stage_name[0] = "a"
            attention_and_router(nc, tensor(stage), bank(stage), sem, io, dram, keep, NB)
        stage_name[0] = "all"
        keep["gate_all"] = sb("gate_all", [P, ST, BATCH * E1])
        keep["f1"] = sb("f1", [P, E1, DC, HID])
        keep["s_f1"] = sem("f1_loaded")
        with ExitStack() as layer1_attention:
            keep["s_c_weights"] = sem("c_weights_loaded")
            c_sb = tensor(layer1_attention)
            for name in ("c_wq", "c_wk", "c_wv"):
                keep[name] = c_sb(name, [P, DC, HD])
            keep["c_wo"] = c_sb("c_wo", [P, HD // P, D])
            keep["router_w"] = c_sb("router_w", [P, DC, E1])
            with ExitStack() as stage:
                stage_name[0] = "b"
                experts(nc, tensor(stage), bank(stage), sem, io, dram, keep, NE)
            with ExitStack() as stage:
                stage_name[0] = "c"
                attention_and_top(nc, tensor(stage), bank(stage), sem, io, dram, keep, NB)
        keep["pos_all"] = sb("pos_all", [P, ST, BATCH * E1])
        with ExitStack() as stage:
            stage_name[0] = "e"
            choose_tokens(nc, tensor(stage), bank(stage), sem, io, dram, keep, NB)
        with ExitStack() as stage:
            stage_name[0] = "d"
            expert_choice(nc, tensor(stage), bank(stage), sem, io, out, dram, keep, NB)


def lay_out(inputs, np):
    a = {k: np.asarray(v) for k, v in inputs.items()}
    t = lambda m: np.ascontiguousarray(np.swapaxes(m, -1, -2))
    return {
        "x": a["x"], "ctxT": t(a["ctx_1024"]), "mask": a["mask_1x1xSxS2_fk1"][0, 0],
        "gates": np.concatenate([a["g_xattn"], a["g_ffn"]]),
        "wq": a["L0_xattn_Wq"], "wk": a["L0_xattn_Wk"], "wv": a["L0_xattn_Wv"], "wo": a["L0_xattn_Wo"],
        "bq": a["L0_xattn_bq"], "bk": a["L0_xattn_bk"], "bv": a["L0_xattn_bv"], "bo": a["L0_xattn_bo"],
        "gate_w": t(a["L0_ffn_gate_w"]), "gate_b": a["L0_ffn_gate_b"],
        "w1": t(a["L0_ffn_w1"]), "w2": t(a["L0_ffn_w2"]), "w3": t(a["L0_ffn_w3"]),
        "ws1": t(a["L0_ffn_ws1"]), "ws2": t(a["L0_ffn_ws2"]), "ws3": t(a["L0_ffn_ws3"]),
        "w_q": a["L1_xattn_W_Q"], "w_k": a["L1_xattn_W_K"], "w_v": a["L1_xattn_W_V"], "w_o": a["L1_xattn_W_O"],
        "router_w": t(a["L1_ffn_router_w"]),
        "f1": a["L1_ffn_w1"], "fb1": a["L1_ffn_b1"], "f2": a["L1_ffn_w2"], "fb2": a["L1_ffn_b2"],
    }


def kernel(**inputs):
    import numpy as _np
    import concourse.bacc as _bacc
    from concourse import mybir as _mybir
    from concourse.bass_utils import run_bass_kernel_spmd as _run

    nc = _bacc.Bacc("TRN2", target_bir_lowering=False, num_devices=1)
    arrays, io = {}, {}
    for name, a in lay_out(inputs, _np).items():
        a = _np.ascontiguousarray(a)
        arrays[f"{name}_in"] = a
        io[name] = nc.dram_tensor(f"{name}_in", a.shape, _mybir.dt.from_np(a.dtype), kind="ExternalInput").ap()
    out = nc.dram_tensor("out", (BATCH, S, D), _mybir.dt.float32, kind="ExternalOutput").ap()
    build(nc, io, out)
    r = _run(nc, [arrays], core_ids=[0])
    return r.results[0]["out"]
```

```python
from contextlib import ExitStack

import concourse.bass as bass
from concourse import mybir

F32 = mybir.dt.float32
U32 = mybir.dt.uint32
I32 = mybir.dt.int32
BF16 = mybir.dt.bfloat16
ALU = mybir.AluOpType
ACT = mybir.ActivationFunctionType
AX = mybir.AxisListType.X

P = 128
BATCH, S, D = 32, 256, 256
ST = S // P
DC = D // P
HEADS = 16
DEPTH = D // HEADS
HPC = P // DEPTH
PACK = 4
PAD = P // PACK
PARTS = 3
PRODUCTS = [(0, 0), (0, 1), (1, 0), (1, 1), (0, 2), (2, 0)]
STACK = len(PRODUCTS) * DEPTH
NEG = -1.0e9
EPS = 1e-5
HUGE = 3.0e38
BIG_SLOT = 1.0e6

E0, TOPK, CAP0, I0 = 64, 6, 128, 176
SI = 2 * I0
SI_CHUNKS = [(0, 128), (128, 128), (256, SI - 256)]
I0_CHUNKS = [(0, 128), (128, I0 - 128)]

DK = 64
HD = HEADS * DK
E1, HID = 8, 1024
CAP1 = int(S * 2.0 / E1) + 1
SLOTS = E1 * CAP1
HC = HID // P
GC = 5
GS = SLOTS // GC


def after(eng, sem, value, alone=None):
    if isinstance(value, int) and value <= 0:
        return
    eng.wait_ge(sem, value)
    if alone is not None and not isinstance(value, int):
        eng.sem_inc(alone, 1)


class Chain:

    def __init__(self, eng, sem, size, step, alone=None):
        self.eng, self.sem, self.size, self.base, self.count = eng, sem, size, step * size, 0
        self.alone = alone

    def done(self, ins):
        self.count += 1
        ins.then_inc(self.sem, 1)

    def wait(self):
        after(self.eng, self.sem, self.base + self.count, self.alone)

    def end(self):
        assert self.count == self.size, (self.count, self.size)


class Fills:

    def __init__(self, per, present):
        self.per, self.present = per, present

    def upto(self, turn, n, bank=None):
        if not isinstance(turn, int):
            step = self.per if bank is None else self.per // 2
            return turn * step + (self.upto(1, n, bank) - step)
        return sum(self.present(r, m) and (r < turn or m <= n) and bank in (None, m % 2)
                   for r in range(-1, turn + 1) for m in range(self.per))


def tiles(ap):
    return ap.rearrange("(t p) d -> p t d", p=P)


def attention_and_router(nc, sb, psum, sem, io, dram, keep, NB):
    wq, wk, wv, wo = (sb(n, [P, DC, D]) for n in ("wq", "wk", "wv", "wo"))
    gate_w = sb("gate_w", [P, DC, E0])
    ws1, ws3 = sb("ws1", [P, DC, SI]), sb("ws3", [P, DC, SI])
    ws2 = sb("ws2", [P, 3, D])
    bq, bk = sb("bq", [P, DC]), sb("bk", [P, DC])
    bv, bo = sb("bv", [P, D]), sb("bo", [P, D])
    gate_b = sb("gate_b", [P, E0])
    mask = sb("mask", [P, ST, S])
    upper = sb("upper", [P, P])
    ones = sb("ones", [P, P])
    minus_half = sb("minus_half", [P, 2])
    expert_base = sb("expert_base", [P, E0])

    x_in = sb("x_in", [P, ST, D])
    stats = sb("stats", [P, ST, 6])
    mv = sb("mv", [P, ST, 2])
    var_eps = sb("var_eps", [P, ST])
    rstd = sb("rstd", [P, ST])
    xln = sb("xln", [P, ST, D])
    xlnT = sb("xlnT", [P, DC, S])
    ctxT = sb("ctxT", [P, DC, S])
    q = sb("q", [P, DC, S])
    kT = sb("kT", [P, DC, S])
    rest = sb("rest", [P, DC, S])
    parts = {"q": sb("q_parts", [P, PARTS, DC, S], BF16), "k": sb("k_parts", [P, PARTS, DC, S], BF16)}
    stack = {"q": sb("q_stack", [P, 2, HEADS, S], BF16), "k": sb("k_stack", [P, 2, HEADS, S], BF16)}
    vx = sb("vx", [P, 2, ST, HEADS * PAD])
    neg_s = sb("neg_s", [P, 4, ST, S])
    neg_max = sb("neg_max", [P, 4, ST])
    probs = sb("probs", [P, 4, ST, S])
    probsT = sb("probsT", [P, 2 * PACK, ST, S])
    oT = sb("oT", [P, 2, S])
    inv_sum = sb("inv_sum", [P, 2, ST, PACK])
    attn = sb("attn", [P, ST, D])
    attnT = sb("attnT", [P, DC, S])
    xr = sb("xr", [P, ST, D])
    stats2 = sb("stats2", [P, ST, 6])
    mv2 = sb("mv2", [P, ST, 2])
    var_eps2 = sb("var_eps2", [P, ST])
    rstd2 = sb("rstd2", [P, ST])
    xf = sb("xf", [P, ST, D])
    xfT = sb("xfT", [P, DC, S])
    r_negmax = sb("r_negmax", [P, ST])
    r_exp = sb("r_exp", [P, ST, E0])
    r_sum = sb("r_sum", [P, ST])
    r_inv = sb("r_inv", [P, ST])
    scores = sb("scores", [P, ST, E0])
    biased = sb("biased", [P, ST, E0 + 2])
    top8 = sb("top8", [P, ST, 8])
    replaced = sb("replaced", [P, ST, E0 + 2])
    chosen = sb("chosen", [P, ST, E0])
    seen = sb("seen", [P, E0])
    fits = sb("fits", [P, ST, E0])
    numbered = sb("numbered", [P, ST, E0])
    slot_of = sb("slot_of", [P, ST, E0])
    weight_of = sb("weight_of", [P, ST, E0])
    slot8 = sb("slot8", [P, ST, 8])
    no_slot = sb("no_slot", [P, ST, 8])
    picked = sb("picked", [P, ST * TOPK, E0])
    slots = sb("slots", [P, ST, 8], U32)
    w8 = sb("w8", [P, ST, 8])
    th = sb("th", [P, 2, S])
    silu2 = sb("silu2", [P, 2, S])
    hidden = sb("hidden", [P, 3, S])
    zero_rows = sb("zero_rows", [P, 8, D])
    ident, tanh_g, slots_all, w_all = keep["ident"], keep["tanh_g"], keep["slots_all"], keep["w_all"]

    ps_s = [psum(f"ps_s{i}") for i in range(2)]
    ps_t = [psum(f"ps_t{i}") for i in range(2)]
    ps_o = [psum(f"ps_o{i}") for i in range(2)]
    ps_m = [psum(f"ps_m{i}") for i in range(2)]

    s_const = sem("a_const_loaded")
    s_zero = sem("a_zeros_stored")
    s_x = sem("a_x_loaded")
    s_ctx = sem("a_ctx_loaded")
    s_xr = sem("a_residual_loaded")
    s_store = sem("a_x1_stored")
    s_scat = sem("a_rows_scattered")
    s_pc = sem("a_pool_consts")
    s_setup = sem("a_vector_setup")
    s_tanh = sem("a_tanh_ready")
    s_zset = sem("a_zero_rows_ready")
    v_waits, p_waits = sem("a_vector_waits"), sem("a_pool_waits")
    v_ln = sem("a_ln1_chain")
    p_rs1 = sem("a_rstd1_ready")
    p_rs1c = sem("a_rstd1_chain")
    v_xln = sem("a_xln_ready")
    t_xln = sem("a_xlnT_in_psum")
    a_xln = sem("a_xlnT_ready")
    t_q = sem("a_q_in_psum")
    a_q = sem("a_q_ready")
    p_rest, p_mid, p_parts = sem("a_rest_ready"), sem("a_middle_ready"), sem("a_parts_ready")
    sp_waits = sem("a_sync_waits")
    s_parts, s_stack = sem("a_parts_stored"), sem("a_stack_loaded")
    t_k, a_k = sem("a_k_in_psum"), sem("a_k_ready")
    t_v, v_v = sem("a_v_in_psum"), sem("a_v_ready")
    t_s = sem("a_scores_in_psum")
    v_m = sem("a_scores_masked")
    a_e = sem("a_probs_ready")
    t_t = sem("a_probsT_in_psum")
    te = [sem("a_probsT_even_ready"), sem("a_probsT_odd_ready")]
    t_pv = sem("a_pv_done")
    a_o, t_o = sem("a_oT_ready"), sem("a_o_in_psum")
    v_inv = sem("a_inv_sum")
    v_on = sem("a_attn_ready")
    t_ot, a_ot = sem("a_attnT_in_psum"), sem("a_attnT_ready")
    t_wo = sem("a_wo_in_psum")
    v_xr = sem("a_residual_biased")
    v_x1 = sem("a_x1_ready")
    v_st = sem("a_ln2_chain")
    p_rs2 = sem("a_rstd2_ready")
    p_rs2c = sem("a_rstd2_chain")
    v_xf = sem("a_xf_ready")
    t_xf, a_xf = sem("a_xfT_in_psum"), sem("a_xfT_ready")
    t_r = sem("a_logits_in_psum")
    v_rm = sem("a_logits_max")
    a_r = sem("a_logits_exp")
    v_rc = sem("a_router_chain")
    v_ch = sem("a_chosen_ready")
    t_pos = sem("a_positions_in_psum")
    p_seen = sem("a_seen_updated")
    v_pos = sem("a_position_chain")
    v_slot = sem("a_slots_ready")
    t_h = sem("a_hidden_in_psum")
    a_th = sem("a_hidden_tanh")
    v_hc = sem("a_hidden_chain")
    v_h = sem("a_hidden_ready")
    t_z = sem("a_z_in_psum")
    v_z = sem("a_x1z_ready")

    RC, PC = 8, 8
    LAG = 3
    STEPS = HEADS + LAG + 2
    GROUPS = HEADS // PACK
    AT_X1 = 3
    N_CONST = 16

    with nc.Block() as block:

        @block.sync
        def _(sp):
            for dst, src in ((wq, io["wq"]), (wk, io["wk"]), (wv, io["wv"]), (wo, io["wo"]),
                             (gate_w, io["gate_w"]), (ws1, io["ws1"]), (ws3, io["ws3"])):
                sp.dma_start(dst[:], src.rearrange("(c p) n -> p c n", p=P)).then_inc(s_const, 16)
            sp.dma_start(ws2[:, 0:2, :], io["ws2"][0:256].rearrange("(c p) n -> p c n", p=P)).then_inc(s_const, 16)
            sp.dma_start(ws2[0:SI - 256, 2, :], io["ws2"][256:SI]).then_inc(s_const, 16)
            sp.dma_start(bq[:], io["bq"].rearrange("(c p) -> p c", p=P), allow_slow_non_contiguous=True).then_inc(s_const, 16)
            sp.dma_start(bk[:], io["bk"].rearrange("(c p) -> p c", p=P), allow_slow_non_contiguous=True).then_inc(s_const, 16)
            sp.dma_start(bv[:], io["bv"].rearrange("(a n) -> a n", a=1).broadcast_to([P, D])).then_inc(s_const, 16)
            sp.dma_start(bo[:], io["bo"].rearrange("(a n) -> a n", a=1).broadcast_to([P, D])).then_inc(s_const, 16)
            sp.dma_start(gate_b[:], io["gate_b"].rearrange("(a n) -> a n", a=1).broadcast_to([P, E0])).then_inc(s_const, 16)
            sp.dma_start(mask[:], tiles(io["mask"])).then_inc(s_const, 16)
            sp.dma_start(keep["gates"][:], io["gates"].rearrange("(a n) -> a n", a=1).broadcast_to([P, 4])).then_inc(s_const, 16)
            sp.dma_start(x_in[:], tiles(io["x"][0])).then_inc(s_x, 16)
            sp.dma_start(ctxT[:], tiles(io["ctxT"][0])).then_inc(s_ctx, 16)
            sp.dma_start(xr[:], tiles(io["x"][0])).then_inc(s_xr, 16)
            sp.wait_ge(s_zset, 1)
            for i in range(8):
                sp.dma_start(dram["rows"][i * 1024:(i + 1) * 1024].rearrange("(p r) d -> p r d", p=P),
                             zero_rows[:]).then_inc(s_zero, 16)

            def load(b):
                sp.wait_ge(v_xln, b)
                sp.dma_start(x_in[:], tiles(io["x"][b])).then_inc(s_x, 16)
                sp.wait_ge(t_v, b)
                sp.dma_start(ctxT[:], tiles(io["ctxT"][b])).then_inc(s_ctx, 16)

            def restack(b, u):
                for i, name in enumerate(("q", "k")):
                    after(sp, p_parts, 2 * b + i + 1, alone=sp_waits)
                    if i == 0 and not (isinstance(b, int) and b == 0):
                        sp.wait_ge(s_stack, 16 * 2 * len(PRODUCTS) * b)
                    sp.dma_start(dram["parts"][i].rearrange("a (c p) s -> p a c s", p=P), parts[name][:]).then_inc(s_parts, 16)
                after(sp, s_parts, 32 * (b + 1), alone=sp_waits)
                if not (isinstance(b, int) and b < 2):
                    sp.wait_ge(t_s, HEADS * (b - 1))
                for i, name in enumerate(("q", "k")):
                    for g, product in enumerate(PRODUCTS):
                        sp.dma_start(stack[name][g * DEPTH:(g + 1) * DEPTH, u, :, :],
                                     dram["parts"][i, product[i]].rearrange("(h d) s -> d h s", d=DEPTH)).then_inc(s_stack, 16)

            def store(p):
                sp.wait_ge(v_z, p + 1)
                sp.dma_start(tiles(dram["x1"][p]), xr[:]).then_inc(s_store, 16)
                sp.wait_ge(s_store, (p + 1) * 16)

            def residual(b):
                sp.dma_start(xr[:], tiles(io["x"][b])).then_inc(s_xr, 16)

            def batch(b, u, last):
                if last > 0:
                    restack(b + 1, 1 - u)
                if not (isinstance(b, int) and b == 0):
                    store(b - 1)
                    residual(b)
                if last > 2:
                    load(b + 3)

            load(1)
            restack(0, 0)
            load(2)
            batch(0, 0, 3)
            batch(1, 1, 3)
            with sp.Fori(1, NB // 2 - 2) as half:
                batch(half * 2, 0, 3)
                batch(half * 2 + 1, 1, 3)
            batch(NB - 4, 0, 3)
            batch(NB - 3, 1, 2)
            batch(NB - 2, 0, 1)
            batch(NB - 1, 1, 0)
            store(NB - 1)
            sp.wait_ge(s_zero, 16 * 8)

        @block.gpsimd
        def _(pool):
            pool.memset(zero_rows[:], 0.0).then_inc(s_zset, 1)
            pool.memset(ident[:], 0.0).then_inc(s_pc, 1)
            pool.memset(upper[:], 1.0).then_inc(s_pc, 1)
            pool.memset(ones[:], 1.0).then_inc(s_pc, 1)
            pool.memset(seen[:], 0.0).then_inc(s_pc, 1)
            pool.memset(minus_half[:], -0.5).then_inc(s_pc, 1)
            pool.iota(expert_base[:], [[CAP0, E0]], base=0, channel_multiplier=0,
                      allow_small_or_imprecise_dtypes=True).then_inc(s_pc, 1)
            pool.wait_ge(s_pc, 6)
            pool.affine_select(out=ident[:], in_=ident[:], compare_op=ALU.not_equal, fill=1.0, base=0,
                               pattern=[[-1, P]], channel_multiplier=1).then_inc(s_pc, 1)
            pool.affine_select(out=upper[:], in_=upper[:], compare_op=ALU.is_ge, fill=0.0, base=0,
                               pattern=[[1, P]], channel_multiplier=-1).then_inc(s_pc, 1)

            def rsqrt(b, mv_, var_eps_, rstd_, chain, stats_done, stats_size, ready):
                after(pool, stats_done, (b + 1) * stats_size, alone=p_waits)
                pool.tensor_scalar(var_eps_[:], mv_[:, :, 1], EPS, None, ALU.add).then_inc(chain, 1)
                pool.wait_ge(chain, b + 1)
                pool.tensor_tensor(rstd_[:], var_eps_[:], minus_half[:], ALU.pow).then_inc(ready, 1)

            def scatter(p):
                for t in range(ST):
                    pool.wait_ge(t_pos, p + 1)
                    if t:
                        pool.wait_ge(p_seen, ST * p + t)
                    pool.tensor_tensor(seen[:], seen[:], chosen[:, t, :], ALU.add).then_inc(p_seen, 1)
                after(pool, v_slot, p + 1, alone=p_waits)
                if isinstance(p, int) and p == 0:
                    pool.wait_ge(s_zero, 16 * 8)
                for t in range(ST):
                    for k in range(TOPK):
                        pool.indirect_dma_start(
                            out=dram["rows"], out_offset=bass.IndirectOffsetOnAxis(ap=slots[:, t, k:k + 1], axis=0),
                            in_=xf[:, t, :], in_offset=None,
                            bounds_check=E0 * CAP0 - 1, oob_is_err=False).then_inc(s_scat, 16)

            def split(b):
                for i, (name, src, ready) in enumerate((("q", q, a_q), ("k", kT, a_k))):
                    n, part = 2 * b + i, parts[name]
                    after(pool, ready, b + 1, alone=p_waits)
                    if not (isinstance(b, int) and b == 0 and i == 0):
                        after(pool, p_parts, n, alone=p_waits)
                    pool.tensor_tensor(rest[:], src[:], part[:, 0], ALU.subtract).then_inc(p_rest, 1)
                    after(pool, p_rest, n + 1, alone=p_waits)
                    pool.tensor_copy(part[:, 1], rest[:]).then_inc(p_mid, 1)
                    after(pool, p_mid, n + 1, alone=p_waits)
                    pool.tensor_tensor(part[:, 2], rest[:], part[:, 1], ALU.subtract).then_inc(p_parts, 1)

            def ln1(b):
                rsqrt(b, mv, var_eps, rstd, p_rs1c, v_ln, 4, p_rs1)

            def batch(b, last):
                first = isinstance(b, int) and b == 0
                if not first:
                    rsqrt(b - 1, mv2, var_eps2, rstd2, p_rs2c, v_st, 4, p_rs2)
                if last > 0:
                    split(b + 1)
                if last > 1:
                    ln1(b + 2)
                if not first:
                    scatter(b - 1)

            ln1(0)
            split(0)
            ln1(1)
            batch(0, 2)
            batch(1, 2)
            with pool.Fori(2, NB - 2) as b:
                batch(b, 2)
            batch(NB - 2, 1)
            batch(NB - 1, 0)
            rsqrt(NB - 1, mv2, var_eps2, rstd2, p_rs2c, v_st, 4, p_rs2)
            scatter(NB - 1)
            pool.wait_ge(s_scat, 16 * ST * TOPK * NB)

        @block.vector
        def _(dve):
            dve.wait_ge(s_const, 16 * N_CONST)
            dve.wait_ge(s_pc, 8)
            dve.memset(vx[:], 0.0).then_inc(s_setup, 1)
            dve.memset(biased[:], -HUGE).then_inc(s_setup, 1)
            dve.wait_ge(s_tanh, 1)
            dve.tensor_scalar(bo[:], bo[:], tanh_g[:, 0:1], None, ALU.mult).then_inc(s_setup, 1)
            dve.tensor_scalar(mask[:], mask[:], NEG, None, ALU.mult).then_inc(s_setup, 1)
            dve.tensor_scalar(bq[:], bq[:], DEPTH ** -0.5, None, ALU.mult).then_inc(s_setup, 1)
            dve.wait_ge(s_setup, 5)
            for u in range(2):
                dve.memset(vx[:, u].rearrange("p t (h e) -> p (t h) e", e=PAD)[:, :, DEPTH], 1.0).then_inc(s_setup, 1)
            dve.wait_ge(s_setup, 7)

            def layernorm1(b):
                c = Chain(dve, v_ln, 4, b, alone=v_waits)
                dve.wait_ge(s_x, (b + 1) * 16)
                for t in range(ST):
                    c.done(dve.bn_stats(stats[:, t, :], x_in[:, t, :]))
                c.wait()
                for t in range(ST):
                    c.done(dve.bn_aggr(mv[:, t, :], stats[:, t, :]))
                c.wait()
                c.end()

            def layernorm1_apply(b):
                dve.wait_ge(p_rs1, b + 1)
                after(dve, t_xln, b)
                for t in range(ST):
                    ins = dve.tensor_scalar(xln[:, t, :], x_in[:, t, :], mv[:, t, 0:1], rstd[:, t:t + 1],
                                            ALU.subtract, ALU.mult)
                ins.then_inc(v_xln, 1)

            def v_evac(b, u):
                dve.wait_ge(t_v, b + 1)
                if not (isinstance(b, int) and b < 2):
                    dve.wait_ge(t_pv, GROUPS * (b - 1))
                for t in range(ST):
                    ins = dve.tensor_tensor(
                        vx[:, u, t, :].rearrange("p (h e) -> p h e", e=PAD)[:, :, 0:DEPTH],
                        ps_m[1][:, t * D:(t + 1) * D].rearrange("p (h e) -> p h e", e=DEPTH),
                        bv[:].rearrange("p (h e) -> p h e", e=DEPTH), ALU.add)
                ins.then_inc(v_v, 1)

            def mask_and_max(b, i):
                after(dve, t_s, HEADS * b + i + 1, alone=v_waits)
                after(dve, a_e, HEADS * b + i - 3, alone=v_waits)
                for t in range(ST):
                    ins = dve.tensor_tensor_reduce(
                        out=neg_s[:, i % 4, t, :], in0=ps_s[i % 2][:, t * S:(t + 1) * S], in1=mask[:, t, :],
                        scale=-1.0, scalar=HUGE, op0=ALU.add, op1=ALU.min, accum_out=neg_max[:, i % 4, t:t + 1])
                ins.then_inc(v_m, 1)

            def probsT_evac(b, i):
                dve.wait_ge(t_t, HEADS * b + i + 1)
                after(dve, t_pv, GROUPS * b + i // PACK - 1)
                dve.tensor_copy(probsT[:, i % (2 * PACK), :, :], ps_t[1][:, :]).then_inc(te[1], 1)

            def normalise(b, g):
                dve.wait_ge(t_o, GROUPS * b + g + 1)
                if g == 0:
                    after(dve, t_ot, b)
                o = ps_o[g % 2][:, S:2 * S].rearrange("p (t h e) -> p t h e", t=ST, e=PAD)
                dve.reciprocal(inv_sum[:, g % 2, :, :], o[:, :, :, DEPTH]).then_inc(v_inv, 1)
                dve.wait_ge(v_inv, GROUPS * b + g + 1)
                dve.tensor_tensor(attn[:, :, g * PACK * DEPTH:(g + 1) * PACK * DEPTH].rearrange("p t (h e) -> p t h e", e=DEPTH),
                                  o[:, :, :, 0:DEPTH],
                                  inv_sum[:, g % 2, :, :].unsqueeze(3).broadcast_to([P, ST, PACK, DEPTH]),
                                  ALU.mult).then_inc(v_on, 1)

            def bias_residual(p):
                dve.wait_ge(s_xr, (p + 1) * 16)
                dve.tensor_tensor(xr[:], xr[:], bo[:].unsqueeze(1).broadcast_to([P, ST, D]), ALU.add).then_inc(v_xr, 1)

            def add_attention(p):
                dve.wait_ge(t_wo, p + 1)
                dve.wait_ge(v_xr, p + 1)
                dve.scalar_tensor_tensor(out=xr[:], in0=ps_m[1][:, :], scalar=tanh_g[:, 0:1], in1=xr[:],
                                         op0=ALU.mult, op1=ALU.add).then_inc(v_x1, 1)
                c = Chain(dve, v_st, 4, p, alone=v_waits)
                dve.wait_ge(v_x1, p + 1)
                for t in range(ST):
                    c.done(dve.bn_stats(stats2[:, t, :], xr[:, t, :]))
                c.wait()
                for t in range(ST):
                    c.done(dve.bn_aggr(mv2[:, t, :], stats2[:, t, :]))
                c.wait()
                c.end()

            def layernorm2(p):
                dve.wait_ge(p_rs2, p + 1)
                after(dve, s_scat, 16 * ST * TOPK * p)
                for t in range(ST):
                    ins = dve.tensor_scalar(xf[:, t, :], xr[:, t, :], mv2[:, t, 0:1], rstd2[:, t:t + 1],
                                            ALU.subtract, ALU.mult)
                ins.then_inc(v_xf, 1)

            def router_max(p):
                dve.wait_ge(t_r, p + 1)
                dve.tensor_reduce(r_negmax[:], ps_m[1][:, 0:ST * E0].rearrange("p (t e) -> p t e", e=E0),
                                  AX, ALU.max, negate=True).then_inc(v_rm, 1)

            router_chain = []

            def router_scores(p):
                c = Chain(dve, v_rc, RC, p, alone=v_waits)
                router_chain[:] = [c]
                dve.wait_ge(a_r, p + 1)
                c.done(dve.reciprocal(r_inv[:], r_sum[:]))
                c.wait()
                c.done(dve.tensor_tensor(scores[:], r_exp[:], r_inv[:].unsqueeze(2).broadcast_to([P, ST, E0]), ALU.mult))
                c.wait()
                c.done(dve.tensor_tensor(biased[:, :, 0:E0], scores[:], gate_b[:].unsqueeze(1).broadcast_to([P, ST, E0]), ALU.add))

            def find_top():
                c = router_chain[0]
                c.wait()
                for t in range(ST):
                    c.done(dve.max(top8[:, t, :], biased[:, t, :]))
                c.wait()
                c.done(dve.memset(top8[:, :, TOPK:8], -HUGE))

            def choose(p):
                c = router_chain[0]
                c.wait()
                for t in range(ST):
                    c.done(dve.match_replace(replaced[:, t, :], top8[:, t, :], biased[:, t, :], HUGE))
                c.wait()
                after(dve, p_seen, ST * p)
                dve.tensor_scalar(chosen[:], replaced[:, :, 0:E0], 0.9 * HUGE, None, ALU.is_ge).then_inc(v_ch, 1)
                c.end()

            def hidden_evac(p, ic):
                n = SI_CHUNKS[ic][1]
                ps = ps_m[ic % 2]
                c = Chain(dve, v_hc, 1, 3 * p + ic)
                dve.wait_ge(a_th, 3 * p + ic + 1)
                c.done(dve.scalar_tensor_tensor(out=silu2[0:n, ic % 2, :], in0=th[0:n, ic % 2, :], scalar=1.0,
                                                in1=ps[0:n, 0:S], op0=ALU.add, op1=ALU.mult))
                c.wait()
                dve.scalar_tensor_tensor(out=hidden[0:n, ic, :], in0=silu2[0:n, ic % 2, :], scalar=0.5,
                                         in1=ps[0:n, S:2 * S], op0=ALU.mult, op1=ALU.mult).then_inc(v_h, 1)

            def add_shared(p):
                dve.wait_ge(t_z, p + 1)
                dve.scalar_tensor_tensor(out=xr[:], in0=ps_m[1][:, :], scalar=tanh_g[:, 2:3], in1=xr[:],
                                         op0=ALU.mult, op1=ALU.add).then_inc(v_z, 1)

            slot_chain = []

            def number_slots(p):
                dve.wait_ge(t_pos, p + 1)
                dve.wait_ge(v_ch, p + 1)
                pos = ps_m[0][:, 0:ST * E0].rearrange("p (t e) -> p t e", e=E0)
                c = Chain(dve, v_pos, PC + ST * TOPK, p, alone=v_waits)
                slot_chain[:] = [c]
                c.done(dve.scalar_tensor_tensor(out=fits[:], in0=pos, scalar=float(CAP0), in1=chosen[:],
                                                op0=ALU.is_le, op1=ALU.mult))
                c.done(dve.tensor_tensor(numbered[:], pos, expert_base[:].unsqueeze(1).broadcast_to([P, ST, E0]), ALU.add))
                c.wait()
                c.done(dve.tensor_tensor(slot_of[:], fits[:], numbered[:], ALU.mult))
                c.wait()
                c.done(dve.scalar_tensor_tensor(out=weight_of[:], in0=slot_of[:], scalar=0.5, in1=scores[:],
                                                op0=ALU.is_ge, op1=ALU.mult))
                for t in range(ST):
                    c.done(dve.max(slot8[:, t, :], slot_of[:, t, :]))
                c.wait()

                c.done(dve.tensor_scalar(no_slot[:], slot8[:], 0.5, BIG_SLOT, ALU.is_lt, ALU.mult))
                c.wait()
                after(dve, s_scat, 16 * ST * TOPK * p)
                c.done(dve.scalar_tensor_tensor(out=slots[:], in0=slot8[:], scalar=-1.0, in1=no_slot[:],
                                                op0=ALU.add, op1=ALU.add))
                c.wait()
                dve.tensor_copy(slots_all[:, bass.ds(p * ST, ST), :], slots[:]).then_inc(v_slot, 1)

            def pick_weights(t):
                for k in range(TOPK):
                    slot_chain[0].done(dve.scalar_tensor_tensor(
                        out=picked[:, t * TOPK + k, :], in0=slot_of[:, t, :], scalar=slot8[:, t, k:k + 1],
                        in1=weight_of[:, t, :], op0=ALU.is_equal, op1=ALU.mult, accum_out=w8[:, t, k:k + 1]))

            def keep_weights(p):
                c = slot_chain[0]
                c.wait()
                c.end()
                dve.tensor_copy(w_all[:, bass.ds(p * ST, ST), 0:TOPK], w8[:, :, 0:TOPK])

            def ffn_at(p, i):
                if p is None:
                    return
                if i == 1:
                    bias_residual(p)
                if i == AT_X1:
                    add_attention(p)
                if i == AT_X1 + 1:
                    layernorm2(p)
                if i == 7:
                    router_max(p)
                if i == 8:
                    hidden_evac(p, 0)
                if i == 9:
                    router_scores(p)
                    hidden_evac(p, 1)
                if i == 10:
                    hidden_evac(p, 2)
                    find_top()
                if i == 11:
                    choose(p)
                if i == 12:
                    add_shared(p)
                if i == 15:
                    number_slots(p)
                if i == 16:
                    pick_weights(0)
                if i == 17:
                    pick_weights(1)
                if i == 18:
                    keep_weights(p)

            def batch(b, u, p, last):
                for i in range(STEPS):
                    if i < HEADS:
                        mask_and_max(b, i)
                    if LAG <= i < HEADS + LAG and (i - LAG) % 2 == 1:
                        probsT_evac(b, i - LAG)
                    if i >= LAG + PACK + 1 and (i - LAG - 1) % PACK == 0:
                        normalise(b, (i - LAG - PACK - 1) // PACK)
                    ffn_at(p, i)
                    if not last:
                        if i == 11:
                            layernorm1(b + 2)
                        if i == 14:
                            layernorm1_apply(b + 2)
                        if i == HEADS + 3:
                            v_evac(b + 2, u)

            for b in range(2):
                layernorm1(b)
                layernorm1_apply(b)
                v_evac(b, b)
            batch(0, 0, None, False)
            batch(1, 1, 0, False)
            with dve.Fori(1, NB // 2 - 1) as half:
                batch(half * 2, 0, half * 2 - 1, False)
                batch(half * 2 + 1, 1, half * 2, False)
            batch(NB - 2, 0, NB - 3, True)
            batch(NB - 1, 1, NB - 2, True)
            for i in range(STEPS):
                ffn_at(NB - 1, i)

        @block.scalar
        def _(act):
            act.wait_ge(s_const, 16 * N_CONST)
            act.activation(tanh_g[:], keep["gates"][:], ACT.Tanh).then_inc(s_tanh, 1)
            act.wait_ge(s_setup, 7)

            def project_evac(b, part):
                if part == 0:
                    act.wait_ge(t_xln, b + 1)
                    act.activation(xlnT[:], ps_m[0][:, :], ACT.Copy).then_inc(a_xln, 1)
                    return
                if part == 1:
                    act.wait_ge(t_q, b + 1)
                    after(act, p_parts, 2 * b)
                    after(act, s_parts, 32 * b)
                    dst, bank, bias, scale, ready, high = q, ps_m[1], bq, DEPTH ** -0.5, a_q, parts["q"]
                else:
                    act.wait_ge(t_k, b + 1)
                    dst, bank, bias, scale, ready, high = kT, ps_m[0], bk, 1.0, a_k, parts["k"]
                for c in range(DC):
                    act.activation(dst[:, c, :], bank[:, c * S:(c + 1) * S], ACT.Identity, bias=bias[:, c:c + 1], scale=scale)
                    ins = act.activation(high[:, 0, c, :], bank[:, c * S:(c + 1) * S], ACT.Identity,
                                         bias=bias[:, c:c + 1], scale=scale)
                ins.then_inc(ready, 1)

            def exponentials(b, i):
                act.wait_ge(v_m, HEADS * b + i + 1)
                after(act, t_t, HEADS * b + i - 3)
                for t in range(ST):
                    ins = act.activation(probs[:, i % 4, t, :], neg_s[:, i % 4, t, :], ACT.Exp,
                                         bias=neg_max[:, i % 4, t:t + 1], scale=-1.0)
                ins.then_inc(a_e, 1)

            def probsT_evac(b, i):
                act.wait_ge(t_t, HEADS * b + i + 1)
                after(act, t_pv, GROUPS * b + i // PACK - 1)
                act.activation(probsT[:, i % (2 * PACK), :, :], ps_t[0][:, :], ACT.Copy).then_inc(te[0], 1)

            def oT_evac(b, g):
                act.wait_ge(t_pv, GROUPS * b + g + 1)
                after(act, t_o, GROUPS * b + g - 1)
                act.activation(oT[:, g % 2, :], ps_o[g % 2][:, 0:S], ACT.Copy).then_inc(a_o, 1)

            def ffn_at(p, i):
                if p is None:
                    return
                if i == 0:
                    act.wait_ge(t_ot, p + 1)
                    act.activation(attnT[:], ps_m[0][:, :], ACT.Copy).then_inc(a_ot, 1)
                if i == 6:
                    act.wait_ge(t_xf, p + 1)
                    act.activation(xfT[:], ps_m[0][:, :], ACT.Copy).then_inc(a_xf, 1)
                if i == 7:
                    act.wait_ge(v_rm, p + 1)
                    for t in range(ST):
                        ins = act.activation(r_exp[:, t, :], ps_m[1][:, t * E0:(t + 1) * E0], ACT.Exp,
                                             bias=r_negmax[:, t:t + 1], accum_out=r_sum[:, t:t + 1])
                    ins.then_inc(a_r, 1)
                if i in (8, 9, 10):
                    ic = i - 8
                    n = SI_CHUNKS[ic][1]
                    act.wait_ge(t_h, 3 * p + ic + 1)
                    act.activation(th[0:n, ic % 2, :], ps_m[ic % 2][0:n, 0:S], ACT.Tanh, scale=0.5).then_inc(a_th, 1)

            def batch(b, p, last):
                for i in range(STEPS):
                    if 1 <= i < HEADS + 1:
                        exponentials(b, i - 1)
                    if LAG <= i < HEADS + LAG and (i - LAG) % 2 == 0:
                        probsT_evac(b, i - LAG)
                    if i >= LAG + PACK and (i - LAG) % PACK == 0:
                        oT_evac(b, (i - LAG - PACK) // PACK)
                    ffn_at(p, i)
                    if not last and 0 <= i - HEADS < 3:
                        project_evac(b + 2, i - HEADS)

            for b in range(2):
                for part in range(3):
                    project_evac(b, part)
            batch(0, None, False)
            batch(1, 0, False)
            with act.Fori(2, NB - 2) as b:
                batch(b, b - 1, False)
            batch(NB - 2, NB - 3, True)
            batch(NB - 1, NB - 2, True)
            for i in range(STEPS):
                ffn_at(NB - 1, i)

        @block.tensor
        def _(pe):
            pe.wait_ge(s_const, 16 * N_CONST)
            pe.wait_ge(s_pc, 8)

            def transposed(dst, src):
                for c in range(DC):
                    for t in range(ST):
                        ins = pe.transpose(dst[:, c * S + t * P:c * S + (t + 1) * P], src[:, t, c * P:(c + 1) * P], ident[:])
                return ins

            def project(b, part):
                if part == 0:
                    pe.wait_ge(v_xln, b + 1)
                    transposed(ps_m[0], xln).then_inc(t_xln, 1)
                if part == 1:
                    pe.wait_ge(a_xln, b + 1)
                    for c in range(DC):
                        for k in range(DC):
                            ins = pe.matmul(ps_m[1][:, c * S:(c + 1) * S], wq[:, k, c * P:(c + 1) * P], xlnT[:, k, :],
                                            start=(k == 0), stop=(k == DC - 1))
                    ins.then_inc(t_q, 1)
                if part == 2:
                    pe.wait_ge(s_ctx, (b + 1) * 16)
                    for c in range(DC):
                        for k in range(DC):
                            ins = pe.matmul(ps_m[0][:, c * S:(c + 1) * S], wk[:, k, c * P:(c + 1) * P], ctxT[:, k, :],
                                            start=(k == 0), stop=(k == DC - 1))
                    ins.then_inc(t_k, 1)
                if part == 3:
                    pe.wait_ge(a_q, b + 1)
                    for t in range(ST):
                        for k in range(DC):
                            ins = pe.matmul(ps_m[1][:, t * D:(t + 1) * D], ctxT[:, k, t * P:(t + 1) * P], wv[:, k, :],
                                            start=(k == 0), stop=(k == DC - 1))
                    ins.then_inc(t_v, 1)

            def head_scores(b, u, i):
                after(pe, v_m, HEADS * b + i - 1)
                for t in range(ST):
                    ins = pe.matmul(ps_s[i % 2][:, t * S:(t + 1) * S], stack["q"][0:STACK, u, i, t * P:(t + 1) * P],
                                    stack["k"][0:STACK, u, i, :], start=True, stop=True)
                ins.then_inc(t_s, 1)

            def head_transpose(b, i):
                pe.wait_ge(a_e, HEADS * b + i + 1)
                after(pe, te[i % 2], HEADS // 2 * b + i // 2)
                for k in range(ST):
                    for t in range(ST):
                        ins = pe.transpose(ps_t[i % 2][:, k * S + t * P:k * S + (t + 1) * P],
                                           probs[:, i % 4, t, k * P:(k + 1) * P], ident[:])
                ins.then_inc(t_t, 1)

            def group_values(b, u, g):
                for parity in range(2):
                    pe.wait_ge(te[parity], HEADS // 2 * b + PACK // 2 * (g + 1))
                if g == 0:
                    pe.wait_ge(v_v, b + 1)
                after(pe, v_on, GROUPS * b + g - 1)
                for k in range(ST):
                    for j in range(PACK):
                        h = g * PACK + j
                        ins = pe.matmul(ps_o[g % 2][j * PAD:(j + 1) * PAD, 0:S], vx[:, u, k, h * PAD:(h + 1) * PAD],
                                        probsT[:, h % (2 * PACK), k, :], start=(k == 0), stop=(k == ST - 1))
                ins.then_inc(t_pv, 1)

            def group_turn(b, g):
                pe.wait_ge(a_o, GROUPS * b + g + 1)
                for t in range(ST):
                    ins = pe.transpose(ps_o[g % 2][:, S + t * P:S + (t + 1) * P], oT[:, g % 2, t * P:(t + 1) * P], ident[:])
                ins.then_inc(t_o, 1)

            def ffn_at(p, i):
                if p is None:
                    return
                if i == 0:
                    pe.wait_ge(v_on, GROUPS * (p + 1))
                    transposed(ps_m[0], attn).then_inc(t_ot, 1)
                if i == 1:
                    pe.wait_ge(a_ot, p + 1)
                    for t in range(ST):
                        for k in range(DC):
                            ins = pe.matmul(ps_m[1][:, t * D:(t + 1) * D], attnT[:, k, t * P:(t + 1) * P], wo[:, k, :],
                                            start=(k == 0), stop=(k == DC - 1))
                    ins.then_inc(t_wo, 1)
                if i == 6:
                    pe.wait_ge(v_xf, p + 1)
                    transposed(ps_m[0], xf).then_inc(t_xf, 1)
                if i == 7:
                    pe.wait_ge(a_xf, p + 1)
                    for t in range(ST):
                        for k in range(DC):
                            ins = pe.matmul(ps_m[1][:, t * E0:(t + 1) * E0], xfT[:, k, t * P:(t + 1) * P], gate_w[:, k, :],
                                            start=(k == 0), stop=(k == DC - 1))
                    ins.then_inc(t_r, 1)
                if i in (8, 9, 10):
                    ic = i - 8
                    o, n = SI_CHUNKS[ic]
                    if ic == 1:
                        pe.wait_ge(a_r, p + 1)
                    if ic == 2:
                        pe.wait_ge(v_h, 3 * p + 1)
                    for j, w in enumerate((ws1, ws3)):
                        for k in range(DC):
                            ins = pe.matmul(ps_m[ic % 2][0:n, j * S:(j + 1) * S], w[:, k, o:o + n], xfT[:, k, :],
                                            start=(k == 0), stop=(k == DC - 1))
                    ins.then_inc(t_h, 1)
                if i == 12:
                    pe.wait_ge(v_h, 3 * p + 3)
                    for t in range(ST):
                        for ic, (o, n) in enumerate(SI_CHUNKS):
                            ins = pe.matmul(ps_m[1][:, t * D:(t + 1) * D], hidden[0:n, ic, t * P:(t + 1) * P],
                                            ws2[0:n, ic, :], start=(ic == 0), stop=(ic == 2))
                    ins.then_inc(t_z, 1)
                if i == 14:
                    pe.wait_ge(v_ch, p + 1)
                    after(pe, p_seen, ST * p)
                    for t in range(ST):
                        o = ps_m[0][:, t * E0:(t + 1) * E0]
                        pe.matmul(o, ones[:], seen[:], start=True, stop=False)
                        if t:
                            pe.matmul(o, ones[:], chosen[:, 0, :], start=False, stop=False)
                        ins = pe.matmul(o, upper[:], chosen[:, t, :], start=False, stop=True)
                    ins.then_inc(t_pos, 1)

            def batch(b, u, p, last):
                made = min(b + 2, NB) if isinstance(b, int) else b + 2
                pe.wait_ge(a_k, made)
                for i in range(STEPS):
                    if i + 1 < HEADS:
                        head_scores(b, u, i + 1)
                    if LAG <= i < HEADS + LAG:
                        head_transpose(b, i - LAG)
                    if i >= LAG + PACK and (i - LAG) % PACK == 0:
                        group_values(b, u, (i - LAG - PACK) // PACK)
                    if i >= LAG + PACK + 1 and (i - LAG - 1) % PACK == 0:
                        group_turn(b, (i - LAG - PACK - 1) // PACK)
                    if i == 1:
                        pe.wait_ge(v_v, made)
                    ffn_at(p, i)
                    if not last and HEADS <= i < HEADS + 4:
                        if i == HEADS and p is not None:
                            pe.wait_ge(v_pos, p * (PC + ST * TOPK) + 2)
                        project(b + 2, i - HEADS)
                if not (isinstance(b, int) and b == NB - 1):
                    pe.wait_ge(s_stack, 16 * 2 * len(PRODUCTS) * (b + 2))
                    head_scores(b + 1, 1 - u, 0)

            for part in range(4):
                project(0, part)
            pe.wait_ge(v_v, 1)
            pe.wait_ge(a_k, 1)
            for part in range(4):
                project(1, part)
            pe.wait_ge(v_v, 2)
            pe.wait_ge(a_k, 2)
            pe.wait_ge(s_stack, 16 * 2 * len(PRODUCTS))
            head_scores(0, 0, 0)
            batch(0, 0, None, False)
            batch(1, 1, 0, False)
            with pe.Fori(1, NB // 2 - 1) as half:
                batch(half * 2, 0, half * 2 - 1, False)
                batch(half * 2 + 1, 1, half * 2, False)
            batch(NB - 2, 0, NB - 3, True)
            batch(NB - 1, 1, NB - 2, True)
            for i in range(STEPS):
                ffn_at(NB - 1, i)


def experts(nc, sb, psum, sem, io, dram, keep, NE):
    RING = 4
    w1, w3 = sb("w1", [P, RING, DC, I0]), sb("w3", [P, RING, DC, I0])
    w2 = sb("w2", [P, RING, 2, D])
    rows = sb("rows", [P, RING, D])
    rowsT = sb("rowsT", [P, 2, DC, P])
    th = sb("th", [P, 2, 2, P])
    silu2 = sb("silu2", [P, 2, 2, P])
    hidden = sb("hidden", [P, 2, 2, P])
    y = sb("y", [P, 2, D])
    ident = keep["ident"]
    ps_t = [psum(f"ps_rows{i}") for i in range(2)]
    ps_h = [psum(f"ps_hid{i}") for i in range(2)]
    ps_y = [psum(f"ps_y{i}") for i in range(2)]

    s_w = [sem(f"b_expert{r}_loaded") for r in range(RING)]
    s_y = [sem(f"b_y{r}_stored") for r in range(2)]
    t_rows, a_rows = sem("b_rowsT_in_psum"), sem("b_rowsT_ready")
    t_h, a_th = sem("b_hidden_in_psum"), sem("b_hidden_tanh")
    v_s, v_h = sem("b_silu_ready"), sem("b_hidden_ready")
    t_y, a_y = sem("b_y_in_psum"), sem("b_y_ready")
    QUADS = (NE - RING) // RING

    def walk(eng, step):
        for e in range(RING + 1):
            step(e, e % RING, e // RING + 1)
        with eng.Fori(1, QUADS) as quad:
            for u in range(RING):
                step(quad * RING + (1 + u), (1 + u) % RING, quad + (2 if u == RING - 1 else 1))
        for e in range(QUADS * RING + 1, NE):
            step(e, e % RING, e // RING + 1)

    with nc.Block() as block:

        @block.sync
        def _(sp):
            def load(e, r):
                if not (isinstance(e, int) and e < RING):
                    sp.wait_ge(t_y, e - (RING - 1))
                for dst, src in ((w1[:, r], io["w1"][e]), (w3[:, r], io["w3"][e])):
                    sp.dma_start(dst, src.rearrange("(c p) n -> p c n", p=P)).then_inc(s_w[r], 16)
                sp.dma_start(w2[:, r, 0, :], io["w2"][e, 0:P]).then_inc(s_w[r], 16)
                sp.dma_start(w2[0:I0 - P, r, 1, :], io["w2"][e, P:I0]).then_inc(s_w[r], 16)
                sp.dma_start(rows[:, r, :], dram["rows"][bass.ds(e * CAP0, CAP0), :] if not isinstance(e, int)
                             else dram["rows"][e * CAP0:(e + 1) * CAP0, :]).then_inc(s_w[r], 16)

            for e in range(RING):
                load(e, e)
            for name, src in (("c_wk", "w_k"), ("c_wv", "w_v"), ("c_wq", "w_q"), ("c_wo", "w_o"), ("router_w", "router_w")):
                sp.dma_start(keep[name][:], io[src].rearrange("(c p) n -> p c n", p=P)).then_inc(keep["s_c_weights"], 16)
            with sp.Fori(1, NE // RING) as turn:
                for r in range(RING):
                    load(turn * RING + r, r)

        @block.tensor
        def _(pe):
            def turn_rows(e, r, n):
                pe.wait_ge(s_w[r], n * 16 * 5)
                after(pe, a_rows, e - 1)
                for c in range(DC):
                    ins = pe.transpose(ps_t[r % 2][:, c * P:(c + 1) * P], rows[:, r, c * P:(c + 1) * P], ident[:])
                ins.then_inc(t_rows, 1)

            def up(e, r):
                pe.wait_ge(a_rows, e + 1)
                after(pe, v_h, e - 1)
                for j, w in enumerate((w1, w3)):
                    for ic, (o, m) in enumerate(I0_CHUNKS):
                        for k in range(DC):
                            col = (2 * j + ic) * P
                            ins = pe.matmul(ps_h[r % 2][0:m, col:col + P], w[:, r, k, o:o + m], rowsT[:, r % 2, k, :],
                                            start=(k == 0), stop=(k == DC - 1))
                ins.then_inc(t_h, 1)

            def down(e, r):
                pe.wait_ge(v_h, e + 1)
                after(pe, a_y, e - 1)
                for ic, (o, m) in enumerate(I0_CHUNKS):
                    ins = pe.matmul(ps_y[r % 2][:, 0:D], hidden[0:m, r % 2, ic, :], w2[0:m, r, ic, :],
                                    start=(ic == 0), stop=(ic == 1))
                ins.then_inc(t_y, 1)

            turn_rows(0, 0, 1)
            up(0, 0)

            def step(e, r, n):
                if isinstance(e, int) and e == 0:
                    return
                turn_rows(e, r, n)
                down(e - 1, (r - 1) % RING)
                up(e, r)
            walk(pe, step)
            down(NE - 1, (NE - 1) % RING)

        @block.scalar
        def _(act):
            def step(e, r, n):
                act.wait_ge(t_rows, e + 1)
                after(act, t_h, e - 1)
                act.activation(rowsT[:, r % 2, :, :], ps_t[r % 2][:, 0:DC * P], ACT.Copy).then_inc(a_rows, 1)
                act.wait_ge(t_h, e + 1)
                after(act, v_h, e - 1)
                act.activation(th[:, r % 2, 0, :], ps_h[r % 2][:, 0:P], ACT.Tanh, scale=0.5)
                m = I0 - P
                act.activation(th[0:m, r % 2, 1, :], ps_h[r % 2][0:m, P:2 * P], ACT.Tanh, scale=0.5).then_inc(a_th, 1)
            walk(act, step)

        @block.vector
        def _(dve):
            def store_y(e, r, n2):
                dve.wait_ge(t_y, e + 1)
                after(dve, s_y[r % 2], n2 * 16)
                dve.tensor_copy(y[:, r % 2, :], ps_y[r % 2][:, 0:D]).then_inc(a_y, 1)

            def step(e, r, n):
                dve.wait_ge(a_th, e + 1)
                after(dve, t_y, e - 1)
                for ic, (o, m) in enumerate(I0_CHUNKS):
                    ins = dve.scalar_tensor_tensor(out=silu2[0:m, r % 2, ic, :], in0=th[0:m, r % 2, ic, :], scalar=1.0,
                                                   in1=ps_h[r % 2][0:m, ic * P:(ic + 1) * P], op0=ALU.add, op1=ALU.mult)
                ins.then_inc(v_s, 1)
                dve.wait_ge(v_s, e + 1)
                for ic, (o, m) in enumerate(I0_CHUNKS):
                    ins = dve.scalar_tensor_tensor(out=hidden[0:m, r % 2, ic, :], in0=silu2[0:m, r % 2, ic, :], scalar=0.5,
                                                   in1=ps_h[r % 2][0:m, (2 + ic) * P:(3 + ic) * P], op0=ALU.mult, op1=ALU.mult)
                ins.then_inc(v_h, 1)

            def step_and_store(e, r, n):
                step(e, r, n)
                if isinstance(e, int):
                    if e > 0:
                        store_y(e - 1, (e - 1) % RING, (e - 1) // 2)
                else:
                    quad = n - (2 if r == 0 else 1)
                    store_y(e - 1, (r - 1) % RING, quad * 2 + ((r - 1) % RING) // 2)
            walk(dve, step_and_store)
            store_y(NE - 1, (NE - 1) % RING, (NE - 1) // 2)

        @block.gpsimd
        def _(pool):
            def store(e, r):
                pool.wait_ge(a_y, e + 1)
                dst = dram["y"][e * CAP0:(e + 1) * CAP0, :] if isinstance(e, int) else dram["y"][bass.ds(e * CAP0, CAP0), :]
                pool.dma_start(dst, y[:, r % 2, :]).then_inc(s_y[r % 2], 16)
            with pool.Fori(0, NE // RING) as quad:
                for r in range(RING):
                    store(quad * RING + r, r)
            for r in range(2):
                pool.wait_ge(s_y[r], 16 * NE // 2)


def attention_and_top(nc, sb, psum, sem, io, dram, keep, NB):
    wq, wk, wv, wo, router_w = (keep[n] for n in ("c_wq", "c_wk", "c_wv", "c_wo", "router_w"))
    minus_half = sb("minus_half", [P, 2])
    x1 = sb("x1", [P, ST, D])
    gathered = sb("gathered", [P, ST * TOPK, D])
    slots = sb("slots", [P, ST, 8], U32)
    w8 = sb("w8", [P, ST, 8])
    x2 = sb("x2", [P, ST, D])
    x2_kept = sb("x2_kept", [P, ST, D])
    stats, mv = sb("stats", [P, ST, 6]), sb("mv", [P, ST, 2])
    var_eps, rstd = sb("var_eps", [P, ST]), sb("rstd", [P, ST])
    xln, xlnT = sb("xln", [P, ST, D]), sb("xlnT", [P, DC, S])
    ctxT = sb("ctxT", [P, DC, S])
    qT, kT = sb("qT", [P, HD // P, S]), sb("kT", [P, HD // P, S])
    v = sb("v", [P, ST, HD])
    RING = 8
    neg_max = sb("neg_max", [P, 4, ST])
    sums, inv = sb("sums", [P, RING, ST]), sb("inv", [P, RING, ST])
    probs = sb("probs", [P, RING, ST, S])
    vs = sb("vs", [P, RING, ST, DK])
    attnT = sb("attnT", [P, HD // P, S])
    x3 = sb("x3", [P, ST, D])
    stats2, mv2 = sb("stats2", [P, ST, 6]), sb("mv2", [P, ST, 2])
    var_eps2, rstd2 = sb("var_eps2", [P, ST]), sb("rstd2", [P, ST])
    xn, xnT = sb("xn", [P, ST, D]), sb("xnT", [P, DC, S])
    r_negmax, r_exp = sb("r_negmax", [P, ST]), sb("r_exp", [P, ST, E1])
    r_sum, r_inv = sb("r_sum", [P, ST]), sb("r_inv", [P, ST])
    ident, tanh_g, slots_all, w_all = keep["ident"], keep["tanh_g"], keep["slots_all"], keep["w_all"]
    gate_all = keep["gate_all"]

    ps_s = [psum(f"ps_c_s{i}") for i in range(4)]
    ps_o = [psum(f"ps_c_o{i}") for i in range(2)]
    ps_m = [psum(f"ps_c_m{i}") for i in range(2)]

    s_x, s_ctx = sem("c_x1_loaded"), sem("c_ctx_loaded")
    s_x3, s_xn = sem("c_x3_stored"), sem("c_x3n_stored")
    s_gat = sem("c_rows_gathered")
    p_const, v_const = sem("c_pool_consts"), sem("c_vector_consts")
    v_waits, p_waits = sem("c_vector_waits"), sem("c_pool_waits")
    v_sl, v_add, v_comb = sem("c_slots_copied"), sem("c_rows_chain"), sem("c_x2_ready")
    v_ln, p_rs, p_rsc, v_xln = sem("c_ln_chain"), sem("c_rstd"), sem("c_rstd_chain"), sem("c_xln_ready")
    t_fill = sem("c_fill_in_psum")
    ev = [sem("c_even_fill_ready"), sem("c_odd_fill_ready")]
    t_s, v_m, a_e = sem("c_scores_in_psum"), sem("c_max_ready"), sem("c_probs_ready")
    v_inv, v_vs = sem("c_inv_sums"), sem("c_v_scaled")
    t_pv = sem("c_pv_done")
    ot = [sem("c_attnT_even_ready"), sem("c_attnT_odd_ready")]
    p_x2 = sem("c_x2_kept")
    v_st, p_rs2, p_rs2c, v_xn = sem("c_ln2_chain"), sem("c_rstd2"), sem("c_rstd2_chain"), sem("c_xn_ready")
    v_rm, v_ri, v_gate = (sem(f"c_router_{n}") for n in ("max", "inv", "scores"))

    PAIRS = HEADS // 2
    STEPS = HEADS + 3
    FILLS = 16
    F_XNT, F_ROUTER = 0, 1
    F_K, F_V = 2, 6
    F_XLNT, F_WO, F_Q = 10, 11, 12

    def present(b, n):
        if n in (F_XNT, F_ROUTER):
            return b > 0
        return 0 <= b < NB if n == F_WO else b < NB - 1

    upto = Fills(FILLS, present).upto

    def empty(n, copy):
        bank = ps_m[n % 2]
        src = bank[:, :].rearrange("p (c s) -> p c s", c=2)
        if n < F_V:
            return copy(kT[:, 2 * (n - F_K):2 * (n - F_K) + 2, :], src, 1.0)
        if n < F_XLNT:
            return copy(v[:, (n - F_V) // 2, (n % 2) * 512:(n % 2 + 1) * 512], bank[:, :], 1.0)
        return copy(qT[:, 2 * (n - F_Q):2 * (n - F_Q) + 2, :], src, DK ** -0.5)

    with nc.Block() as block:

        @block.sync
        def _(sp):
            sp.dma_start(ctxT[:], tiles(io["ctxT"][0])).then_inc(s_ctx, 16)
            sp.dma_start(x1[:], tiles(dram["x1"][0])).then_inc(s_x, 16)
            for e in range(E1):
                sp.dma_start(keep["f1"][:, e], io["f1"][e].rearrange("(c p) n -> p c n", p=P)).then_inc(keep["s_f1"], 16)

            def loads(b):
                sp.wait_ge(v_comb, b + 1)
                sp.dma_start(x1[:], tiles(dram["x1"][b + 1])).then_inc(s_x, 16)
                sp.wait_ge(t_fill, upto(b - 1, F_V + 3))
                sp.dma_start(ctxT[:], tiles(io["ctxT"][b + 1])).then_inc(s_ctx, 16)

            def stores(p):
                sp.wait_ge(ev[1], upto(p, F_WO, 1))
                sp.dma_start(tiles(dram["x3"][p]), x3[:]).then_inc(s_x3, 16)
                sp.wait_ge(v_xn, p + 1)
                sp.dma_start(tiles(dram["x3n"][p]), xn[:]).then_inc(s_xn, 16)

            loads(0)
            loads(1)
            stores(0)
            with sp.Fori(2, NB - 1) as b:
                loads(b)
                stores(b - 1)
            stores(NB - 2)
            stores(NB - 1)
            sp.wait_ge(s_x3, 16 * NB)
            sp.wait_ge(s_xn, 16 * NB)
            sp.wait_ge(keep["s_f1"], 16 * E1)

        @block.gpsimd
        def _(pool):
            pool.memset(minus_half[:], -0.5).then_inc(p_const, 1)
            pool.memset(gathered[:], 0.0).then_inc(p_const, 1)
            pool.wait_ge(p_const, 2)

            def rsqrt(b, mv_, var_eps_, rstd_, chain, stats_done, ready):
                after(pool, stats_done, (b + 1) * 4, alone=p_waits)
                pool.tensor_scalar(var_eps_[:], mv_[:, :, 1], EPS, None, ALU.add).then_inc(chain, 1)
                pool.wait_ge(chain, b + 1)
                pool.tensor_tensor(rstd_[:], var_eps_[:], minus_half[:], ALU.pow).then_inc(ready, 1)

            def gather(b):
                after(pool, v_comb, b, alone=p_waits)
                after(pool, v_sl, b + 1, alone=p_waits)
                for t in range(ST):
                    for k in range(TOPK):
                        pool.indirect_dma_start(
                            out=gathered[:, t * TOPK + k, :], out_offset=None, in_=dram["y"],
                            in_offset=bass.IndirectOffsetOnAxis(ap=slots[:, t, k:k + 1], axis=0),
                            bounds_check=E0 * CAP0 - 1, oob_is_err=False).then_inc(s_gat, 16)

            def keep_x2(b):
                after(pool, v_comb, b + 1, alone=p_waits)
                if not (isinstance(b, int) and b == 0):
                    after(pool, ev[1], upto(b - 1, F_WO, 1), alone=p_waits)
                pool.tensor_copy(x2_kept[:], x2[:]).then_inc(p_x2, 1)

            def batch(b, p, last):
                keep_x2(b)
                if p is not None:
                    rsqrt(p, mv2, var_eps2, rstd2, p_rs2c, v_st, p_rs2)
                if not last:
                    gather(b + 1)
                    rsqrt(b + 1, mv, var_eps, rstd, p_rsc, v_ln, p_rs)

            gather(0)
            rsqrt(0, mv, var_eps, rstd, p_rsc, v_ln, p_rs)
            batch(0, None, False)
            batch(1, 0, False)
            with pool.Fori(2, NB - 1) as b:
                batch(b, b - 1, False)
            batch(NB - 1, NB - 2, True)
            rsqrt(NB - 1, mv2, var_eps2, rstd2, p_rs2c, v_st, p_rs2)

        @block.vector
        def _(dve):
            def take_slots(b):
                after(dve, s_gat, 16 * ST * TOPK * b)
                dve.tensor_copy(slots[:], slots_all[:, bass.ds(b * ST, ST), :] if not isinstance(b, int)
                                else slots_all[:, b * ST:(b + 1) * ST, :])
                dve.tensor_scalar(w8[:, :, 0:TOPK], w_all[:, bass.ds(b * ST, ST), 0:TOPK] if not isinstance(b, int)
                                  else w_all[:, b * ST:(b + 1) * ST, 0:TOPK], tanh_g[:, 2:3], None, ALU.mult).then_inc(v_sl, 1)

            def combine(b, k):
                if k == 0:
                    dve.wait_ge(s_x, 16 * (b + 1))
                    dve.wait_ge(s_gat, 16 * ST * TOPK * (b + 1))
                    dve.wait_ge(v_sl, b + 1)
                    after(dve, p_x2, b)
                else:
                    dve.wait_ge(v_add, ST * (TOPK - 1) * b + ST * k)
                for t in range(ST):
                    ins = dve.scalar_tensor_tensor(out=x2[:, t, :], in0=gathered[:, t * TOPK + k, :],
                                                   scalar=w8[:, t, k:k + 1], in1=(x2 if k else x1)[:, t, :],
                                                   op0=ALU.mult, op1=ALU.add)
                    if k < TOPK - 1:
                        ins.then_inc(v_add, 1)
                if k == TOPK - 1:
                    ins.then_inc(v_comb, 1)

            def statistics(b, src, stats_, mv_, chain_sem, ready, value):
                c = Chain(dve, chain_sem, 4, b, alone=v_waits)
                dve.wait_ge(ready, value)
                for t in range(ST):
                    c.done(dve.bn_stats(stats_[:, t, :], src[:, t, :]))
                c.wait()
                for t in range(ST):
                    c.done(dve.bn_aggr(mv_[:, t, :], stats_[:, t, :]))
                c.wait()
                c.end()

            def layernorm1(b):
                dve.wait_ge(p_rs, b + 1)
                after(dve, t_fill, upto(b - 2, F_XLNT) if not (isinstance(b, int) and b == 0) else 0)
                for t in range(ST):
                    ins = dve.tensor_scalar(xln[:, t, :], x2[:, t, :], mv[:, t, 0:1], rstd[:, t:t + 1],
                                            ALU.subtract, ALU.mult)
                ins.then_inc(v_xln, 1)

            def layernorm2(p):
                dve.wait_ge(p_rs2, p + 1)
                after(dve, s_xn, 16 * p)
                for t in range(ST):
                    ins = dve.tensor_scalar(xn[:, t, :], x3[:, t, :], mv2[:, t, 0:1], rstd2[:, t:t + 1],
                                            ALU.subtract, ALU.mult)
                ins.then_inc(v_xn, 1)

            def fill_evac(b, n):
                dve.wait_ge(t_fill, upto(b, n))
                empty(n, lambda dst, src, scale: dve.tensor_scalar(dst, src, scale, None, ALU.mult) if scale != 1.0
                      else dve.tensor_copy(dst, src)).then_inc(ev[1], 1)

            def head_max(b, i):
                dve.wait_ge(t_s, HEADS * b + i + 1)
                dve.tensor_reduce(neg_max[:, i % 4, :], ps_s[i % 4][:, :].rearrange("p (k s) -> p k s", k=ST),
                                  AX, ALU.max, negate=True).then_inc(v_m, 1)

            def scale_v(b, i):
                dve.wait_ge(a_e, HEADS * b + i + 1)
                dve.reciprocal(inv[:, i % RING, :], sums[:, i % RING, :]).then_inc(v_inv, 1)
                dve.wait_ge(v_inv, HEADS * b + i + 1)
                after(dve, t_pv, PAIRS * b + (i - RING) // 2 + 1)
                dve.tensor_tensor(vs[:, i % RING, :, :], v[:, :, i * DK:(i + 1) * DK],
                                  inv[:, i % RING, :].unsqueeze(2).broadcast_to([P, ST, DK]), ALU.mult).then_inc(v_vs, 1)

            def attnT_evac(b, c):
                dve.wait_ge(t_pv, PAIRS * b + c + 1)
                dve.tensor_copy(attnT[:, c, :], ps_o[1][:, 0:S]).then_inc(ot[1], 1)

            def add_attention(b):
                dve.wait_ge(t_fill, upto(b, F_WO))
                dve.wait_ge(p_x2, b + 1)
                after(dve, s_x3, 16 * b)
                dve.scalar_tensor_tensor(out=x3[:], in0=ps_m[1][:, :], scalar=tanh_g[:, 1:2], in1=x2_kept[:],
                                         op0=ALU.mult, op1=ALU.add).then_inc(ev[1], 1)
                statistics(b, x3, stats2, mv2, v_st, ev[1], upto(b, F_WO, 1))

            def tail_at(p, i):
                if p is None:
                    return
                if i == 1:
                    layernorm2(p)
                if i == 8:
                    dve.wait_ge(t_fill, upto(p + 1, F_ROUTER))
                    dve.tensor_reduce(r_negmax[:], ps_m[1][:, 0:ST * E1].rearrange("p (t e) -> p t e", e=E1),
                                      AX, ALU.max, negate=True).then_inc(v_rm, 1)
                if i == 10:
                    dve.wait_ge(ev[1], upto(p + 1, F_ROUTER, 1))
                    dve.reciprocal(r_inv[:], r_sum[:]).then_inc(v_ri, 1)
                    dve.wait_ge(v_ri, p + 1)
                    for t in range(ST):
                        dst = gate_all[:, t, p * E1:(p + 1) * E1] if isinstance(p, int) else gate_all[:, t, bass.ds(p * E1, E1)]
                        ins = dve.tensor_scalar(dst, r_exp[:, t, :], r_inv[:, t:t + 1], None, ALU.mult)
                    ins.then_inc(v_gate, 1)

            def batch(b, p, last):
                for i in range(STEPS):
                    if i < HEADS:
                        head_max(b, i)
                    if 1 <= i < HEADS + 1:
                        scale_v(b, i - 1)
                    if i >= 7 and i % 4 == 3:
                        attnT_evac(b, (i - 5) // 2)
                    tail_at(p, i)
                    if not last:
                        if i == 0:
                            take_slots(b + 1)
                        if i >= HEADS:
                            fill_evac(b, F_K + 1 + 2 * (i - HEADS))
                        if 12 <= i < 12 + TOPK:
                            combine(b + 1, i - 12)
                if not last:
                    statistics(b + 1, x2, stats, mv, v_ln, v_comb, b + 2)
                attnT_evac(b, PAIRS - 1)
                if not last:
                    layernorm1(b + 1)
                    fill_evac(b, F_V + 3)
                add_attention(b)
                if not last:
                    fill_evac(b, F_Q + 1)
                    fill_evac(b, F_Q + 3)

            dve.wait_ge(p_const, 2)
            take_slots(0)
            for n in range(F_K + 1, F_V + 4, 2):
                fill_evac(-1, n)
            for k in range(TOPK):
                combine(0, k)
            statistics(0, x2, stats, mv, v_ln, v_comb, 1)
            layernorm1(0)
            fill_evac(-1, F_Q + 1)
            fill_evac(-1, F_Q + 3)
            batch(0, None, False)
            batch(1, 0, False)
            with dve.Fori(2, NB - 1) as b:
                batch(b, b - 1, False)
            batch(NB - 1, NB - 2, True)
            for i in range(STEPS):
                tail_at(NB - 1, i)

        @block.scalar
        def _(act):
            def fill_evac(b, n):
                act.wait_ge(t_fill, upto(b, n))
                if n == F_XNT:
                    ins = act.activation(xnT[:], ps_m[0][:, :], ACT.Copy)
                elif n == F_XLNT:
                    ins = act.activation(xlnT[:], ps_m[0][:, :], ACT.Copy)
                else:
                    if n == F_V:
                        after(act, v_vs, HEADS * (b + 1))
                    ins = empty(n, lambda dst, src, scale: act.activation(dst, src, ACT.Copy, scale=scale))
                ins.then_inc(ev[0], 1)

            def exponentials(b, i):
                act.wait_ge(v_m, HEADS * b + i + 1)
                after(act, t_pv, PAIRS * b + (i - RING) // 2 + 1)
                for k in range(ST):
                    ins = act.activation(probs[:, i % RING, k, :], ps_s[i % 4][:, k * S:(k + 1) * S], ACT.Exp,
                                         bias=neg_max[:, i % 4, k:k + 1], accum_out=sums[:, i % RING, k:k + 1])
                ins.then_inc(a_e, 1)

            def tail_at(p, i):
                if p is None:
                    return
                if i == 4:
                    fill_evac(p + 1, F_XNT)
                if i == 8:
                    act.wait_ge(v_rm, p + 1)
                    after(act, v_gate, p)
                    for t in range(ST):
                        ins = act.activation(r_exp[:, t, :], ps_m[1][:, t * E1:(t + 1) * E1], ACT.Exp,
                                             bias=r_negmax[:, t:t + 1], accum_out=r_sum[:, t:t + 1])
                    ins.then_inc(ev[1], 1)

            def batch(b, p, last):
                for i in range(STEPS):
                    if i < HEADS:
                        exponentials(b, i)
                    if i >= 5 and i % 4 == 1:
                        c = (i - 5) // 2
                        act.wait_ge(t_pv, PAIRS * b + c + 1)
                        act.activation(attnT[:, c, :], ps_o[0][:, 0:S], ACT.Copy).then_inc(ot[0], 1)
                    tail_at(p, i)
                    if not last and i >= HEADS:
                        fill_evac(b, F_K + 2 * (i - HEADS))
                if not last:
                    for n in (F_V + 2, F_XLNT, F_Q, F_Q + 2):
                        fill_evac(b, n)

            for n in (*range(F_K, F_V + 4, 2), F_XLNT, F_Q, F_Q + 2):
                fill_evac(-1, n)
            batch(0, None, False)
            batch(1, 0, False)
            with act.Fori(2, NB - 1) as b:
                batch(b, b - 1, False)
            batch(NB - 1, NB - 2, True)
            for i in range(STEPS):
                tail_at(NB - 1, i)

        @block.tensor
        def _(pe):
            pe.wait_ge(keep["s_c_weights"], 16 * 5)

            def transposed(dst, src):
                for c in range(DC):
                    for t in range(ST):
                        ins = pe.transpose(dst[:, c * S + t * P:c * S + (t + 1) * P], src[:, t, c * P:(c + 1) * P], ident[:])
                return ins

            def fill(b, n):
                after(pe, ev[n % 2], upto(b, n, n % 2) - 1)
                bank = ps_m[n % 2]
                if n == F_XNT:
                    pe.wait_ge(v_xn, b)
                    ins = transposed(bank, xn)
                elif n == F_ROUTER:
                    pe.wait_ge(ev[0], upto(b, F_XNT, 0))
                    for t in range(ST):
                        for k in range(DC):
                            ins = pe.matmul(bank[:, t * E1:(t + 1) * E1], xnT[:, k, t * P:(t + 1) * P], router_w[:, k, :],
                                            start=(k == 0), stop=(k == DC - 1))
                elif n == F_XLNT:
                    pe.wait_ge(v_xln, b + 2)
                    ins = transposed(bank, xln)
                elif n == F_WO:
                    for j in range(2):
                        pe.wait_ge(ot[j], PAIRS // 2 * (b + 1))
                    for t in range(ST):
                        for c in range(HD // P):
                            ins = pe.matmul(bank[:, t * D:(t + 1) * D], attnT[:, c, t * P:(t + 1) * P], wo[:, c, :],
                                            start=(c == 0), stop=(c == HD // P - 1))
                elif F_V <= n < F_XLNT:
                    t, half = (n - F_V) // 2, n % 2
                    for k in range(DC):
                        ins = pe.matmul(bank[:, :], ctxT[:, k, t * P:(t + 1) * P], wv[:, k, half * 512:(half + 1) * 512],
                                        start=(k == 0), stop=(k == DC - 1))
                else:
                    w, x, first = (wq, xlnT, F_Q) if n >= F_Q else (wk, ctxT, F_K)
                    if n == F_Q:
                        pe.wait_ge(ev[0], upto(b, F_XLNT, 0))
                    if n == F_K:
                        pe.wait_ge(s_ctx, 16 * (b + 2))
                    for j in range(2):
                        c = 2 * (n - first) + j
                        for k in range(DC):
                            ins = pe.matmul(bank[:, j * S:(j + 1) * S], w[:, k, c * P:(c + 1) * P], x[:, k, :],
                                            start=(k == 0), stop=(k == DC - 1))
                ins.then_inc(t_fill, 1)

            def head_scores(b, i):
                c, r = i // 2, DK * (i % 2)
                if i % 4 == 0:
                    n = i // 4
                    for first in (F_K, F_Q):
                        pe.wait_ge(ev[n % 2], upto(b - 1, first + n, n % 2))
                after(pe, a_e, HEADS * b + i - 3)
                for k in range(ST):
                    ins = pe.matmul(ps_s[i % 4][:, k * S:(k + 1) * S], kT[r:r + DK, c, k * P:(k + 1) * P],
                                    qT[r:r + DK, c, :], start=True, stop=True)
                ins.then_inc(t_s, 1)

            def pair_values(b, c):
                pe.wait_ge(v_vs, HEADS * b + 2 * c + 2)
                after(pe, ot[c % 2], PAIRS // 2 * b + c // 2)
                for k in range(ST):
                    for j in range(2):
                        i = 2 * c + j
                        ins = pe.matmul(ps_o[c % 2][j * DK:(j + 1) * DK, 0:S], vs[:, i % RING, k, :], probs[:, i % RING, k, :],
                                        start=(k == 0), stop=(k == ST - 1))
                ins.then_inc(t_pv, 1)

            def batch(b, p, last):
                for i in range(STEPS):
                    if i < HEADS:
                        head_scores(b, i)
                    if p is not None and i == 4:
                        fill(b, F_XNT)
                    if p is not None and i == 8:
                        fill(b, F_ROUTER)
                    if not last and i >= HEADS:
                        fill(b, F_K + 2 * (i - HEADS))
                        fill(b, F_K + 2 * (i - HEADS) + 1)
                    if i >= 4 and i % 2 == 0:
                        pair_values(b, (i - 4) // 2)
                if not last:
                    for n in (F_V + 2, F_V + 3, F_XLNT):
                        fill(b, n)
                fill(b, F_WO)
                if not last:
                    for n in range(F_Q, F_Q + 4):
                        fill(b, n)

            for n in (*range(F_K, F_WO), *range(F_Q, F_Q + 4)):
                fill(-1, n)
            batch(0, None, False)
            batch(1, 0, False)
            with pe.Fori(2, NB - 1) as b:
                batch(b, b - 1, False)
            batch(NB - 1, NB - 2, True)
            fill(NB, F_XNT)
            fill(NB, F_ROUTER)


def choose_tokens(nc, sb, psum, sem, io, dram, keep, NB):
    rows_of = [(o, min(P, NB * E1 - o)) for o in range(0, NB * E1, P)]
    NT = len(rows_of)
    WIDE = S + 8
    work = sb("work", [P, NT, WIDE])
    top8 = sb("top8", [P, NT, 8])
    ones = sb("ones", [P, S])
    chosen, counted, place = (sb(n, [P, NT, S]) for n in ("chosen", "counted", "place"))
    gate_all, pos_all, ident = keep["gate_all"], keep["pos_all"], keep["ident"]
    ps = [psum(f"ps_e{i}") for i in range(2)]
    t_sc, v_ch, t_pos, v_pos = sem("e_scores_in_psum"), sem("e_chain"), sem("e_places_in_psum"), sem("e_places_ready")
    v_done = sem("e_places_turned")

    with nc.Block() as block:

        @block.tensor
        def _(pe):
            for i, (o, n) in enumerate(rows_of):
                for t in range(ST):
                    ins = pe.transpose(ps[0][0:n, i * S + t * P:i * S + (t + 1) * P], gate_all[:, t, o:o + n], ident[:])
            ins.then_inc(t_sc, 1)
            pe.wait_ge(v_pos, 1)
            for i, (o, n) in enumerate(rows_of):
                for t in range(ST):
                    ins = pe.transpose(ps[1][:, t * NB * E1 + o:t * NB * E1 + o + n], place[0:n, i, t * P:(t + 1) * P],
                                       ident[0:n, 0:n])
            ins.then_inc(t_pos, 1)

        @block.vector
        def _(dve):
            c = Chain(dve, v_ch, 0, 0)
            c.done(dve.memset(ones[:], 1.0))
            c.done(dve.memset(work[:, :, S:WIDE], -1.0))
            dve.wait_ge(t_sc, 1)
            for i, (o, n) in enumerate(rows_of):
                c.done(dve.tensor_copy(work[0:n, i, 0:S], ps[0][0:n, i * S:(i + 1) * S]))
            c.wait()
            for turn in range((CAP1 + 7) // 8):
                take = min(8, CAP1 - 8 * turn)
                for i, (o, n) in enumerate(rows_of):
                    c.done(dve.max(top8[0:n, i, :], work[0:n, i, :]))
                c.wait()
                if take < 8:
                    c.done(dve.memset(top8[:, :, take:8], -1.0))
                    c.wait()
                for i, (o, n) in enumerate(rows_of):
                    c.done(dve.match_replace(work[0:n, i, :], top8[0:n, i, :], work[0:n, i, :], -2.0))
                c.wait()
            for i, (o, n) in enumerate(rows_of):
                c.done(dve.tensor_scalar(chosen[0:n, i, :], work[0:n, i, 0:S], -1.5, None, ALU.is_lt))
            c.wait()
            for i, (o, n) in enumerate(rows_of):
                c.done(dve.tensor_tensor_scan(counted[0:n, i, :], ones[0:n, :], chosen[0:n, i, :], 0.0, ALU.mult, ALU.add))
            c.wait()
            for i, (o, n) in enumerate(rows_of):
                c.done(dve.tensor_tensor(place[0:n, i, :], counted[0:n, i, :], chosen[0:n, i, :], ALU.mult))
            c.wait()
            dve.tensor_copy(ones[:, 0:1], ones[:, 1:2]).then_inc(v_pos, 1)
            dve.wait_ge(t_pos, 1)
            dve.tensor_copy(pos_all[:, :, 0:NB * E1],
                            ps[1][:, 0:ST * NB * E1].rearrange("p (t e) -> p t e", t=ST)).then_inc(v_done, 1)


def expert_choice(nc, sb, psum, sem, io, out, dram, keep, NB):
    f1 = keep["f1"]
    NQ = NB // 2
    f2 = sb("f2", [P, E1, HC, D])
    b1, b2 = sb("b1", [P, E1, HC]), sb("b2", [P, E1, DC])
    slot_id = sb("slot_id", [P, CAP1])
    xn, x3 = sb("xn", [P, 2 * ST, D]), sb("x3", [P, 2 * ST, D])
    sel, gated = sb("sel", [P, 2 * ST, SLOTS]), sb("gated", [P, 2 * ST, SLOTS])
    tokT = sb("tokT", [P, DC, 2, SLOTS])
    gatedT = sb("gatedT", [GS, 2, GC, S])
    hid = sb("hid", [P, 2, HC, 2 * CAP1])
    yT = sb("yT", [P, DC, 2, SLOTS])
    y = sb("y", [GS, 2, GC, D])
    ident, tanh_g, gate_all, pos_all = keep["ident"], keep["tanh_g"], keep["gate_all"], keep["pos_all"]

    ps_h = [psum(f"ps_d_h{i}") for i in range(4)]
    ps_y = [psum(f"ps_d_y{i}") for i in range(2)]
    ps_m = [psum(f"ps_d_m{i}") for i in range(2)]

    s_f2 = [sem(f"d_f2_{e % 2}_loaded") for e in range(2)]
    s_const, s_xn, s_x3, s_out = sem("d_const_loaded"), sem("d_xn_loaded"), sem("d_x3_loaded"), sem("d_out_stored")
    p_const = sem("d_pool_const")
    p_waits = sem("d_pool_waits")
    v_sel, p_gated = sem("d_sel_ready"), sem("d_gated_ready")
    t_fill = sem("d_fill_in_psum")
    ev = [sem("d_even_fill_ready"), sem("d_odd_fill_ready")]
    t_h, a_h = sem("d_hidden_in_psum"), sem("d_hidden_ready")
    t_y, v_y = sem("d_yT_in_psum"), sem("d_yT_ready")

    HALF = SLOTS // 2
    N2 = 2 * CAP1
    UNITS = [(0, 3), (3, 3), (6, 2)]
    UPE = len(UNITS)

    FILLS = 20
    TOKENS = {1: (1, 0, 0), 2: (1, 0, 1), 4: (1, 1, 0), 6: (1, 1, 1),
              10: (0, 0, 0), 12: (0, 0, 1), 14: (0, 1, 0), 15: (0, 1, 1)}
    GATES = {7: (0, 0), 8: (0, 1), 9: (1, 0), 16: (1, 1), 17: (2, 0)}
    RESULTS = {11: (0, 0), 13: (0, 1), 18: (1, 0), 19: (1, 1), 0: (2, 0)}
    SUMS = {3: 0, 5: 1}
    OLD = (0, 3, 5)
    NEW = (10, 12, 14, 15)

    def present(q, n):
        if n in OLD:
            return q > 0
        return (q < NQ - 1) if n in NEW else (0 <= q < NQ)

    upto = Fills(FILLS, present).upto

    def chunks(g, u):
        return [(u, 2 * g), (u, 2 * g + 1)] if g < 2 else [(0, GC - 1), (1, GC - 1)]

    def part(buf, g, u):
        return buf[:, u, 2 * g:2 * g + 2, :] if g < 2 else buf[:, :, GC - 1, :]

    def dyn(ap, i, q):
        t, u = i % ST, i // ST
        return ap[:, t, bass.ds(q * (2 * E1) + u * E1, E1)] if not isinstance(q, int) \
            else ap[:, t, (2 * q + u) * E1:(2 * q + u + 1) * E1]

    def pair_of(ap, q):
        v_ = ap.rearrange("b (t p) d -> p (b t) d", p=P)
        return v_[:, q * 2 * ST:(q + 1) * 2 * ST, :] if isinstance(q, int) else v_[:, bass.ds(q * (2 * ST), 2 * ST), :]

    def empty(n, copy):
        bank = ps_m[n % 2]
        if n in TOKENS:
            half, u, c = TOKENS[n]
            return copy(tokT[:, c, u, half * HALF:(half + 1) * HALF], bank[:, 0:HALF])
        g, u = GATES[n] if n in GATES else RESULTS[n]
        return copy(part(gatedT if n in GATES else y, g, u), bank[0:GS, :].rearrange("p (c s) -> p c s", c=2))

    with nc.Block() as block:

        @block.sync
        def _(sp):
            sp.dma_start(xn[:], pair_of(dram["x3n"], 0)).then_inc(s_xn, 16)
            sp.dma_start(x3[:], pair_of(dram["x3"], 0)).then_inc(s_x3, 16)
            sp.dma_start(b1[:], io["fb1"].rearrange("e (c p) -> p e c", p=P), allow_slow_non_contiguous=True).then_inc(s_const, 16)
            sp.dma_start(b2[:], io["fb2"].rearrange("e (c p) -> p e c", p=P), allow_slow_non_contiguous=True).then_inc(s_const, 16)
            for e in range(E1):
                if e >= 2:
                    sp.wait_ge(s_f2[e % 2], 16 * (e // 2))
                sp.dma_start(f2[:, e], io["f2"][e].rearrange("(c p) n -> p c n", p=P)).then_inc(s_f2[e % 2], 16)

            def load_xn(q):
                sp.wait_ge(t_fill, upto(q - 1, 6))
                sp.dma_start(xn[:], pair_of(dram["x3n"], q)).then_inc(s_xn, 16)

            def store(p):
                sp.wait_ge(ev[1], upto(p + 1, 5, 1))
                sp.dma_start(pair_of(out, p), x3[:]).then_inc(s_out, 16)
                sp.wait_ge(s_out, 16 * (p + 1))

            def load_x3(q):
                sp.dma_start(x3[:], pair_of(dram["x3"], q)).then_inc(s_x3, 16)

            load_xn(1)
            with sp.Fori(1, NQ - 1) as q:
                store(q - 1)
                load_x3(q)
                load_xn(q + 1)
            store(NQ - 2)
            load_x3(NQ - 1)
            store(NQ - 1)

        @block.gpsimd
        def _(pool):
            pool.iota(slot_id[:], [[1, CAP1]], base=1, channel_multiplier=0,
                      allow_small_or_imprecise_dtypes=True).then_inc(p_const, 1)

            def gate(q):
                after(pool, v_sel, q + 1, alone=p_waits)
                after(pool, t_fill, upto(q - 1, 17), alone=p_waits)
                for i in range(2 * ST):
                    ins = pool.tensor_tensor(gated[:, i, :].rearrange("p (e c) -> p e c", c=CAP1),
                                             sel[:, i, :].rearrange("p (e c) -> p e c", c=CAP1),
                                             dyn(gate_all, i, q).unsqueeze(2).broadcast_to([P, E1, CAP1]), ALU.mult)
                ins.then_inc(p_gated, 1)

            pool.wait_ge(v_sel, 1)
            gate(0)
            gate(1)
            with pool.Fori(2, NQ) as q:
                gate(q)

        @block.vector
        def _(dve):
            dve.wait_ge(p_const, 1)
            dve.wait_ge(s_const, 32)

            def select(q):
                after(dve, t_fill, upto(q - 1, 6) if not (isinstance(q, int) and q == 0) else 0)
                after(dve, p_gated, q)
                for i in range(2 * ST):
                    ins = dve.tensor_tensor(sel[:, i, :].rearrange("p (e c) -> p e c", c=CAP1),
                                            slot_id[:].unsqueeze(1).broadcast_to([P, E1, CAP1]),
                                            dyn(pos_all, i, q).unsqueeze(2).broadcast_to([P, E1, CAP1]), ALU.is_equal)
                ins.then_inc(v_sel, 1)

            def fill_evac(q, n):
                dve.wait_ge(t_fill, upto(q, n))
                if n in SUMS:
                    u = SUMS[n]
                    if u == 0:
                        dve.wait_ge(s_x3, 16 * q)
                    ins = dve.scalar_tensor_tensor(out=x3[:, u * ST:(u + 1) * ST, :], in0=ps_m[1][:, :], scalar=tanh_g[:, 3:4],
                                                   in1=x3[:, u * ST:(u + 1) * ST, :], op0=ALU.mult, op1=ALU.add)
                else:
                    ins = empty(n, dve.tensor_copy)
                ins.then_inc(ev[1], 1)

            def yT_evac(q, e):
                dve.wait_ge(t_y, E1 * q + e + 1)
                for c in range(DC):
                    ins = dve.tensor_scalar(yT[:, c, :, e * CAP1:(e + 1) * CAP1],
                                            ps_y[e % 2][:, c * N2:(c + 1) * N2].rearrange("p (u s) -> p u s", u=2),
                                            b2[:, e, c:c + 1], None, ALU.add)
                ins.then_inc(v_y, 1)

            def pair(q, first, last):
                for s in range(E1 + 1):
                    n = 2 * s + 1
                    if not (first and n in OLD) and not (last and n in NEW):
                        fill_evac(q, n)
                    if s == 3 and not last:
                        select(q + 1)
                    if s > 0:
                        yT_evac(q, s - 1)
                fill_evac(q, FILLS - 1)

            select(0)
            fill_evac(-1, 15)
            pair(0, True, False)
            with dve.Fori(1, NQ - 1) as q:
                pair(q, False, False)
            pair(NQ - 1, False, True)
            fill_evac(NQ, 3)
            fill_evac(NQ, 5)

        @block.scalar
        def _(act):
            act.wait_ge(s_const, 32)

            def fill_evac(q, n):
                act.wait_ge(t_fill, upto(q, n))
                empty(n, lambda dst, src: act.activation(dst, src, ACT.Copy)).then_inc(ev[0], 1)

            def gelu(q, e):
                for i, (o, m) in enumerate(UNITS):
                    unit = UPE * e + i
                    act.wait_ge(t_h, q * (UPE * E1) + (unit + 1))
                    if i == 0:
                        after(act, t_y, E1 * q + e - 1)
                    for c in range(m):
                        ins = act.activation(hid[:, e % 2, o + c, :], ps_h[unit % 4][:, c * N2:(c + 1) * N2],
                                             ACT.Gelu, bias=b1[:, e, o + c:o + c + 1])
                    ins.then_inc(a_h, 1)

            def pair(q, first, last):
                for s in range(E1 + 1):
                    if s < E1:
                        gelu(q, s)
                    n = 2 * s
                    if not (first and n in OLD) and not (last and n in NEW):
                        fill_evac(q, n)
                fill_evac(q, FILLS - 2)

            for n in (10, 12, 14):
                fill_evac(-1, n)
            pair(0, True, False)
            with act.Fori(1, NQ - 1) as q:
                pair(q, False, False)
            pair(NQ - 1, False, True)
            fill_evac(NQ, 0)

        @block.tensor
        def _(pe):
            def fill(q, n):
                after(pe, ev[n % 2], upto(q, n, n % 2) - 1)
                bank = ps_m[n % 2]
                if n in TOKENS:
                    half, u, c = TOKENS[n]
                    if n == min(NEW):
                        pe.wait_ge(s_xn, 16 * (q + 2))
                        pe.wait_ge(v_sel, q + 2)
                    for t in range(ST):
                        i = u * ST + t
                        ins = pe.matmul(bank[:, 0:HALF], xn[:, i, c * P:(c + 1) * P], sel[:, i, half * HALF:(half + 1) * HALF],
                                        start=(t == 0), stop=(t == ST - 1))
                elif n in GATES:
                    if n == min(GATES):
                        pe.wait_ge(p_gated, q + 1)
                    for j, (u, c) in enumerate(chunks(*GATES[n])):
                        for t in range(ST):
                            ins = pe.transpose(bank[0:GS, j * S + t * P:j * S + (t + 1) * P],
                                               gated[:, u * ST + t, c * GS:(c + 1) * GS], ident[:])
                elif n in RESULTS:
                    pe.wait_ge(v_y, {0: E1 * q, 11: E1 * q + 4, 13: E1 * q + 4, 18: E1 * q + 7, 19: E1 * q + 7}[n])
                    for j, (u, c) in enumerate(chunks(*RESULTS[n])):
                        for d in range(DC):
                            ins = pe.transpose(bank[0:GS, j * D + d * P:j * D + (d + 1) * P],
                                               yT[:, d, u, c * GS:(c + 1) * GS], ident[:])
                else:
                    u = SUMS[n]
                    pe.wait_ge(ev[0], upto(q, 0, 0))
                    for t in range(ST):
                        for c in range(GC):
                            ins = pe.matmul(bank[:, t * D:(t + 1) * D], gatedT[:, u, c, t * P:(t + 1) * P], y[:, u, c, :],
                                            start=(c == 0), stop=(c == GC - 1))
                ins.then_inc(t_fill, 1)

            def up(q, e):
                if e % 4 == 0:
                    for bank, n in ((0, 14), (1, 15)) if e == 0 else ((0, 6), (1, 1)):
                        pe.wait_ge(ev[bank], upto(q - 1 if e == 0 else q, n, bank))
                for i, (o, m) in enumerate(UNITS):
                    unit = UPE * e + i
                    after(pe, a_h, q * (UPE * E1) + (unit - 3))
                    for c in range(m):
                        for k in range(DC):
                            ins = pe.matmul(ps_h[unit % 4][:, c * N2:(c + 1) * N2],
                                            f1[:, e, k, (o + c) * P:(o + c + 1) * P], tokT[:, k, :, e * CAP1:(e + 1) * CAP1],
                                            start=(k == 0), stop=(k == DC - 1))
                    ins.then_inc(t_h, 1)

            def down(q, e):
                pe.wait_ge(a_h, q * (UPE * E1) + UPE * (e + 1))
                after(pe, v_y, E1 * q + e - 1)
                if isinstance(q, int) and q == 0:
                    pe.wait_ge(s_f2[e % 2], 16 * (e // 2 + 1))
                for d in range(DC):
                    for c in range(HC):
                        ins = pe.matmul(ps_y[e % 2][:, d * N2:(d + 1) * N2], f2[:, e, c, d * P:(d + 1) * P],
                                        hid[:, e % 2, c, :], start=(c == 0), stop=(c == HC - 1))
                ins.then_inc(t_y, 1)

            def pair(q, first, last):
                for s in range(E1 + 1):
                    if s < E1:
                        up(q, s)
                    for n in (2 * s, 2 * s + 1):
                        if not (first and n in OLD) and not (last and n in NEW):
                            fill(q, n)
                    if s > 0:
                        down(q, s - 1)
                fill(q, FILLS - 2)
                fill(q, FILLS - 1)

            for n in NEW:
                fill(-1, n)
            pair(0, True, False)
            with pe.Fori(1, NQ - 1) as q:
                pair(q, False, False)
            pair(NQ - 1, False, True)
            for n in OLD:
                fill(NQ, n)


def build(nc, io, out, NB=BATCH, NE=E0, debug=None):
    with ExitStack() as whole:
        stage_name = ["all"]

        def tensor(stack):
            return lambda name, shape, dt=F32: stack.enter_context(nc.sbuf_tensor(f"{stage_name[0]}_{name}", shape, dt))

        def bank(stack):
            return lambda name: stack.enter_context(nc.psum_tensor(name, [P, 512], F32))

        def sem(name):
            return whole.enter_context(nc.semaphore(name))

        dram = debug or {}
        for name, shape in (("x1", (BATCH, S, D)), ("rows", (E0 * CAP0, D)), ("y", (E0 * CAP0, D)),
                            ("x3", (BATCH, S, D)), ("x3n", (BATCH, S, D))):
            if name not in dram:
                dram[name] = nc.dram_tensor(f"{name}_scratch", shape, F32).ap()
        dram["parts"] = nc.dram_tensor("parts_scratch", (2, PARTS, D, S), BF16).ap()
        sb = tensor(whole)
        keep = {
            "ident": sb("ident", [P, P]), "gates": sb("gates", [P, 4]), "tanh_g": sb("tanh_g", [P, 4]),
            "slots_all": sb("slots_all", [P, BATCH * ST, 8], U32), "w_all": sb("w_all", [P, BATCH * ST, 8]),
        }
        with ExitStack() as stage:
            stage_name[0] = "a"
            attention_and_router(nc, tensor(stage), bank(stage), sem, io, dram, keep, NB)
        stage_name[0] = "all"
        keep["gate_all"] = sb("gate_all", [P, ST, BATCH * E1])
        keep["f1"] = sb("f1", [P, E1, DC, HID])
        keep["s_f1"] = sem("f1_loaded")
        with ExitStack() as layer1_attention:
            keep["s_c_weights"] = sem("c_weights_loaded")
            c_sb = tensor(layer1_attention)
            for name in ("c_wq", "c_wk", "c_wv"):
                keep[name] = c_sb(name, [P, DC, HD])
            keep["c_wo"] = c_sb("c_wo", [P, HD // P, D])
            keep["router_w"] = c_sb("router_w", [P, DC, E1])
            with ExitStack() as stage:
                stage_name[0] = "b"
                experts(nc, tensor(stage), bank(stage), sem, io, dram, keep, NE)
            with ExitStack() as stage:
                stage_name[0] = "c"
                attention_and_top(nc, tensor(stage), bank(stage), sem, io, dram, keep, NB)
        keep["pos_all"] = sb("pos_all", [P, ST, BATCH * E1])
        with ExitStack() as stage:
            stage_name[0] = "e"
            choose_tokens(nc, tensor(stage), bank(stage), sem, io, dram, keep, NB)
        with ExitStack() as stage:
            stage_name[0] = "d"
            expert_choice(nc, tensor(stage), bank(stage), sem, io, out, dram, keep, NB)


def lay_out(inputs, np):
    a = {k: np.asarray(v) for k, v in inputs.items()}
    t = lambda m: np.ascontiguousarray(np.swapaxes(m, -1, -2))
    return {
        "x": a["x"], "ctxT": t(a["ctx_1024"]), "mask": a["mask_1x1xSxS2_fk1"][0, 0],
        "gates": np.concatenate([a["g_xattn"], a["g_ffn"]]),
        "wq": a["L0_xattn_Wq"], "wk": a["L0_xattn_Wk"], "wv": a["L0_xattn_Wv"], "wo": a["L0_xattn_Wo"],
        "bq": a["L0_xattn_bq"], "bk": a["L0_xattn_bk"], "bv": a["L0_xattn_bv"], "bo": a["L0_xattn_bo"],
        "gate_w": t(a["L0_ffn_gate_w"]), "gate_b": a["L0_ffn_gate_b"],
        "w1": t(a["L0_ffn_w1"]), "w2": t(a["L0_ffn_w2"]), "w3": t(a["L0_ffn_w3"]),
        "ws1": t(a["L0_ffn_ws1"]), "ws2": t(a["L0_ffn_ws2"]), "ws3": t(a["L0_ffn_ws3"]),
        "w_q": a["L1_xattn_W_Q"], "w_k": a["L1_xattn_W_K"], "w_v": a["L1_xattn_W_V"], "w_o": a["L1_xattn_W_O"],
        "router_w": t(a["L1_ffn_router_w"]),
        "f1": a["L1_ffn_w1"], "fb1": a["L1_ffn_b1"], "f2": a["L1_ffn_w2"], "fb2": a["L1_ffn_b2"],
    }


def kernel(**inputs):
    import numpy as _np
    import concourse.bacc as _bacc
    from concourse import mybir as _mybir
    from concourse.bass_utils import run_bass_kernel_spmd as _run

    nc = _bacc.Bacc("TRN2", target_bir_lowering=False, num_devices=1)
    arrays, io = {}, {}
    for name, a in lay_out(inputs, _np).items():
        a = _np.ascontiguousarray(a)
        arrays[f"{name}_in"] = a
        io[name] = nc.dram_tensor(f"{name}_in", a.shape, _mybir.dt.from_np(a.dtype), kind="ExternalInput").ap()
    out = nc.dram_tensor("out", (BATCH, S, D), _mybir.dt.float32, kind="ExternalOutput").ap()
    build(nc, io, out)
    r = _run(nc, [arrays], core_ids=[0])
    return r.results[0]["out"]
```
